# Optimizing a Trainium2 kernel written in Bass

```python
import numpy as np
import jax
import jax.numpy as jnp

def _softmax(x, axis=-1):
    return jax.nn.softmax(x, axis=axis)

def _gelu(x):
    return jax.nn.gelu(x, approximate=True)

def _silu(x):
    return jax.nn.silu(x)

def _sigmoid(x):
    return jax.nn.sigmoid(x)

def _layernorm(x, axis=-1, eps=1e-05):
    m = jnp.mean(x, axis=axis, keepdims=True)
    v = jnp.var(x, axis=axis, keepdims=True)
    return (x - m) / jnp.sqrt(v + eps)

def _scatter_add(tgt, idx, src, axis=0):
    return tgt.at[idx].add(src)

def _segment_sum(src, seg, n):
    return jax.ops.segment_sum(src, seg, n)
kernel_name = 'mk_xattn_ffn_d1_seqx_r4_db1f3e'

def setup_inputs(seed: int=0):
    np.random.seed(seed)
    _w = jnp.asarray

    def _rec_inputs():
        import jax
        import jax.numpy as jnp
        _rk = jax.random.key(seed)
        x = -0.000125 + 0.9999 * jax.random.normal(jax.random.fold_in(_rk, 1), (32, 112, 512), jnp.float32)
        _lenS = 112 - jax.random.randint(jax.random.fold_in(_rk, 7), (32,), 0, max(1, 112 // 4) + 1, jnp.int32)
        _lenS2 = 375 - jax.random.randint(jax.random.fold_in(_rk, 8), (32,), 0, max(1, 375 // 4) + 1, jnp.int32)
        _ctx_2048P = jax.random.normal(jax.random.fold_in(_rk, 11), (32, 16, 512), jnp.float32)
        _ctx_2048c = jax.random.dirichlet(jax.random.fold_in(_rk, 511), 0.3 * jnp.ones((16,), jnp.float32), (32, 375))
        _ctx_2048t = jnp.einsum('bsk,bkd->bsd', _ctx_2048c, _ctx_2048P)
        _ctx_2048t = _ctx_2048t * jax.lax.rsqrt(jnp.mean(jnp.square(_ctx_2048t)) + 1e-12) * 0.953939
        ctx_2048 = 1.72703e-05 + 1.00003 * (_ctx_2048t + 0.3 * jax.random.normal(jax.random.fold_in(_rk, 611), (32, 375, 512), jnp.float32))
        return (x, ctx_2048)
    x, ctx_2048 = _rec_inputs()

    def _L0_xattn_setup():
        import jax, jax.numpy as jnp
        import numpy as np
        DIM = 512
        NH = 16
        HD = DIM // NH
        EPS = 1e-06
        IMG_LEN = 257

        def rms_norm(x, w, eps=EPS):
            xf = x.astype(jnp.float32)
            y = xf * jax.lax.rsqrt(jnp.mean(xf * xf, axis=-1, keepdims=True) + eps)
            return y.astype(x.dtype) * w

        def linear(x, w, b):
            return jnp.einsum('blc,oc->blo', x, w) + b

        def attention(q, k, v):
            scale = 1.0 / jnp.sqrt(jnp.asarray(HD, q.dtype))
            scores = jnp.einsum('bqhd,bkhd->bhqk', q, k) * scale
            probs = jax.nn.softmax(scores, axis=-1)
            return jnp.einsum('bhqk,bkhd->bqhd', probs, v)
        key = jax.random.key(seed)
        ks = jax.random.split(key, 12)
        B, L = (2, 2048)
        s = 0.02
        inp = {'x': jax.random.normal(ks[0], (B, L, DIM), jnp.float32), 'context': jax.random.normal(ks[1], (B, 769, DIM), jnp.float32), 'q_w': jax.random.normal(ks[2], (DIM, DIM), jnp.float32) * s, 'q_b': jnp.zeros((DIM,), jnp.float32), 'k_w': jax.random.normal(ks[3], (DIM, DIM), jnp.float32) * s, 'k_b': jnp.zeros((DIM,), jnp.float32), 'v_w': jax.random.normal(ks[4], (DIM, DIM), jnp.float32) * s, 'v_b': jnp.zeros((DIM,), jnp.float32), 'k_img_w': jax.random.normal(ks[5], (DIM, DIM), jnp.float32) * s, 'k_img_b': jnp.zeros((DIM,), jnp.float32), 'v_img_w': jax.random.normal(ks[6], (DIM, DIM), jnp.float32) * s, 'v_img_b': jnp.zeros((DIM,), jnp.float32), 'o_w': jax.random.normal(ks[7], (DIM, DIM), jnp.float32) * s, 'o_b': jnp.zeros((DIM,), jnp.float32), 'norm_q_w': jnp.ones((DIM,), jnp.float32), 'norm_k_w': jnp.ones((DIM,), jnp.float32), 'norm_k_img_w': jnp.ones((DIM,), jnp.float32)}
        return inp
    _L0_xattn_all = _L0_xattn_setup()
    _L0_xattn_in = {k: v for k, v in _L0_xattn_all.items() if k in ('q_w', 'q_b', 'k_w', 'k_b', 'v_w', 'v_b', 'k_img_w', 'k_img_b', 'v_img_w', 'v_img_b', 'o_w', 'o_b', 'norm_q_w', 'norm_k_w', 'norm_k_img_w')}
    del _L0_xattn_all

    def _L0_ffn_setup():
        import jax, jax.numpy as jnp
        import numpy as np
        CAPACITY = 0.125
        HEAD_DIM = 128
        N_HEADS = 16
        N_KV_HEADS = 8
        ROPE_THETA = 10000.0
        EPS = 1e-06

        def _rms_norm(x, w):
            return x * jax.lax.rsqrt(jnp.mean(x * x, axis=-1, keepdims=True) + EPS) * w

        def _rotate_half(t):
            h = t.shape[-1] // 2
            return jnp.concatenate([-t[..., h:], t[..., :h]], axis=-1)
        key = jax.random.key(seed)
        ks = jax.random.split(key, 12)
        B, T, D = (4, 1024, 512)
        I = 2048
        s = 0.02
        return {'hidden_states': jax.random.normal(ks[0], (B, T, D), jnp.float32), 'w_router': jax.random.normal(ks[1], (D,), jnp.float32) * s, 'wq': jax.random.normal(ks[2], (D, N_HEADS * HEAD_DIM), jnp.float32) * s, 'bq': jnp.zeros((N_HEADS * HEAD_DIM,), jnp.float32), 'wk': jax.random.normal(ks[3], (D, N_KV_HEADS * HEAD_DIM), jnp.float32) * s, 'bk': jnp.zeros((N_KV_HEADS * HEAD_DIM,), jnp.float32), 'wv': jax.random.normal(ks[4], (D, N_KV_HEADS * HEAD_DIM), jnp.float32) * s, 'bv': jnp.zeros((N_KV_HEADS * HEAD_DIM,), jnp.float32), 'wo': jax.random.normal(ks[5], (N_HEADS * HEAD_DIM, D), jnp.float32) * s, 'w_gate': jax.random.normal(ks[6], (D, I), jnp.float32) * s, 'w_up': jax.random.normal(ks[7], (D, I), jnp.float32) * s, 'w_down': jax.random.normal(ks[8], (I, D), jnp.float32) * s, 'ln1_w': jnp.ones((D,), jnp.float32), 'ln2_w': jnp.ones((D,), jnp.float32)}
    _L0_ffn_all = _L0_ffn_setup()
    _L0_ffn_in = {k: v for k, v in _L0_ffn_all.items() if k in ('w_router', 'wq', 'bq', 'wk', 'bk', 'wv', 'bv', 'wo', 'w_gate', 'w_up', 'w_down', 'ln1_w', 'ln2_w')}
    del _L0_ffn_all
    return {'x': x, 'ctx_2048': ctx_2048, 'L0_xattn_q_w': _L0_xattn_in['q_w'], 'L0_xattn_q_b': _L0_xattn_in['q_b'], 'L0_xattn_k_w': _L0_xattn_in['k_w'], 'L0_xattn_k_b': _L0_xattn_in['k_b'], 'L0_xattn_v_w': _L0_xattn_in['v_w'], 'L0_xattn_v_b': _L0_xattn_in['v_b'], 'L0_xattn_k_img_w': _L0_xattn_in['k_img_w'], 'L0_xattn_k_img_b': _L0_xattn_in['k_img_b'], 'L0_xattn_v_img_w': _L0_xattn_in['v_img_w'], 'L0_xattn_v_img_b': _L0_xattn_in['v_img_b'], 'L0_xattn_o_w': _L0_xattn_in['o_w'], 'L0_xattn_o_b': _L0_xattn_in['o_b'], 'L0_xattn_norm_q_w': _L0_xattn_in['norm_q_w'], 'L0_xattn_norm_k_w': _L0_xattn_in['norm_k_w'], 'L0_xattn_norm_k_img_w': _L0_xattn_in['norm_k_img_w'], 'L0_ffn_w_router': _L0_ffn_in['w_router'], 'L0_ffn_wq': _L0_ffn_in['wq'], 'L0_ffn_bq': _L0_ffn_in['bq'], 'L0_ffn_wk': _L0_ffn_in['wk'], 'L0_ffn_bk': _L0_ffn_in['bk'], 'L0_ffn_wv': _L0_ffn_in['wv'], 'L0_ffn_bv': _L0_ffn_in['bv'], 'L0_ffn_wo': _L0_ffn_in['wo'], 'L0_ffn_w_gate': _L0_ffn_in['w_gate'], 'L0_ffn_w_up': _L0_ffn_in['w_up'], 'L0_ffn_w_down': _L0_ffn_in['w_down'], 'L0_ffn_ln1_w': _L0_ffn_in['ln1_w'], 'L0_ffn_ln2_w': _L0_ffn_in['ln2_w']}

def reference(x, ctx_2048, L0_xattn_q_w, L0_xattn_q_b, L0_xattn_k_w, L0_xattn_k_b, L0_xattn_v_w, L0_xattn_v_b, L0_xattn_k_img_w, L0_xattn_k_img_b, L0_xattn_v_img_w, L0_xattn_v_img_b, L0_xattn_o_w, L0_xattn_o_b, L0_xattn_norm_q_w, L0_xattn_norm_k_w, L0_xattn_norm_k_img_w, L0_ffn_w_router, L0_ffn_wq, L0_ffn_bq, L0_ffn_wk, L0_ffn_bk, L0_ffn_wv, L0_ffn_bv, L0_ffn_wo, L0_ffn_w_gate, L0_ffn_w_up, L0_ffn_w_down, L0_ffn_ln1_w, L0_ffn_ln2_w):
    import jax
    import jax.numpy as jnp

    def _L0_xattn_ref(x, context, q_w, q_b, k_w, k_b, v_w, v_b, k_img_w, k_img_b, v_img_w, v_img_b, o_w, o_b, norm_q_w, norm_k_w, norm_k_img_w):
        import jax, jax.numpy as jnp
        import numpy as np
        DIM = 512
        NH = 16
        HD = DIM // NH
        EPS = 1e-06
        IMG_LEN = 257

        def rms_norm(x, w, eps=EPS):
            xf = x.astype(jnp.float32)
            y = xf * jax.lax.rsqrt(jnp.mean(xf * xf, axis=-1, keepdims=True) + eps)
            return y.astype(x.dtype) * w

        def linear(x, w, b):
            return jnp.einsum('blc,oc->blo', x, w) + b

        def attention(q, k, v):
            scale = 1.0 / jnp.sqrt(jnp.asarray(HD, q.dtype))
            scores = jnp.einsum('bqhd,bkhd->bhqk', q, k) * scale
            probs = jax.nn.softmax(scores, axis=-1)
            return jnp.einsum('bhqk,bkhd->bqhd', probs, v)
        B, L, _ = x.shape
        ctx_img = context[:, :IMG_LEN]
        ctx_txt = context[:, IMG_LEN:]
        q = rms_norm(linear(x, q_w, q_b), norm_q_w).reshape(B, L, NH, HD)
        k = rms_norm(linear(ctx_txt, k_w, k_b), norm_k_w).reshape(B, -1, NH, HD)
        v = linear(ctx_txt, v_w, v_b).reshape(B, -1, NH, HD)
        k_img = rms_norm(linear(ctx_img, k_img_w, k_img_b), norm_k_img_w).reshape(B, -1, NH, HD)
        v_img = linear(ctx_img, v_img_w, v_img_b).reshape(B, -1, NH, HD)
        img_x = attention(q, k_img, v_img)
        txt_x = attention(q, k, v)
        out = (txt_x + img_x).reshape(B, L, DIM)
        return linear(out, o_w, o_b)

    def _L0_ffn_ref(hidden_states, w_router, wq, bq, wk, bk, wv, bv, wo, w_gate, w_up, w_down, ln1_w, ln2_w):
        import jax, jax.numpy as jnp
        import numpy as np
        CAPACITY = 0.125
        HEAD_DIM = 128
        N_HEADS = 16
        N_KV_HEADS = 8
        ROPE_THETA = 10000.0
        EPS = 1e-06

        def _rms_norm(x, w):
            return x * jax.lax.rsqrt(jnp.mean(x * x, axis=-1, keepdims=True) + EPS) * w

        def _rotate_half(t):
            h = t.shape[-1] // 2
            return jnp.concatenate([-t[..., h:], t[..., :h]], axis=-1)
        B, T, D = hidden_states.shape
        k = max(1, int(T * CAPACITY))
        scores = jnp.einsum('btd,d->bt', hidden_states, w_router)
        _, idx = jax.lax.top_k(scores, k)
        idx = jnp.sort(idx, axis=-1)
        b = jnp.arange(B)[:, None]
        sel = hidden_states[b, idx]
        sel_scores = scores[b, idx]
        S = B * k
        x = sel.reshape(S, D)
        pos = idx.reshape(S)
        inv_freq = 1.0 / ROPE_THETA ** (jnp.arange(0, HEAD_DIM, 2, dtype=jnp.float32) / HEAD_DIM)
        ang = pos.astype(jnp.float32)[:, None] * inv_freq
        cos = jnp.concatenate([jnp.cos(ang), jnp.cos(ang)], axis=-1)[:, None, :]
        sin = jnp.concatenate([jnp.sin(ang), jnp.sin(ang)], axis=-1)[:, None, :]
        h = _rms_norm(x, ln1_w)
        q = (h @ wq + bq).reshape(S, N_HEADS, HEAD_DIM)
        kk = (h @ wk + bk).reshape(S, N_KV_HEADS, HEAD_DIM)
        v = (h @ wv + bv).reshape(S, N_KV_HEADS, HEAD_DIM)
        q = q * cos + _rotate_half(q) * sin
        kk = kk * cos + _rotate_half(kk) * sin
        rep = N_HEADS // N_KV_HEADS
        kk = jnp.repeat(kk, rep, axis=1)
        v = jnp.repeat(v, rep, axis=1)
        att = jnp.einsum('shd,thd->hst', q, kk) / np.sqrt(HEAD_DIM)
        causal = jnp.tril(jnp.ones((S, S), bool))
        att = jnp.where(causal[None], att, jnp.finfo(att.dtype).min)
        att = jax.nn.softmax(att, axis=-1)
        attn_out = jnp.einsum('hst,thd->shd', att, v).reshape(S, N_HEADS * HEAD_DIM) @ wo
        x1 = x + attn_out
        h2 = _rms_norm(x1, ln2_w)
        mlp = jax.nn.silu(h2 @ w_gate) * (h2 @ w_up) @ w_down
        processed = x1 + mlp
        gate = jax.nn.sigmoid(sel_scores).reshape(S, 1)
        gated = gate * processed + (1.0 - gate) * x
        output = hidden_states.at[b, idx].set(gated.reshape(B, k, D))
        return output
    x = x + _L0_xattn_ref(_layernorm(x, axis=-1), ctx_2048, L0_xattn_q_w, L0_xattn_q_b, L0_xattn_k_w, L0_xattn_k_b, L0_xattn_v_w, L0_xattn_v_b, L0_xattn_k_img_w, L0_xattn_k_img_b, L0_xattn_v_img_w, L0_xattn_v_img_b, L0_xattn_o_w, L0_xattn_o_b, L0_xattn_norm_q_w, L0_xattn_norm_k_w, L0_xattn_norm_k_img_w)
    x = x + _L0_ffn_ref(_layernorm(x, axis=-1), L0_ffn_w_router, L0_ffn_wq, L0_ffn_bq, L0_ffn_wk, L0_ffn_bk, L0_ffn_wv, L0_ffn_bv, L0_ffn_wo, L0_ffn_w_gate, L0_ffn_w_up, L0_ffn_w_down, L0_ffn_ln1_w, L0_ffn_ln2_w)
    return x

_drawn_inputs = setup_inputs


def setup_inputs(seed=0):
    import zlib

    import numpy as np

    out = dict(_drawn_inputs(seed))
    spreads = {'L0_xattn_q_b': (0.0, 0.617),
     'L0_xattn_k_b': (0.0, 0.8),
     'L0_xattn_v_b': (0.0, 0.1),
     'L0_xattn_k_img_b': (0.0, 0.8),
     'L0_xattn_v_img_b': (0.0, 0.1),
     'L0_xattn_o_b': (0.0, 0.1),
     'L0_xattn_norm_q_w': (1.0, 0.6),
     'L0_xattn_norm_k_w': (1.0, 0.6),
     'L0_xattn_norm_k_img_w': (1.0, 0.6),
     'L0_ffn_bq': (0.0, 0.8),
     'L0_ffn_bk': (0.0, 0.8),
     'L0_ffn_bv': (0.0, 0.675),
     'L0_ffn_ln1_w': (1.0, 0.6),
     'L0_ffn_ln2_w': (1.0, 0.6)}
    factors = {'L0_ffn_w_router': 2.905,
     'L0_ffn_wq': 8.0,
     'L0_ffn_wk': 8.0,
     'L0_ffn_wv': 4.977,
     'L0_ffn_wo': 3.75,
     'L0_ffn_w_gate': 4.47,
     'L0_ffn_w_up': 4.384,
     'L0_ffn_w_down': 4.396}
    for name, (base, spread) in spreads.items():
        noise = np.random.default_rng([zlib.crc32(name.encode()), seed]).standard_normal(out[name].shape)
        drawn = base * np.exp(spread * noise) if base else spread * noise
        out[name] = jnp.asarray(drawn.astype(out[name].dtype))
    for name, factor in factors.items():
        out[name] = (out[name] * factor).astype(out[name].dtype)
    return out
```

```python
from contextlib import ExitStack

import concourse.bass as bass
from concourse import mybir

ACT = mybir.ActivationFunctionType
ALU = mybir.AluOpType
AX = mybir.AxisListType
F32 = mybir.dt.float32
F32R = mybir.dt.float32r
BF16 = mybir.dt.bfloat16

B, L, D = 32, 112, 512
IMG, CTX = 257, 375
TXT = CTX - IMG
NH, HD = 16, 32
P = 128
KC = D // P
GH = P // HD
NG = NH // GH
IMG_MAIN = IMG - 1
TAIL = TXT
NKEY = CTX + 1
CHUNK_C = TXT + 1
CTXC = TXT + IMG_MAIN
QCOL = NKEY
RAWC = NKEY + L
VW = HD + 1
LN_EPS, RMS_EPS = 1e-5, 1e-6
SCALE = HD ** -0.5
CHUNKS = [(0, CHUNK_C), (CHUNK_C, P), (CHUNK_C + P, P)]
TOPK = max(1, int(L * 0.125))
S = B * TOPK
NC = S // L
BPC = B // NC
FH, FKV, FD = 16, 8, 128
FF = 2048
FC = FF // P
FSCALE = FD ** -0.5
HALF = FD // 2
MASKED = -1e30
FAR = 1000.0


def build(nc, t, out):
    with ExitStack() as ctx:
        def sb(name, shape, dt=F32):
            return ctx.enter_context(nc.sbuf_tensor(name, shape, dt))

        def sem(name):
            return ctx.enter_context(nc.semaphore(name))

        ps = ctx.enter_context(nc.psum_tensor("ps", [P, 8, 512], F32))
        bank0, bank1 = ps[:, 0, :], ps[:, 1, :]
        vtail_dram = nc.dram_tensor("vtail_dram", (B, NH * VW), F32, kind="Internal").ap()
        xh_dram = nc.dram_tensor("xh_dram", (B * L, 2 * D), F32, kind="Internal").ap()
        score_dram = nc.dram_tensor("score_dram", (B, L), F32, kind="Internal").ap()

        ident = sb("ident", [P, P])
        ln_eps = sb("ln_eps", [P, 1])
        rms_eps = sb("rms_eps", [P, 1])
        wr = sb("wr", [L, D])
        score = sb("score", [L, B])

        phase1 = ExitStack()

        def p1(name, shape, dt=F32):
            return phase1.enter_context(nc.sbuf_tensor(name, shape, dt))

        neg_ident = p1("neg_ident", [L, L])
        ones = p1("ones", [P, P])
        ones_img = p1("ones_img", [L, P], BF16)
        ones_c_txt = p1("ones_c_txt", [L, CHUNK_C], BF16)
        ones_c_tail = p1("ones_c_tail", [L, CHUNK_C], BF16)
        W = ["q", "k", "v", "k_img", "v_img", "o"]
        w_hi = {w: p1(f"w_{w}_hi", [P, KC, D], F32R) for w in W}
        w_lo = {w: p1(f"w_{w}_lo", [P, KC, D], F32R) for w in W}
        vecs = p1("vecs", [P, 8, KC])
        qb, kb, kib, vb, vib, nq, nk, nki = (vecs[:, j, :] for j in range(8))
        w_txt = p1("w_txt", [P, KC])
        w_img = p1("w_img", [P, KC])
        out_bias = p1("out_bias", [L, D])
        ctx_tail = p1("ctx_tail", [P, KC, B])
        k_tail = p1("k_tail", [P, KC, B])
        ctx_raw = p1("ctx_raw", [P, KC, CTXC])
        ctx_hi = p1("ctx_hi", [P, KC, CTXC], F32R)
        ctx_lo = p1("ctx_lo", [P, KC, CTXC], F32R)
        x_in = p1("x_in", [L, D])
        xn = x_in
        ln1_stats = p1("ln1_stats", [L, 6])
        ln1_mv = p1("ln1_mv", [L, 2])
        ln1_sd = p1("ln1_sd", [L, 1])
        ln1_rstd = p1("ln1_rstd", [L, 1])
        xT_hi = p1("xT_hi", [P, KC, L], F32R)
        xT_lo = p1("xT_lo", [P, KC, L], F32R)
        raw = p1("raw", [P, KC, RAWC])
        work = p1("work", [P, KC, RAWC])
        sq_sum = p1("sq_sum", [P, RAWC])
        rms = sq_sum
        vbias_cols = work[:, :, 0:L]
        k_hi = p1("k_hi", [P, KC, NKEY], F32R)
        k_lo = p1("k_lo", [P, KC, NKEY], F32R)
        q_hi = p1("q_hi", [P, NG, GH, L], F32R)
        q_lo = p1("q_lo", [P, NG, GH, L], F32R)
        v_c = p1("v_c", [CHUNK_C, NH, 2 * VW])
        v_a = p1("v_a", [P, NH, VW])
        v_b = p1("v_b", [P, NH, VW])
        top = p1("top", [L, NG, 2, GH])
        shift = p1("shift", [L, NG, 2, GH, L], BF16)
        prob = p1("prob", [P, 2, 3, GH * L])
        stage = prob[:].rearrange("p a c n -> p a (c n)")[:, :, 0:1024]
        rec = p1("rec", [L, GH, 2])
        o_parts = p1("o_parts", [L, 2, GH, HD])
        o = p1("o", [L, D])
        oT_hi, oT_lo = xT_hi, xT_lo
        x_res = p1("x_res", [L, D])
        xh = p1("xh", [L, 2, D])
        ln2_stats = p1("ln2_stats", [L, 6])
        ln2_mv = p1("ln2_mv", [L, 2])
        ln2_sd = p1("ln2_sd", [L, 1])
        ln2_rstd = p1("ln2_rstd", [L, 1])
        score_junk = o
        out_sb = x_res
        v_tail = xh[0:B].rearrange("b a d -> b (a d)")[:, 0:NH * VW].rearrange("b (h w) -> b h w", h=NH)


        phase1.close()
        ring = [sb(f"ring{j}", [P, 4 * FF]) for j in range(3)]
        wq = ring[0][:].rearrange("p (c n) -> p c n", c=KC)
        wk = ring[1][:, 0:2 * FF].rearrange("p (c n) -> p c n", c=KC)
        wv = ring[1][:, 2 * FF:4 * FF].rearrange("p (c n) -> p c n", c=KC)
        wo = ring[2][:].rearrange("p (c n) -> p c n", c=FH)
        w_gate = ring[0][:].rearrange("p (c n) -> p c n", c=KC)
        w_up = ring[1][:].rearrange("p (c n) -> p c n", c=KC)
        w_down = ring[2][:].rearrange("p (c n) -> p c n", c=FC)
        fvec = sb("fvec", [P, FH + FKV + 2 * KC])
        bv_row = sb("bv_row", [L, FKV * FD])
        tok = sb("tok", [L, NC], mybir.dt.int32)
        token_base = sb("token_base", [L, NC])
        xh_sel = sb("xh_sel", [L, NC, 2, D])
        sel_score = sb("sel_score", [L, NC])
        gate_e = sb("gate_e", [L, NC])
        gate = sb("gate", [L, NC])
        keep = xh_sel[:, :, 0, :]
        sums = sb("sums", [L, NC])
        rstd = sb("rstd", [L, NC])
        normed = sb("normed", [L, NC, D])
        hT = sb("hT", [P, KC, S])
        cos = sb("cos", [P, S])
        sin = sb("sin", [P, S])
        topk = ExitStack()

        def tk(name, shape, dt=F32):
            return topk.enter_context(nc.sbuf_tensor(name, shape, dt))

        score_row = tk("score_row", [L, B, L])
        above = tk("above", [L, B, L])
        equal = tk("equal", [L, B, L])
        rank = tk("rank", [L, B])
        chosen = tk("chosen", [L, B])
        before = tk("before", [L, B])
        slot_hot = tk("slot_hot", [L, B, TOPK])
        earlier = tk("earlier", [L, L])
        later = tk("later", [L, L])
        slot_far = tk("slot_far", [L, TOPK])
        token_no = tk("token_no", [L, 1])
        cos_tab = tk("cos_tab", [L, P])
        sin_tab = tk("sin_tab", [L, P])
        topk.close()
        qT = sb("qT", [P, FH, S])
        attnT, mT = qT, qT
        kT = sb("kT", [P, FKV, S])
        vals = sb("vals", [L, NC, FKV * FD])
        x_mid = vals[:, :, 0:D]
        biased = sb("biased", [P, 2, S])
        rot = sb("rot", [P, 2, S])
        causal = sb("causal", [L, L], BF16)
        ident_bf = sb("ident_bf", [L, L], BF16)
        neg_top = sb("neg_top", [L, NC])
        prob_sum = sb("prob_sum", [L, NC])
        prob2 = sb("prob2", [L, 2, S])
        probT = normed[:].rearrange("l c d -> l (c d)")[:, 0:NC * S].rearrange("l (c s) -> l c s", c=NC)
        silu_e = biased
        silu_g = rot

        consts_zeroed, consts_ready = sem("consts_zeroed"), sem("consts_ready")
        vecs_loaded, rows_loaded, tails_loaded = sem("vecs_loaded"), sem("rows_loaded"), sem("tails_loaded")
        piece_loaded = [sem("piece_loaded0"), sem("piece_loaded1")]
        piece_hi, piece_lo = sem("piece_hi"), sem("piece_lo")
        vecs_ready = sem("vecs_ready")
        pro_full, pro_done, vtail_stored = sem("pro_full"), sem("pro_done"), sem("vtail_stored")
        ctx_loaded, ctx_hi_done, ctx_lo_done = sem("ctx_loaded"), sem("ctx_hi_done"), sem("ctx_lo_done")
        x_loaded, ln1_step, ln1_sd_done = sem("x_loaded"), sem("ln1_step"), sem("ln1_sd_done")
        xn_ready, xT_hi_done = sem("xn_ready"), sem("xT_hi_done")
        b0_full, b0_done, b1_full, b1_done = sem("b0_full"), sem("b0_done"), sem("b1_full"), sem("b1_done")
        sq_step, sq_ready, rms_inv = sem("sq_step"), sem("sq_ready"), sem("rms_inv")
        scaled, k_hi_done, q_hi_done = sem("scaled"), sem("k_hi_done"), sem("q_hi_done")
        kq_lo_done, vtail_loaded = sem("kq_lo_done"), sem("vtail_loaded")
        s_full, s_done, shift_ready = sem("s_full"), sem("s_done"), sem("shift_ready")
        st_full, exp_done = sem("st_full"), sem("exp_done")
        pv_full, norm_step, pv_done = sem("pv_full"), sem("norm_step"), sem("pv_done")
        oT_hi_done, xres_loaded, xres_ready = sem("oT_hi_done"), sem("xres_loaded"), sem("xres_ready")
        ln2_step, ln2_sd_done, h_ready = sem("ln2_step"), sem("ln2_sd_done"), sem("h_ready")
        h_step, rows_ready, passed = sem("h_step"), sem("rows_ready"), sem("passed")
        score_ready, out_ready = sem("score_ready"), sem("out_ready")
        xh_stored, out_stored, score_stored = sem("xh_stored"), sem("out_stored"), sem("score_stored")

        topk_loaded, score_row_loaded, fvec_loaded = sem("topk_loaded"), sem("score_row_loaded"), sem("fvec_loaded")
        ring_loaded = [sem(f"ring_loaded{j}") for j in range(3)]
        rank_step, chosen_ready, before_full, hot_ready = sem("rank_step"), sem("chosen_ready"), sem("before_full"), sem("hot_ready")
        tok_full, tok_ready, rope_full, rope_ready = sem("tok_full"), sem("tok_ready"), sem("rope_full"), sem("rope_ready")
        gathered = [sem(f"gathered{c}") for c in range(NC)]
        sums_ready, root_ready, rstd_ready, normed_ready = sem("sums_ready"), sem("root_ready"), sem("rstd_ready"), sem("normed_ready")
        hT_full, hT_ready = sem("hT_full"), sem("hT_ready")
        head_full, head_biased, rot_step, head_ready = sem("head_full"), sem("head_biased"), sem("rot_step"), sem("head_ready")
        val_full, val_ready = sem("val_full"), sem("val_ready")
        att_full, top_ready, prob_ready = sem("att_full"), sem("top_ready"), sem("prob_ready")
        inv_ready, prob_scaled, pT_full, pT_ready = sem("inv_ready"), sem("prob_scaled"), sem("pT_full"), sem("pT_ready")
        attn_full, attn_ready = sem("attn_full"), sem("attn_ready")
        mid_full, mid_ready = sem("mid_full"), sem("mid_ready")
        mlp_full, silu_exp, silu_step, hid_ready = sem("mlp_full"), sem("silu_exp"), sem("silu_step"), sem("hid_ready")
        down_full, sum_ready, final_ready, scattered = sem("down_full"), sem("sum_ready"), sem("final_ready"), sem("scattered")
        gate_step, gate_exp, consts2 = sem("gate_step"), sem("gate_exp"), sem("consts2")
        blocks_read = sem("blocks_read")

        block = ctx.enter_context(nc.Block())

        def slot0(n, k):
            return 6 * n + k

        def slot1(n, k):
            return 6 * n - 2 + k if not isinstance(n, int) or n else k

        def slot1_own(i, k):
            return 6 * i + 8 + k if not isinstance(i, int) or i < B - 1 else 6 * i + 4 + k

        def over_batches(eng, pre, body):
            pre()
            with eng.Fori(0, B - 2) as i:
                body(i, i + 1, i + 2)
            body(B - 2, B - 1, None)
            body(B - 1, None, None)

        PIECES = 2 * len(W)

        @block.sync
        def _(sp):
            sp.dma_start(vecs[:], t["vecs"]).then_inc(vecs_loaded, 16)
            sp.dma_start(ctx_tail[:], t["ctx_tail"]).then_inc(tails_loaded, 16)
            sp.dma_start(out_bias[:], t["o_b"].partition_broadcast(L)).then_inc(rows_loaded, 16)
            sp.dma_start(wr[:], t["w_router"].partition_broadcast(L)).then_inc(rows_loaded, 16)

            def load_x(m):
                sp.dma_start(x_in[:], t["x"][bass.ds(m, 1)].rearrange("o t d -> t (o d)")).then_inc(x_loaded, 16)

            def load_ctx(n):
                sp.dma_start(ctx_raw[:], t["ctx"][bass.ds(n, 1)].rearrange("o p c n -> p (o c) n")).then_inc(ctx_loaded, 16)

            def pre():
                for stored in (xh_stored, score_stored, out_stored):
                    sp.sem_inc(stored, 16)
                load_x(0)
                load_ctx(0)
                for j in range(PIECES):
                    if j >= 2:
                        sp.wait_ge(piece_hi, j - 1)
                        sp.wait_ge(piece_lo, j - 1)
                    sp.dma_start(stage[:, j % 2, :], t["w_" + W[j // 2]].rearrange(
                        "(c p) o -> p c o", p=P)[:, 2 * (j % 2):2 * (j % 2) + 2, :]).then_inc(piece_loaded[j % 2], 16)
                sp.wait_ge(ctx_hi_done, 1)
                sp.wait_ge(ctx_lo_done, 1)
                load_ctx(1)
                sp.wait_ge(xT_hi_done, 1)
                load_x(1)
                sp.wait_ge(pro_done, 2)
                sp.dma_start(vtail_dram, v_tail.rearrange("b h w -> b (h w)")).then_inc(vtail_stored, 16)
                sp.wait_ge(vtail_stored, 16)
                sp.wait_ge(consts_ready, 3)
                sp.dma_start(v_c[TXT:TXT + 1, :, 0:VW], vtail_dram[0:1].rearrange("o (h w) -> o h w", h=NH)).then_inc(vtail_loaded, 16)

            def body(i, n, m):
                sp.wait_ge(out_stored, 16 * i + 16)
                sp.dma_start(x_res[:], t["x"][bass.ds(i, 1)].rearrange("o t d -> t (o d)")).then_inc(xres_loaded, 16)
                if m is not None:
                    sp.wait_ge(ctx_hi_done, m)
                    sp.wait_ge(ctx_lo_done, m)
                    load_ctx(m)
                    sp.wait_ge(xT_hi_done, m)
                    load_x(m)
                if n is not None:
                    sp.wait_ge(pv_full, 4 * n)
                    sp.dma_start(v_c[TXT:TXT + 1, :, 0:VW], vtail_dram[bass.ds(n, 1)].rearrange(
                        "o (h w) -> o h w", h=NH)).then_inc(vtail_loaded, 16)
                sp.wait_ge(score_ready, i + 1)
                sp.dma_start(xh_dram.rearrange("(b l) d -> b l d", b=B)[bass.ds(i, 1)].rearrange("o l d -> l (o d)"),
                             xh[:].rearrange("l a d -> l (a d)")).then_inc(xh_stored, 16)
                sp.dma_start(score_dram[bass.ds(i, 1)].rearrange("o l -> l o"), score[:, bass.ds(i, 1)]).then_inc(score_stored, 16)
                sp.wait_ge(out_ready, i + 1)
                sp.dma_start(out[bass.ds(i, 1)].rearrange("o l d -> l (o d)"), out_sb[:]).then_inc(out_stored, 16)

            over_batches(sp, pre, body)
            sp.wait_ge(xh_stored, 16 * B + 16)
            sp.wait_ge(score_stored, 16 * B + 16)
            sp.wait_ge(out_stored, 16 * B + 16)

            sp.dma_start(score_row[:], score_dram.partition_broadcast(L)).then_inc(score_row_loaded, 16)
            for dst, name in ((earlier, "earlier"), (later, "later"), (slot_far, "slot_far"), (token_no, "token_no"),
                              (cos_tab, "cos_tab"), (sin_tab, "sin_tab"), (token_base, "token_base")):
                sp.dma_start(dst[:], t[name]).then_inc(topk_loaded, 16)
            sp.dma_start(fvec[:], t["fvec"]).then_inc(fvec_loaded, 16)
            sp.dma_start(bv_row[:], t["bv"].partition_broadcast(L)).then_inc(fvec_loaded, 16)
            sp.dma_start(wq, t["wq"].rearrange("(c p) n -> p c n", p=P)).then_inc(ring_loaded[0], 16)
            sp.dma_start(wk, t["wk"].rearrange("(c p) n -> p c n", p=P)).then_inc(ring_loaded[1], 16)
            sp.dma_start(wv, t["wv"].rearrange("(c p) n -> p c n", p=P)).then_inc(ring_loaded[1], 16)
            sp.dma_start(wo, t["wo"].rearrange("(c p) n -> p c n", p=P)).then_inc(ring_loaded[2], 16)
            sp.wait_ge(head_full, FH)
            sp.dma_start(w_gate, t["w_gate"].rearrange("(c p) n -> p c n", p=P)).then_inc(ring_loaded[0], 16)
            sp.wait_ge(val_full, 2 * NC)
            sp.dma_start(w_up, t["w_up"].rearrange("(c p) n -> p c n", p=P)).then_inc(ring_loaded[1], 16)
            sp.wait_ge(mid_full, NC)
            sp.dma_start(w_down, t["w_down"].rearrange("(c p) n -> p c n", p=P)).then_inc(ring_loaded[2], 16)

        @block.gpsimd
        def _(pool):
            def split_ctx(n):
                pool.wait_ge(ctx_hi_done, n + 1)
                nc.gpsimd.tensor_tensor(ctx_lo[:], ctx_raw[:], ctx_hi[:].bitcast(F32), ALU.subtract).then_inc(ctx_lo_done, 1)

            def normalise_x(m):
                pool.wait_ge(ln1_step, 3 * m + 3)
                pool.sem_inc(passed, 1)
                nc.gpsimd.tensor_scalar(xn[:], x_in[:], ln1_mv[:, 0:1], ln1_rstd[:], ALU.subtract, ALU.mult).then_inc(xn_ready, 1)

            def squares(n):
                nc.gpsimd.tensor_copy(raw[:, :, TAIL:TAIL + 1], k_tail[:, :, bass.ds(n, 1)]).then_inc(sq_step, 1)
                pool.wait_ge(b0_done, slot0(n, 3))
                pool.wait_ge(b1_done, slot1(n, 3))
                pool.wait_ge(sq_step, 3 * n + 1)
                nc.gpsimd.tensor_tensor(work[:], raw[:], raw[:], ALU.mult).then_inc(sq_step, 1)
                pool.wait_ge(sq_step, 3 * n + 2)
                nc.gpsimd.tensor_tensor(work[:, 0:2], work[:, 0:2], work[:, 2:4], ALU.add).then_inc(sq_step, 1)
                pool.wait_ge(sq_step, 3 * n + 3)
                nc.gpsimd.tensor_tensor(sq_sum[:], work[:, 0], work[:, 1], ALU.add).then_inc(sq_ready, 1)

            def pre():
                nc.gpsimd.memset(ident[:], 0.0)
                nc.gpsimd.memset(neg_ident[:], 0.0)
                nc.gpsimd.memset(ones_c_txt[:], 1.0)
                nc.gpsimd.memset(ones_c_tail[:], 0.0).then_inc(consts_zeroed, 1)
                pool.wait_ge(consts_zeroed, 1)
                nc.gpsimd.affine_select(out=ident[:], in_=ident[:], compare_op=ALU.not_equal, fill=1.0, base=0,
                                        pattern=[[-1, P]], channel_multiplier=1)
                nc.gpsimd.affine_select(out=neg_ident[:], in_=neg_ident[:], compare_op=ALU.not_equal, fill=-1.0, base=0,
                                        pattern=[[-1, L]], channel_multiplier=1)
                nc.gpsimd.memset(ones_c_txt[:, TAIL:TAIL + 1], 0.0)
                nc.gpsimd.memset(ones_c_tail[:, TAIL:TAIL + 1], 1.0)
                nc.gpsimd.memset(ones[:], 1.0)
                nc.gpsimd.memset(ones_img[:], 1.0)
                nc.gpsimd.memset(ln_eps[:], LN_EPS)
                nc.gpsimd.memset(rms_eps[:], RMS_EPS).then_inc(consts_ready, 1)
                nc.gpsimd.memset(raw[:, :, NKEY - 1:NKEY], 0.0)
                nc.gpsimd.memset(q_hi[:].bitcast(F32), 0.0)
                nc.gpsimd.memset(q_lo[:].bitcast(F32), 0.0).then_inc(consts_ready, 1)
                nc.gpsimd.memset(v_c[:], 0.0)
                nc.gpsimd.memset(v_tail[:, :, HD:VW], 1.0)
                nc.gpsimd.memset(v_a[:, :, HD:VW], 1.0)
                nc.gpsimd.memset(v_b[:, :, HD:VW], 1.0).then_inc(consts_zeroed, 1)
                pool.wait_ge(consts_zeroed, 2)
                nc.gpsimd.memset(v_c[0:TXT, :, VW + HD:2 * VW], 1.0).then_inc(consts_ready, 1)
                normalise_x(0)
                split_ctx(0)
                pool.wait_ge(pro_done, 1)
                squares(0)
                normalise_x(1)
                split_ctx(1)

            def body(i, n, m):
                pool.wait_ge(xres_loaded, 16 * i + 16)
                pool.wait_ge(rows_ready, 1)
                nc.gpsimd.tensor_tensor(x_res[:], x_res[:], out_bias[:], ALU.add).then_inc(xres_ready, 1)
                if n is not None:
                    squares(n)
                if m is not None:
                    normalise_x(m)
                    split_ctx(m)
                pool.wait_ge(h_ready, i + 1)
                nc.gpsimd.tensor_tensor(out_sb[:], xh[:, 0], xh[:, 1], ALU.add).then_inc(out_ready, 1)

            over_batches(pool, pre, body)

            pool.wait_ge(tok_ready, 1)
            for c in range(NC):
                nc.gpsimd.indirect_dma_start(xh_sel[:, c].rearrange("l a d -> l (a d)"), None, xh_dram,
                                             bass.IndirectOffsetOnAxis(ap=tok[:, c:c + 1], axis=0)).then_inc(gathered[c], 16)
            pool.wait_ge(rope_ready, 2)
            nc.gpsimd.memset(causal[:], 0.0)
            nc.gpsimd.memset(ident_bf[:], 0.0).then_inc(consts2, 1)
            pool.wait_ge(consts2, 1)
            nc.gpsimd.affine_select(out=causal[:], in_=causal[:], compare_op=ALU.is_ge, fill=MASKED, base=0,
                                    pattern=[[-1, L]], channel_multiplier=1)
            nc.gpsimd.affine_select(out=ident_bf[:], in_=ident_bf[:], compare_op=ALU.not_equal, fill=1.0, base=0,
                                    pattern=[[-1, L]], channel_multiplier=1).then_inc(consts2, 1)
            for c in range(NC):
                pool.wait_ge(final_ready, c + 1)
                nc.gpsimd.indirect_dma_start(out.rearrange("b l d -> (b l) d"), bass.IndirectOffsetOnAxis(ap=tok[:, c:c + 1], axis=0),
                                             keep[:, c], None).then_inc(scattered, 16)
            pool.wait_ge(scattered, 16 * NC)


        @block.scalar
        def _(act):
            def split_ctx(n):
                act.wait_ge(ctx_loaded, 16 * n + 16)
                if not isinstance(n, int) or n >= 1:
                    act.wait_ge(b0_full, slot0(n, 0))
                nc.scalar.activation(ctx_hi[:], ctx_raw[:], ACT.Copy).then_inc(ctx_hi_done, 1)

            def key_evac(n, c, bank):
                nc.scalar.activation(raw[:, c, 0:TXT], bank[:, 0:TXT], ACT.Identity, bias=kb[:, c:c + 1])
                return nc.scalar.activation(raw[:, c, TAIL + 1:CTX], bank[:, TXT:CTXC], ACT.Identity, bias=kib[:, c:c + 1])

            def project(n):
                act.wait_ge(b1_full, slot1(n, 1))
                nc.scalar.activation(xT_hi[:], bank1[:, 0:KC * L].rearrange("p (c l) -> p c l", c=KC), ACT.Copy).then_inc(xT_hi_done, 1)
                act.wait_ge(b0_full, slot0(n, 1))
                key_evac(n, 0, bank0).then_inc(b0_done, 1)
                act.wait_ge(b0_full, slot0(n, 2))
                key_evac(n, 2, bank0).then_inc(b0_done, 1)
                act.wait_ge(b0_full, slot0(n, 3))
                for c in range(KC):
                    last = nc.scalar.activation(raw[:, c, QCOL:RAWC], bank0[:, c * L:(c + 1) * L], ACT.Identity, bias=qb[:, c:c + 1])
                last.then_inc(b0_done, 1)

            def roots(n, m):
                act.wait_ge(b0_full, slot0(n, 4))
                nc.scalar.activation(rms[:], bank0[:, 0:RAWC], ACT.Sqrt, bias=rms_eps[:], scale=1.0 / D).then_inc(b0_done, 1)
                if m is not None:
                    act.wait_ge(ln1_step, 3 * m + 2)
                    nc.scalar.activation(ln1_sd[:], ln1_mv[:, 1:2], ACT.Sqrt, bias=ln_eps[0:L]).then_inc(ln1_sd_done, 1)

            def values(n):
                act.wait_ge(b0_full, slot0(n, 5))
                nc.scalar.activation(v_a[:, :, 0:HD], bank0.rearrange("p (h d) -> p h d", h=NH), ACT.Copy).then_inc(b0_done, 1)
                act.wait_ge(scaled, n + 1)
                for c in range(KC):
                    nc.scalar.activation(k_hi[:, c, 0:TXT], work[:, c, 0:TXT], ACT.Copy, scale=w_txt[:, c:c + 1])
                    last = nc.scalar.activation(k_hi[:, c, TAIL:NKEY], work[:, c, TAIL:NKEY], ACT.Copy, scale=w_img[:, c:c + 1])
                last.then_inc(k_hi_done, 1)
                for j in range(GH):
                    part = slice(HD * j, HD * (j + 1))
                    last = nc.scalar.activation(q_hi[part, :, j, :], work[part, :, QCOL:RAWC], ACT.Copy)
                last.then_inc(q_hi_done, 1)
                act.wait_ge(b0_full, slot0(n, 6))
                nc.scalar.activation(v_c[0:TXT, :, VW:VW + HD], bank0[0:TXT].rearrange("p (h d) -> p h d", h=NH), ACT.Copy).then_inc(b0_done, 1)

            def pre():
                act.wait_ge(consts_ready, 1)
                act.wait_ge(ln1_step, 2)
                nc.scalar.activation(ln1_sd[:], ln1_mv[:, 1:2], ACT.Sqrt, bias=ln_eps[0:L]).then_inc(ln1_sd_done, 1)
                split_ctx(0)
                for j in range(PIECES):
                    act.wait_ge(piece_loaded[j % 2], 16 * (j // 2) + 16)
                    nc.scalar.activation(w_hi[W[j // 2]][:, 2 * (j % 2):2 * (j % 2) + 2, :],
                                         stage[:, j % 2, :].rearrange("p (c o) -> p c o", c=2), ACT.Copy).then_inc(piece_hi, 1)
                act.wait_ge(consts_ready, 3)
                project(0)
                roots(0, 1)
                values(0)
                split_ctx(1)

            def body(i, n, m):
                if n is not None:
                    project(n)
                for g in range(NG):
                    for c, (_, rows) in enumerate(CHUNKS):
                        k = 3 * g + c
                        act.wait_ge(st_full, 12 * i + k + 1)
                        if c == 0 and g >= 2:
                            act.wait_ge(pv_full, 4 * i + g - 1)
                        nc.scalar.activation(prob[0:rows, g % 2, c, :], ps[0:rows, 2 + k % 4, 0:GH * L], ACT.Exp).then_inc(exp_done, 1)
                if n is not None:
                    roots(n, m)
                    values(n)
                act.wait_ge(b1_full, slot1_own(i, 1))
                nc.scalar.activation(oT_hi[:], bank1[:, 0:KC * L].rearrange("p (c l) -> p c l", c=KC), ACT.Copy).then_inc(oT_hi_done, 1)
                if m is not None:
                    split_ctx(m)
                act.wait_ge(ln2_step, 3 * i + 3)
                nc.scalar.activation(ln2_sd[:], ln2_mv[:, 1:2], ACT.Sqrt, bias=ln_eps[0:L]).then_inc(ln2_sd_done, 1)

            over_batches(act, pre, body)

            def token_roots(k):
                act.wait_ge(sums_ready, k + 1)
                nc.scalar.activation(rstd[:], sums[:], ACT.Sqrt, bias=rms_eps[0:L], scale=1.0 / D).then_inc(root_ready, 1)

            def hT_scaled(k, at):
                act.wait_ge(fvec_loaded, 32)
                for kc in range(KC):
                    act.wait_ge(hT_full, KC * k + kc + 1)
                    nc.scalar.activation(hT[:, kc, :], ps[:, 4 + kc, 0:S], ACT.Copy, scale=fvec[:, at + kc:at + kc + 1]).then_inc(hT_ready, 1)

            for k, table in enumerate((cos, sin)):
                act.wait_ge(rope_full, k + 1)
                nc.scalar.activation(table[:], ps[:, 2 + k, 0:S], ACT.Copy).then_inc(rope_ready, 1)
            token_roots(0)
            hT_scaled(0, FH + FKV)
            for h in range(FH + FKV):
                act.wait_ge(head_full, h + 1)
                if h >= 2:
                    act.wait_ge(head_ready, h - 1)
                nc.scalar.activation(biased[:, h % 2, :], ps[:, h % 2, 0:S], ACT.Identity, bias=fvec[:, h:h + 1]).then_inc(head_biased, 1)
            act.wait_ge(gate_step, 1)
            nc.scalar.activation(gate_e[:], sel_score[:], ACT.Exp, scale=-1.0).then_inc(gate_exp, 1)

            def turn_evac(k):
                c = k % NC
                act.wait_ge(pT_full, k + 1)
                if c == 0 and k:
                    act.wait_ge(attn_full, k // NC)
                nc.scalar.activation(probT[:, 0:c + 1, c * L:(c + 1) * L],
                                     ps[0:L, 4 + k % 2, 0:(c + 1) * L].rearrange("t (b q) -> t b q", b=c + 1), ACT.Copy).then_inc(pT_ready, 1)

            for k in range(FH * NC + 2):
                if k < FH * NC:
                    c = k % NC
                    n_keys = (c + 1) * L
                    act.wait_ge(top_ready, k + 1)
                    if k >= 2:
                        act.wait_ge(pT_full, k - 1)
                    nc.scalar.activation(prob2[:, k % 2, 0:n_keys], ps[0:L, c, 0:n_keys], ACT.Exp, bias=neg_top[:, c:c + 1],
                                         accum_out=prob_sum[:, c:c + 1]).then_inc(prob_ready, 1)
                if k >= 2:
                    turn_evac(k - 2)
            token_roots(1)
            hT_scaled(1, FH + FKV + KC)
            for j in range(FC):
                act.wait_ge(mlp_full, j + 1)
                if j >= 2:
                    act.wait_ge(hid_ready, j - 1)
                nc.scalar.activation(silu_e[:, j % 2, :], ps[:, 2 * (j % 2), 0:S], ACT.Exp, scale=-1.0).then_inc(silu_exp, 1)

        @block.vector
        def _(dve):
            def ln1(m):
                dve.wait_ge(x_loaded, 16 * m + 16)
                nc.vector.bn_stats(ln1_stats[:], x_in[:]).then_inc(ln1_step, 1)
                dve.wait_ge(ln1_step, 3 * m + 1)
                dve.sem_inc(passed, 1)
                nc.vector.bn_aggr(ln1_mv[:], ln1_stats[:]).then_inc(ln1_step, 1)

            def ln1_finish(m):
                dve.wait_ge(ln1_sd_done, m + 1)
                nc.vector.reciprocal(ln1_rstd[:], ln1_sd[:]).then_inc(ln1_step, 1)

            def xT_rest(n):
                dve.wait_ge(xT_hi_done, n + 1)
                nc.vector.tensor_tensor(xT_lo[:], bank1[:, 0:KC * L].rearrange("p (c l) -> p c l", c=KC),
                                        xT_hi[:].bitcast(F32), ALU.subtract).then_inc(b1_done, 1)

            def key_evac(n, k, c):
                dve.wait_ge(b1_full, slot1(n, k + 1))
                nc.vector.tensor_scalar(raw[:, c, 0:TXT], bank1[:, 0:TXT], kb[:, c:c + 1], None, ALU.add)
                nc.vector.tensor_scalar(raw[:, c, TAIL + 1:CTX], bank1[:, TXT:CTXC], kib[:, c:c + 1], None, ALU.add).then_inc(b1_done, 1)

            def scale_kq(n):
                dve.wait_ge(b0_done, slot0(n, 4))
                nc.vector.reciprocal(rms[:], rms[:]).then_inc(rms_inv, 1)
                dve.wait_ge(rms_inv, n + 1)
                nc.vector.tensor_tensor(work[:], raw[:], rms[:].unsqueeze(1).to_broadcast([P, KC, RAWC]), ALU.mult).then_inc(scaled, 1)

            def value_evac(n):
                dve.wait_ge(b1_full, slot1(n, 4))
                nc.vector.tensor_copy(v_b[:, :, 0:HD], bank1.rearrange("p (h d) -> p h d", h=NH)).then_inc(b1_done, 1)

            def kq_rest(n):
                dve.wait_ge(k_hi_done, n + 1)
                for c in range(KC):
                    nc.vector.scalar_tensor_tensor(k_lo[:, c, 0:TXT], work[:, c, 0:TXT], w_txt[:, c:c + 1],
                                                   k_hi[:, c, 0:TXT].bitcast(F32), ALU.mult, ALU.subtract)
                    nc.vector.scalar_tensor_tensor(k_lo[:, c, TAIL:NKEY], work[:, c, TAIL:NKEY], w_img[:, c:c + 1],
                                                   k_hi[:, c, TAIL:NKEY].bitcast(F32), ALU.mult, ALU.subtract)
                dve.wait_ge(q_hi_done, n + 1)
                for j in range(GH):
                    part = slice(HD * j, HD * (j + 1))
                    last = nc.vector.tensor_tensor(q_lo[part, :, j, :], work[part, :, QCOL:RAWC],
                                                   q_hi[part, :, j, :].bitcast(F32), ALU.subtract)
                last.then_inc(kq_lo_done, 1)

            def pair_max(i, p):
                dve.wait_ge(s_full, 8 * i + p + 1)
                bank = 2 + 2 * (p % 2)
                heads = slice(2 * (p % 2), 2 * (p % 2) + 2)
                nc.vector.tensor_reduce(top[:, p // 2, 0, heads], ps[0:L, bank:bank + 2, 0:TXT], AX.X, ALU.max)
                nc.vector.tensor_reduce(top[:, p // 2, 1, heads], ps[0:L, bank:bank + 2, TAIL:CTX], AX.X, ALU.max).then_inc(s_done, 1)

            def diagonals(i, g):
                dve.wait_ge(s_done, 8 * i + 2 * g + 2)
                nc.vector.tensor_tensor(shift[:, g].rearrange("l s h q -> l (s h) q"),
                                        neg_ident[:].unsqueeze(1).to_broadcast([L, 2 * GH, L]),
                                        top[:, g].rearrange("l s h -> l (s h)").unsqueeze(2).to_broadcast([L, 2 * GH, L]),
                                        ALU.mult).then_inc(shift_ready, 1)

            def normalise(i, g):
                dve.wait_ge(pv_full, 4 * i + g + 1)
                pv = ps[0:L, 6 + g % 2, 0:GH * 2 * VW].rearrange("l (h s w) -> l h s w", h=GH, s=2)
                nc.vector.reciprocal(rec[:], pv[:, :, :, HD]).then_inc(norm_step, 1)
                dve.wait_ge(norm_step, 8 * i + 2 * g + 1)
                for s in range(2):
                    last = nc.vector.tensor_tensor(o_parts[:, s], pv[:, :, s, 0:HD],
                                                   rec[:, :, s:s + 1].to_broadcast([L, GH, HD]), ALU.mult)
                last.then_inc(norm_step, 1)
                dve.wait_ge(norm_step, 8 * i + 2 * g + 2)
                nc.vector.tensor_tensor(o[:, g * P:(g + 1) * P].rearrange("l (h d) -> l h d", h=GH),
                                        o_parts[:, 0], o_parts[:, 1], ALU.add).then_inc(pv_done, 1)

            def pre():
                ln1(0)
                ln1_finish(0)
                dve.wait_ge(vecs_loaded, 16)
                nc.vector.scalar_tensor_tensor(w_txt[:], nq, SCALE, nk, ALU.mult, ALU.mult)
                nc.vector.scalar_tensor_tensor(w_img[:], nq, SCALE, nki, ALU.mult, ALU.mult)
                nc.vector.tensor_tensor(vbias_cols[:], vb.unsqueeze(2).to_broadcast([P, KC, L]),
                                        vib.unsqueeze(2).to_broadcast([P, KC, L]), ALU.add).then_inc(vecs_ready, 1)
                for j in range(PIECES):
                    dve.wait_ge(piece_hi, j + 1)
                    c2 = slice(2 * (j % 2), 2 * (j % 2) + 2)
                    nc.vector.tensor_tensor(w_lo[W[j // 2]][:, c2, :], stage[:, j % 2, :].rearrange("p (c o) -> p c o", c=2),
                                            w_hi[W[j // 2]][:, c2, :].bitcast(F32), ALU.subtract).then_inc(piece_lo, 1)
                dve.wait_ge(pro_full, 1)
                nc.vector.tensor_tensor(k_tail[:], ps[:, 6, 0:KC * B].rearrange("p (c b) -> p c b", c=KC),
                                        kib.unsqueeze(2).to_broadcast([P, KC, B]), ALU.add).then_inc(pro_done, 1)
                dve.wait_ge(pro_full, 2)
                dve.wait_ge(consts_ready, 3)
                nc.vector.tensor_copy(v_tail[:, :, 0:HD], ps[0:B, 7, :].rearrange("b (h d) -> b h d", h=NH)).then_inc(pro_done, 1)
                dve.wait_ge(pro_full, 3)
                dve.wait_ge(rows_loaded, 32)
                nc.vector.tensor_tensor(out_bias[:], ps[0:L, 6, :], out_bias[:], ALU.add).then_inc(rows_ready, 1)
                xT_rest(0)
                key_evac(0, 1, 1)
                key_evac(0, 2, 3)
                ln1(1)
                scale_kq(0)
                ln1_finish(1)
                value_evac(0)
                kq_rest(0)

            def body(i, n, m):
                if n is not None:
                    xT_rest(n)
                pair_max(i, 0)
                pair_max(i, 1)
                if n is not None:
                    key_evac(n, 1, 1)
                diagonals(i, 0)
                pair_max(i, 2)
                pair_max(i, 3)
                if n is not None:
                    key_evac(n, 2, 3)
                diagonals(i, 1)
                pair_max(i, 4)
                pair_max(i, 5)
                diagonals(i, 2)
                pair_max(i, 6)
                pair_max(i, 7)
                diagonals(i, 3)
                if m is not None:
                    ln1(m)
                normalise(i, 0)
                normalise(i, 1)
                normalise(i, 2)
                if n is not None:
                    scale_kq(n)
                if m is not None:
                    ln1_finish(m)
                normalise(i, 3)
                if n is not None:
                    value_evac(n)
                dve.wait_ge(oT_hi_done, i + 1)
                nc.vector.tensor_tensor(oT_lo[:], bank1[:, 0:KC * L].rearrange("p (c l) -> p c l", c=KC),
                                        oT_hi[:].bitcast(F32), ALU.subtract).then_inc(b1_done, 1)
                if n is not None:
                    kq_rest(n)
                dve.wait_ge(b1_full, slot1_own(i, 2))
                dve.wait_ge(xres_ready, i + 1)
                dve.wait_ge(xh_stored, 16 * i + 16)
                nc.vector.tensor_tensor(xh[:, 0], bank1[0:L], x_res[:], ALU.add).then_inc(b1_done, 1)
                dve.wait_ge(b1_done, slot1_own(i, 2))
                nc.vector.bn_stats(ln2_stats[:], xh[:, 0]).then_inc(ln2_step, 1)
                dve.wait_ge(ln2_step, 3 * i + 1)
                dve.sem_inc(passed, 1)
                nc.vector.bn_aggr(ln2_mv[:], ln2_stats[:]).then_inc(ln2_step, 2)
                dve.wait_ge(ln2_sd_done, i + 1)
                nc.vector.reciprocal(ln2_rstd[:], ln2_sd[:]).then_inc(h_step, 1)
                dve.wait_ge(h_step, i + 1)
                nc.vector.tensor_scalar(xh[:, 1], xh[:, 0], ln2_mv[:, 0:1], ln2_rstd[:], ALU.subtract, ALU.mult).then_inc(h_ready, 1)
                dve.wait_ge(h_ready, i + 1)
                nc.vector.scalar_tensor_tensor(score_junk[:], xh[:, 1], 1.0, wr[:], ALU.mult, ALU.mult,
                                               accum_out=score[:, bass.ds(i, 1)]).then_inc(score_ready, 1)

            over_batches(dve, pre, body)

            dve.wait_ge(score_row_loaded, 16)
            dve.wait_ge(topk_loaded, 16 * 7)
            own = score[:].unsqueeze(2).to_broadcast([L, B, L])
            nc.vector.tensor_tensor(equal[:], score_row[:], own, ALU.is_equal).then_inc(rank_step, 1)
            nc.vector.tensor_tensor(above[:], score_row[:], own, ALU.is_gt).then_inc(rank_step, 1)
            dve.wait_ge(rank_step, 1)
            nc.vector.tensor_tensor(equal[:], equal[:], earlier[:].unsqueeze(1).to_broadcast([L, B, L]), ALU.mult).then_inc(rank_step, 1)
            dve.wait_ge(rank_step, 3)
            nc.vector.tensor_tensor(above[:], above[:], equal[:], ALU.add).then_inc(rank_step, 1)
            dve.wait_ge(rank_step, 4)
            nc.vector.tensor_reduce(rank[:], above[:], AX.X, ALU.add).then_inc(rank_step, 1)
            dve.wait_ge(rank_step, 5)
            nc.vector.tensor_scalar(chosen[:], rank[:], TOPK - 0.5, None, ALU.is_lt).then_inc(chosen_ready, 1)
            dve.wait_ge(before_full, 1)
            nc.vector.scalar_tensor_tensor(before[:], chosen[:], -FAR, ps[0:L, 0, 0:B], ALU.mult, ALU.add).then_inc(rank_step, 1)
            dve.wait_ge(rank_step, 6)
            nc.vector.tensor_tensor(slot_hot[:], before[:].unsqueeze(2).to_broadcast([L, B, TOPK]),
                                    slot_far[:].unsqueeze(1).to_broadcast([L, B, TOPK]), ALU.is_equal).then_inc(hot_ready, 1)
            dve.wait_ge(tok_full, 1)
            nc.vector.tensor_tensor(tok[:], ps[0:L, 1, 0:NC], token_base[:], ALU.add).then_inc(tok_ready, 1)

            def normalise_tokens(k, src):
                dve.wait_ge(root_ready, k + 1)
                nc.vector.reciprocal(rstd[:], rstd[:]).then_inc(rstd_ready, 1)
                dve.wait_ge(rstd_ready, k + 1)
                for c in range(NC):
                    nc.vector.tensor_scalar(normed[:, c], src(c), rstd[:, c:c + 1], None, ALU.mult).then_inc(normed_ready, 1)

            for c in range(NC):
                dve.wait_ge(gathered[c], 16)
                last = nc.vector.scalar_tensor_tensor(normed[:, c], xh_sel[:, c, 1], 1.0, xh_sel[:, c, 1], ALU.mult, ALU.mult,
                                                      accum_out=sums[:, c:c + 1])
            last.then_inc(sums_ready, 1)
            dve.wait_ge(sums_ready, 1)
            for c in range(NC):
                last = nc.vector.scalar_tensor_tensor(normed[:, c], xh_sel[:, c, 1], 1.0, wr[:], ALU.mult, ALU.mult,
                                                      accum_out=sel_score[:, c:c + 1])
            last.then_inc(gate_step, 1)
            dve.wait_ge(gate_step, 1)
            normalise_tokens(0, lambda c: xh_sel[:, c, 1])
            dve.wait_ge(rope_ready, 2)
            for h in range(FH + FKV):
                dve.wait_ge(head_biased, h + 1)
                b = biased[:, h % 2, :]
                dst = qT[:, h, :] if h < FH else kT[:, h - FH, :]
                if h >= 2:
                    dve.wait_ge(head_ready, h - 1)
                r = rot[:, h % 2, :]
                scale = 1.0 if h < FH else FSCALE
                nc.vector.scalar_tensor_tensor(r[0:HALF], b[HALF:P], scale, sin[HALF:P], ALU.mult, ALU.mult)
                nc.vector.scalar_tensor_tensor(r[HALF:P], b[0:HALF], scale, sin[0:HALF], ALU.mult, ALU.mult)
                nc.vector.scalar_tensor_tensor(dst, b, scale, cos[:], ALU.mult, ALU.mult).then_inc(rot_step, 1)
                dve.wait_ge(rot_step, h + 1)
                nc.vector.tensor_tensor(dst, dst, r, ALU.add).then_inc(head_ready, 1)
            dve.wait_ge(fvec_loaded, 32)
            for k in range(2 * NC):
                dve.wait_ge(val_full, k + 1)
                half = slice(512 * (k % 2), 512 * (k % 2) + 512)
                nc.vector.tensor_tensor(vals[:, k // 2, half], ps[0:L, 2 + k % 2, :], bv_row[:, half], ALU.add).then_inc(val_ready, 1)
            dve.wait_ge(gate_exp, 1)
            nc.vector.tensor_scalar(gate_e[:], gate_e[:], 1.0, None, ALU.add).then_inc(gate_step, 1)
            dve.wait_ge(gate_step, 2)
            nc.vector.reciprocal(gate[:], gate_e[:]).then_inc(gate_step, 1)
            dve.wait_ge(gate_step, 3)
            nc.vector.tensor_scalar(gate_e[:], gate[:], -1.0, 1.0, ALU.mult, ALU.add).then_inc(gate_step, 1)
            dve.wait_ge(gate_step, 4)
            for c in range(NC):
                last = nc.vector.scalar_tensor_tensor(keep[:, c], xh_sel[:, c, 1], gate_e[:, c:c + 1], xh_sel[:, c, 0], ALU.mult, ALU.add)
            last.then_inc(gate_step, 1)

            def scale_probs(k):
                c = k % NC
                dve.wait_ge(prob_ready, k + 1)
                nc.vector.reciprocal(prob_sum[:, c:c + 1], prob_sum[:, c:c + 1]).then_inc(inv_ready, 1)
                dve.wait_ge(inv_ready, k + 1)
                part = prob2[:, k % 2, 0:(c + 1) * L]
                nc.vector.tensor_scalar(part, part, prob_sum[:, c:c + 1], None, ALU.mult).then_inc(prob_scaled, 1)

            for k in range(FH * NC + 3):
                c = k % NC
                if k < FH * NC:
                    dve.wait_ge(att_full, k + 1)
                    nc.vector.tensor_reduce(neg_top[:, c:c + 1], ps[0:L, c, 0:(c + 1) * L], AX.X, ALU.max, negate=True).then_inc(top_ready, 1)
                if 1 <= k <= FH * NC:
                    scale_probs(k - 1)
                if c == 2 and k >= NC:
                    h = k // NC - 1
                    dve.wait_ge(attn_full, h + 1)
                    nc.vector.tensor_copy(attnT[:, h, :], ps[:, 6 + h % 2, 0:S]).then_inc(attn_ready, 1)
            for c in range(NC):
                dve.wait_ge(mid_full, c + 1)
                nc.vector.tensor_tensor(x_mid[:, c], ps[0:L, c, :], xh_sel[:, c, 1], ALU.add).then_inc(mid_ready, 1)
            for c in range(NC):
                dve.wait_ge(mid_ready, c + 1)
                last = nc.vector.scalar_tensor_tensor(normed[:, c], x_mid[:, c], 1.0, x_mid[:, c], ALU.mult, ALU.mult,
                                                      accum_out=sums[:, c:c + 1])
            last.then_inc(sums_ready, 1)
            dve.wait_ge(sums_ready, 2)
            normalise_tokens(1, lambda c: x_mid[:, c])
            for j in range(FC):
                e = silu_e[:, j % 2, :]
                g, u = (ps[:, 2 * (j % 2) + a, 0:S] for a in range(2))
                dve.wait_ge(silu_exp, j + 1)
                nc.vector.tensor_scalar(e, e, 1.0, None, ALU.add).then_inc(silu_step, 1)
                dve.wait_ge(silu_step, 3 * j + 1)
                nc.vector.reciprocal(e, e).then_inc(silu_step, 1)
                dve.wait_ge(silu_step, 3 * j + 2)
                nc.vector.tensor_tensor(silu_g[:, j % 2, :], g, e, ALU.mult).then_inc(silu_step, 1)
                dve.wait_ge(silu_step, 3 * j + 3)
                nc.vector.tensor_tensor(mT[:, j, :], u, silu_g[:, j % 2, :], ALU.mult).then_inc(hid_ready, 1)
            dve.wait_ge(gate_step, 5)
            for c in range(NC):
                dve.wait_ge(down_full, c + 1)
                nc.vector.tensor_tensor(x_mid[:, c], ps[0:L, 4 + c, :], x_mid[:, c], ALU.add).then_inc(sum_ready, 1)
                dve.wait_ge(sum_ready, c + 1)
                nc.vector.scalar_tensor_tensor(keep[:, c], x_mid[:, c], gate[:, c:c + 1], keep[:, c], ALU.mult, ALU.add).then_inc(final_ready, 1)

        @block.tensor
        def _(pe):
            def mm3(o_, a_hi, a_lo, b_hi, b_lo, start, stop):
                nc.tensor.matmul(o_, a_hi, b_hi, start=start, stop=False)
                nc.tensor.matmul(o_, a_hi, b_lo, start=False, stop=False)
                return nc.tensor.matmul(o_, a_lo, b_hi, start=False, stop=stop)

            def transpose_x(n):
                pe.wait_ge(xn_ready, n + 1)
                if not isinstance(n, int) or n >= 1:
                    pe.wait_ge(b1_done, slot1(n, 0))
                for c in range(KC):
                    last = nc.tensor.transpose(bank1[:, c * L:(c + 1) * L], xn[:, c * P:(c + 1) * P], ident[0:L, 0:L])
                last.then_inc(b1_full, 1)

            def keys(n, c):
                oc = slice(c * P, (c + 1) * P)
                if c == 0:
                    pe.wait_ge(ctx_lo_done, n + 1)
                if c % 2 == 0:
                    pe.wait_ge(b0_done, slot0(n, c // 2))
                else:
                    pe.wait_ge(b1_done, slot1(n, 1 + c // 2))
                bank = (bank0, bank1)[c % 2]
                for o_, cols, w in ((bank[:, 0:TXT], slice(0, TXT), "k"), (bank[:, TXT:CTXC], slice(TXT, CTXC), "k_img")):
                    for kc in range(KC):
                        last = mm3(o_, w_hi[w][:, kc, oc], w_lo[w][:, kc, oc], ctx_hi[:, kc, cols], ctx_lo[:, kc, cols],
                                   kc == 0, kc == KC - 1)
                last.then_inc((b0_full, b1_full)[c % 2], 1)

            def queries(n):
                pe.wait_ge(b0_done, slot0(n, 2))
                pe.wait_ge(b1_done, slot1(n, 1))
                for c in range(KC):
                    oc = slice(c * P, (c + 1) * P)
                    for kc in range(KC):
                        last = mm3(bank0[:, c * L:(c + 1) * L], w_hi["q"][:, kc, oc], w_lo["q"][:, kc, oc],
                                   xT_hi[:, kc, :], xT_lo[:, kc, :], kc == 0, kc == KC - 1)
                last.then_inc(b0_full, 1)

            def square_sums(n):
                pe.wait_ge(sq_ready, n + 1)
                pe.wait_ge(b0_done, slot0(n, 3))
                nc.tensor.matmul(bank0[:, 0:RAWC], ones[:], sq_sum[:], start=True, stop=True).then_inc(b0_full, 1)

            def values(n, k):
                cols, w, rows = ((slice(TXT, TXT + P), "v_img", P), (slice(TXT + P, CTXC), "v_img", P), (slice(0, TXT), "v", TXT))[k]
                if k == 1:
                    pe.wait_ge(b1_done, slot1(n, 3))
                else:
                    pe.wait_ge(b0_done, slot0(n, 4 + k // 2))
                bank = (bank0, bank1)[k % 2]
                for kc in range(KC):
                    last = mm3(bank[0:rows], ctx_hi[:, kc, cols], ctx_lo[:, kc, cols], w_hi[w][:, kc, :], w_lo[w][:, kc, :],
                               kc == 0, kc == KC - 1)
                last.then_inc((b0_full, b1_full)[k % 2], 1)

            def scores(i, p):
                if p == 0:
                    pe.wait_ge(k_hi_done, i + 1)
                    pe.wait_ge(q_hi_done, i + 1)
                if p >= 2:
                    pe.wait_ge(s_done, 8 * i + p - 1)
                for e in range(2):
                    g, j = p // 2, 2 * (p % 2) + e
                    last = nc.tensor.matmul(ps[0:L, 2 + 2 * (p % 2) + e, 0:NKEY], q_hi[:, g, j, :], k_hi[:, g, :], start=True, stop=True)
                last.then_inc(s_full, 1)

            def scores_T(i, g):
                pe.wait_ge(shift_ready, 4 * i + g + 1)
                if g == 0:
                    pe.wait_ge(s_done, 8 * i + 8)
                    pe.wait_ge(kq_lo_done, i + 1)
                for c, (at, rows) in enumerate(CHUNKS):
                    k = 3 * g + c
                    if k >= 4:
                        pe.wait_ge(exp_done, 12 * i + k - 3)
                    o_ = ps[0:rows, 2 + k % 4, 0:GH * L]
                    cols = slice(at, at + rows)
                    q = [x[:, g].rearrange("p h q -> p (h q)") for x in (q_hi, q_lo)]
                    sh = [shift[:, g, s].rearrange("l h q -> l (h q)") for s in range(2)]
                    mm3(o_, k_hi[:, g, cols], k_lo[:, g, cols], q[0], q[1], True, False)
                    if c == 0:
                        nc.tensor.matmul(o_, ones_c_txt[:], sh[0], start=False, stop=False)
                        last = nc.tensor.matmul(o_, ones_c_tail[:], sh[1], start=False, stop=True)
                    else:
                        last = nc.tensor.matmul(o_, ones_img[:], sh[1], start=False, stop=True)
                    last.then_inc(st_full, 1)

            def weighted_values(i, g):
                pe.wait_ge(exp_done, 12 * i + 3 * g + 3)
                if g == 0:
                    pe.wait_ge(vtail_loaded, 16 * i + 16)
                    pe.wait_ge(b0_done, slot0(i, 6))
                if g >= 2:
                    pe.wait_ge(pv_done, 4 * i + g - 1)
                for j in range(GH):
                    h, at = GH * g + j, 2 * VW * j
                    qs = slice(L * j, L * (j + 1))
                    bank = ps[0:L, 6 + g % 2, :]
                    nc.tensor.matmul(bank[:, at:at + 2 * VW], prob[0:CHUNK_C, g % 2, 0, qs], v_c[:, h, :], start=True, stop=False)
                    nc.tensor.matmul(bank[:, at:at + VW], prob[:, g % 2, 1, qs], v_a[:, h, :], start=False, stop=False)
                    last = nc.tensor.matmul(bank[:, at:at + VW], prob[:, g % 2, 2, qs], v_b[:, h, :], start=False, stop=True)
                last.then_inc(pv_full, 1)

            def pre():
                pe.wait_ge(tails_loaded, 16)
                pe.wait_ge(consts_ready, 1)
                pe.wait_ge(vecs_ready, 1)
                transpose_x(0)
                pe.wait_ge(piece_lo, PIECES)
                for c in range(KC):
                    for kc in range(KC):
                        oc = slice(c * P, (c + 1) * P)
                        for w in (w_hi, w_lo):
                            last = nc.tensor.matmul(ps[:, 6, c * B:(c + 1) * B], w["k_img"][:, kc, oc].bitcast(F32), ctx_tail[:, kc, :],
                                                    start=kc == 0 and w is w_hi, stop=kc == KC - 1 and w is w_lo)
                last.then_inc(pro_full, 1)
                for kc in range(KC):
                    for w in (w_hi, w_lo):
                        last = nc.tensor.matmul(ps[0:B, 7, :], ctx_tail[:, kc, :], w["v_img"][:, kc, :].bitcast(F32),
                                                start=kc == 0 and w is w_hi, stop=kc == KC - 1 and w is w_lo)
                last.then_inc(pro_full, 1)
                pe.wait_ge(pro_done, 1)
                for kc in range(KC):
                    for w in (w_hi, w_lo):
                        last = nc.tensor.matmul(ps[0:L, 6, :], vbias_cols[:, kc, :], w["o"][:, kc, :].bitcast(F32),
                                                start=kc == 0 and w is w_hi, stop=kc == KC - 1 and w is w_lo)
                last.then_inc(pro_full, 1)
                for c in range(KC):
                    keys(0, c)
                queries(0)
                square_sums(0)
                for k in range(3):
                    values(0, k)
                pe.wait_ge(rows_ready, 1)

            def body(i, n, m):
                if n is not None:
                    transpose_x(n)
                for p in range(8):
                    scores(i, p)
                    if n is not None and p < 4:
                        keys(n, p)
                    if n is not None and p == 4:
                        queries(n)
                scores_T(i, 0)
                scores_T(i, 1)
                weighted_values(i, 0)
                scores_T(i, 2)
                weighted_values(i, 1)
                scores_T(i, 3)
                weighted_values(i, 2)
                if n is not None:
                    square_sums(n)
                weighted_values(i, 3)
                if n is not None:
                    for k in range(3):
                        values(n, k)
                pe.wait_ge(pv_done, 4 * i + 4)
                pe.wait_ge(b1_done, slot1_own(i, 0))
                for c in range(KC):
                    last = nc.tensor.transpose(bank1[:, c * L:(c + 1) * L], o[:, c * P:(c + 1) * P], ident[0:L, 0:L])
                last.then_inc(b1_full, 1)
                pe.wait_ge(b1_done, slot1_own(i, 1))
                for kc in range(KC):
                    last = mm3(bank1[0:L], oT_hi[:, kc, :], oT_lo[:, kc, :], w_hi["o"][:, kc, :], w_lo["o"][:, kc, :], kc == 0, kc == KC - 1)
                last.then_inc(b1_full, 1)

            over_batches(pe, pre, body)

            pe.wait_ge(chosen_ready, 1)
            nc.tensor.matmul(ps[0:L, 0, 0:B], later[:], chosen[:], start=True, stop=True).then_inc(before_full, 1)
            pe.wait_ge(hot_ready, 1)
            hot = slot_hot[:].rearrange("l b k -> l (b k)")
            for c in range(NC):
                last = nc.tensor.matmul(ps[0:L, 1, c:c + 1], hot[:, c * L:(c + 1) * L], token_no[:], start=True, stop=True)
            last.then_inc(tok_full, 1)
            for k, table in enumerate((cos_tab, sin_tab)):
                nc.tensor.matmul(ps[:, 2 + k, 0:S], table[:], hot, start=True, stop=True).then_inc(rope_full, 1)

            def turn_tokens(k):
                pe.wait_ge(normed_ready, NC * k + NC)
                for kc in range(KC):
                    for c in range(NC):
                        last = nc.tensor.transpose(ps[:, 4 + kc, c * L:(c + 1) * L], normed[:, c, kc * P:(kc + 1) * P], ident[0:L, 0:L])
                    last.then_inc(hT_full, 1)

            turn_tokens(0)
            pe.wait_ge(hT_ready, KC)
            for h in range(FH + FKV):
                w, hh = (wq, h) if h < FH else (wk, h - FH)
                if h == 0:
                    pe.wait_ge(ring_loaded[0], 16)
                if h == FH:
                    pe.wait_ge(ring_loaded[1], 32)
                if h >= 2:
                    pe.wait_ge(head_biased, h - 1)
                for kc in range(KC):
                    last = nc.tensor.matmul(ps[:, h % 2, 0:S], w[:, kc, hh * FD:(hh + 1) * FD], hT[:, kc, :], start=kc == 0, stop=kc == KC - 1)
                last.then_inc(head_full, 1)
            for k in range(2 * NC):
                if k >= 2:
                    pe.wait_ge(val_ready, k - 1)
                c, half = k // 2, slice(512 * (k % 2), 512 * (k % 2) + 512)
                for kc in range(KC):
                    last = nc.tensor.matmul(ps[0:L, 2 + k % 2, :], hT[:, kc, c * L:(c + 1) * L], wv[:, kc, half], start=kc == 0, stop=kc == KC - 1)
                last.then_inc(val_full, 1)

            def att(k):
                h, c = k // NC, k % NC
                if c == 0:
                    pe.wait_ge(head_ready, FH + h // 2 + 1)
                if k >= NC:
                    pe.wait_ge(prob_ready, k - NC + 1)
                o_ = ps[0:L, c, 0:(c + 1) * L]
                nc.tensor.matmul(o_, qT[:, h, c * L:(c + 1) * L], kT[:, h // 2, 0:(c + 1) * L], start=True, stop=False)
                nc.tensor.matmul(o_[:, c * L:(c + 1) * L], ident_bf[:], causal[:], start=False, stop=True).then_inc(att_full, 1)

            def turn_probs(k):
                c = k % NC
                pe.wait_ge(prob_scaled, k + 1)
                if k >= 2:
                    pe.wait_ge(pT_ready, k - 1)
                for b in range(c + 1):
                    last = nc.tensor.transpose(ps[0:L, 4 + k % 2, b * L:(b + 1) * L], prob2[:, k % 2, b * L:(b + 1) * L], ident[0:L, 0:L])
                last.then_inc(pT_full, 1)

            def weigh(h):
                pe.wait_ge(pT_ready, NC * h + NC)
                if h >= 2:
                    pe.wait_ge(attn_ready, h - 1)
                for b in range(NC):
                    last = nc.tensor.matmul(ps[:, 6 + h % 2, b * L:S], vals[:, b, (h // 2) * FD:(h // 2 + 1) * FD], probT[:, b, b * L:S],
                                            start=b == 0, stop=b == NC - 1)
                last.then_inc(attn_full, 1)

            pe.wait_ge(consts2, 2)
            pe.wait_ge(val_ready, 2 * NC)
            for k in range(FH * NC + 3):
                if k < FH * NC:
                    att(k)
                if 2 <= k < FH * NC + 2:
                    turn_probs(k - 2)
                if k >= NC and k % NC == 2:
                    weigh(k // NC - 1)
            pe.wait_ge(ring_loaded[2], 16)
            pe.wait_ge(attn_ready, FH)
            for c in range(NC):
                for h in range(FH):
                    last = nc.tensor.matmul(ps[0:L, c, :], attnT[:, h, c * L:(c + 1) * L], wo[:, h, :], start=h == 0, stop=h == FH - 1)
                last.then_inc(mid_full, 1)
            turn_tokens(1)
            pe.wait_ge(hT_ready, 2 * KC)
            pe.wait_ge(mid_ready, NC)
            pe.wait_ge(ring_loaded[0], 32)
            pe.wait_ge(ring_loaded[1], 48)

            def down(j):
                pe.wait_ge(hid_ready, j + 1)
                if j == 0:
                    pe.wait_ge(ring_loaded[2], 32)
                for c in range(NC):
                    last = nc.tensor.matmul(ps[0:L, 4 + c, :], mT[:, j, c * L:(c + 1) * L], w_down[:, j, :], start=j == 0, stop=j == FC - 1)
                    if j == FC - 1:
                        last.then_inc(down_full, 1)

            for j in range(FC + 2):
                if j < FC:
                    if j >= 2:
                        pe.wait_ge(hid_ready, j - 1)
                    for a, w in enumerate((w_gate, w_up)):
                        for kc in range(KC):
                            last = nc.tensor.matmul(ps[:, 2 * (j % 2) + a, 0:S], w[:, kc, j * P:(j + 1) * P], hT[:, kc, :], start=kc == 0, stop=kc == KC - 1)
                    last.then_inc(mlp_full, 1)
                if j >= 2:
                    down(j - 2)


def kernel(**inputs):
    import numpy as np
    import concourse.bacc as bacc
    from concourse.bass_utils import run_bass_kernel_spmd as run

    nc = bacc.Bacc("TRN2", target_bir_lowering=False, num_devices=1)
    a = {k: np.asarray(v) for k, v in inputs.items()}
    c, f = np.ascontiguousarray, np.float32

    def columns(v):
        return v.reshape(KC, P).T

    x_ = "L0_xattn_"
    ctxT = a["ctx_2048"].transpose(0, 2, 1)
    order = np.concatenate([np.arange(IMG, CTX), np.arange(IMG_MAIN)])
    arrays = {
        "x": c(a["x"]),
        "ctx": c(ctxT[:, :, order].reshape(B, KC, P, CTXC).transpose(0, 2, 1, 3)),
        "ctx_tail": c(ctxT[:, :, IMG_MAIN].T.reshape(KC, P, B).transpose(1, 0, 2)),
        "vecs": c(np.stack([columns(a[x_ + n]) for n in ("q_b", "k_b", "k_img_b", "v_b", "v_img_b", "norm_q_w", "norm_k_w", "norm_k_img_w")], 1)),
        "o_b": c(a[x_ + "o_b"]),
        "w_router": c(a["L0_ffn_w_router"]),
    }
    f_ = "L0_ffn_"
    arrays["fvec"] = c(np.concatenate([a[f_ + "bq"].reshape(FH, FD).T, a[f_ + "bk"].reshape(FKV, FD).T,
                                       columns(a[f_ + "ln1_w"]), columns(a[f_ + "ln2_w"])], 1))
    arrays["bv"] = c(a[f_ + "bv"])
    for w in ("wq", "wk", "wv", "wo", "w_gate", "w_up", "w_down"):
        arrays[w] = c(a[f_ + w])
    token = np.arange(L)
    arrays["earlier"] = (token[None, :] < token[:, None]).astype(f)
    arrays["later"] = (token[None, :] > token[:, None]).astype(f)
    arrays["slot_far"] = np.broadcast_to(np.arange(TOPK, dtype=f) - f(FAR), (L, TOPK)).copy()
    arrays["token_no"] = token.astype(f)[:, None].copy()
    arrays["token_base"] = (L * (BPC * np.arange(NC)[None, :] + token[:, None] // TOPK)).astype(f)
    freq = f(1.0) / np.power(f(10000.0), np.arange(0, FD, 2, dtype=f) / f(FD))
    angle = token.astype(f)[:, None] * freq
    arrays["cos_tab"] = np.concatenate([np.cos(angle), np.cos(angle)], 1).astype(f)
    arrays["sin_tab"] = np.concatenate([np.sin(angle), -np.sin(angle)], 1).astype(f)
    for w in ("q", "k", "v", "k_img", "v_img", "o"):
        arrays["w_" + w] = c(a[x_ + w + "_w"].T)
    feeds, t = {}, {}
    for k, v in arrays.items():
        feeds[f"in_{k}_dram"] = v
        t[k] = nc.dram_tensor(f"in_{k}_dram", v.shape, mybir.dt.from_np(v.dtype), kind="ExternalInput").ap()
    out = nc.dram_tensor("out_dram", (B, L, D), F32, kind="ExternalOutput").ap()
    build(nc, t, out)
    r = run(nc, [feeds], core_ids=[0])
    return r.results[0]["out_dram"]
```

```python
from contextlib import ExitStack

import concourse.bass as bass
from concourse import mybir

ACT = mybir.ActivationFunctionType
ALU = mybir.AluOpType
AX = mybir.AxisListType
F32 = mybir.dt.float32
F32R = mybir.dt.float32r
BF16 = mybir.dt.bfloat16

B, L, D = 32, 112, 512
IMG, CTX = 257, 375
TXT = CTX - IMG
NH, HD = 16, 32
P = 128
KC = D // P
GH = P // HD
NG = NH // GH
IMG_MAIN = IMG - 1
TAIL = TXT
NKEY = CTX + 1
CHUNK_C = TXT + 1
CTXC = TXT + IMG_MAIN
TOK_ROWS = (L, TXT, P, P)
KEY_AT = (None, 0, TAIL + 1, TAIL + 1 + P)
VW = HD + 1
LN_EPS, RMS_EPS = 1e-5, 1e-6
SCALE = HD ** -0.5
CHUNKS = [(0, CHUNK_C), (CHUNK_C, P), (CHUNK_C + P, P)]
TOPK = max(1, int(L * 0.125))
S = B * TOPK
NC = S // L
BPC = B // NC
FH, FKV, FD = 16, 8, 128
FF = 2048
FC = FF // P
FSCALE = FD ** -0.5
HALF = FD // 2
MASKED = -1e30
FAR = 1000.0


def build(nc, t, out):
    with ExitStack() as ctx:
        def sb(name, shape, dt=F32):
            return ctx.enter_context(nc.sbuf_tensor(name, shape, dt))

        def sem(name):
            return ctx.enter_context(nc.semaphore(name))

        ps = ctx.enter_context(nc.psum_tensor("ps", [P, 8, 512], F32))
        bank0, bank1 = ps[:, 0, :], ps[:, 1, :]
        vtail_dram = nc.dram_tensor("vtail_dram", (B, NH * VW), F32, kind="Internal").ap()
        xh_dram = nc.dram_tensor("xh_dram", (B * L, 2 * D), F32, kind="Internal").ap()
        score_dram = nc.dram_tensor("score_dram", (B, L), F32, kind="Internal").ap()

        ident = sb("ident", [P, P])
        ln_eps = sb("ln_eps", [P, 1])
        rms_eps = sb("rms_eps", [P, 1])
        wr = sb("wr", [L, D])
        score = sb("score", [L, B])

        phase1 = ExitStack()

        def p1(name, shape, dt=F32):
            return phase1.enter_context(nc.sbuf_tensor(name, shape, dt))

        neg_ident = p1("neg_ident", [L, L], BF16)
        ones_img = p1("ones_img", [L, P], BF16)
        ones_c_txt = p1("ones_c_txt", [L, CHUNK_C], BF16)
        ones_c_tail = p1("ones_c_tail", [L, CHUNK_C], BF16)
        W = ["k", "q", "k_img", "v_img", "v", "o"]
        w_hi = {w: p1(f"w_{w}_hi", [P, KC, D], F32R) for w in W}
        w_lo = {w: p1(f"w_{w}_lo", [P, KC, D], F32R) for w in W}
        vecs = p1("vecs", [P, 2, KC])
        q_bias, k_bias, ki_bias = (p1(n, [P, D]) for n in ("q_bias", "k_bias", "ki_bias"))
        nq_row = q_bias
        w_txt = p1("w_txt", [P, D])
        w_img = p1("w_img", [P, D])
        out_bias = p1("out_bias", [L, D])
        k_tail_hi = p1("k_tail_hi", [P, KC, B], F32R)
        k_tail_lo = p1("k_tail_lo", [P, KC, B], F32R)
        ctx_raw = p1("ctx_raw", [P, KC, CTXC])
        ctx_hi = p1("ctx_hi", [P, KC, CTXC], F32R)
        ctx_lo = p1("ctx_lo", [P, KC, CTXC], F32R)
        x_in = p1("x_in", [L, D])
        xn = x_in
        ln1_stats = p1("ln1_stats", [L, 6])
        ln1_mv = p1("ln1_mv", [L, 2])
        ln1_sd = p1("ln1_sd", [L, 1])
        ln1_rstd = p1("ln1_rstd", [L, 1])
        xT_hi = p1("xT_hi", [P, KC, L], F32R)
        xT_lo = p1("xT_lo", [P, KC, L], F32R)
        proj = p1("proj", [P, 4, D])
        sq_junk = p1("sq_junk", [P, D], BF16)
        sq_sum = p1("sq_sum", [P, 5])
        rms = p1("rms", [P, 5])
        rstd1 = p1("rstd1", [P, 5])
        k_hi = p1("k_hi", [P, KC, NKEY], F32R)
        k_lo = p1("k_lo", [P, KC, NKEY], F32R)
        q_hi = p1("q_hi", [P, NG, GH, L], F32R)
        q_lo = p1("q_lo", [P, NG, GH, L], F32R)
        v_c = p1("v_c", [CHUNK_C, NH, 2 * VW])
        v_a = p1("v_a", [P, NH, VW])
        v_b = p1("v_b", [P, NH, VW])
        top = p1("top", [L, NG, 2, GH])
        shift = p1("shift", [L, NG, 2, GH, L], BF16)
        prob = p1("prob", [P, 2, 3, GH * L])
        prob_flat = prob[:].rearrange("p a c n -> p (a c n)")
        stage = prob_flat[:, 0:4 * D].rearrange("p (a n) -> p a n", a=2)
        vbias_cols = prob_flat[:, 4 * D:4 * D + KC * L].rearrange("p (c l) -> p c l", c=KC)
        ctx_tail = prob_flat[:, 4 * D + KC * L:4 * D + KC * (L + B)].rearrange("p (c b) -> p c b", c=KC)
        rec = p1("rec", [L, GH, 2])
        o_parts = p1("o_parts", [L, 2, GH, HD])
        o = p1("o", [L, D])
        tail_proj = o[0:B]
        oT_hi, oT_lo = xT_hi, xT_lo
        x_res = p1("x_res", [L, D])
        xh = p1("xh", [L, 2, D])
        ln2_stats = p1("ln2_stats", [L, 6])
        ln2_mv = p1("ln2_mv", [L, 2])
        ln2_sd = p1("ln2_sd", [L, 1])
        ln2_rstd = p1("ln2_rstd", [L, 1])
        out_sb = p1("out_sb", [L, D])
        score_junk = out_sb
        v_tail = xh[0:B].rearrange("b a d -> b (a d)")[:, 0:NH * VW].rearrange("b (h w) -> b h w", h=NH)

        phase1.close()
        ring = [sb(f"ring{j}", [P, 4 * FF]) for j in range(3)]
        wq = ring[0][:].rearrange("p (c n) -> p c n", c=KC)
        wk = ring[1][:, 0:2 * FF].rearrange("p (c n) -> p c n", c=KC)
        wv = ring[1][:, 2 * FF:4 * FF].rearrange("p (c n) -> p c n", c=KC)
        wo = ring[2][:].rearrange("p (c n) -> p c n", c=FH)
        w_gate = ring[0][:].rearrange("p (c n) -> p c n", c=KC)
        w_up = ring[1][:].rearrange("p (c n) -> p c n", c=KC)
        w_down = ring[2][:].rearrange("p (c n) -> p c n", c=FC)
        fvec = sb("fvec", [P, FH + FKV + 2 * KC])
        bv_row = sb("bv_row", [L, FKV * FD])
        tok = sb("tok", [L, NC], mybir.dt.int32)
        token_base = sb("token_base", [L, NC])
        xh_sel = sb("xh_sel", [L, NC, 2, D])
        sel_score = sb("sel_score", [L, NC])
        gate_e = sb("gate_e", [L, NC])
        gate = sb("gate", [L, NC])
        keep = xh_sel[:, :, 0, :]
        sums = sb("sums", [L, NC])
        rstd = sb("rstd", [L, NC])
        normed = sb("normed", [L, NC, D])
        hT = sb("hT", [P, KC, S])
        cos = sb("cos", [P, S])
        sin = sb("sin", [P, S])
        topk = ExitStack()

        def tk(name, shape, dt=F32):
            return topk.enter_context(nc.sbuf_tensor(name, shape, dt))

        score_row = tk("score_row", [L, B, L])
        above = tk("above", [L, B, L])
        equal = tk("equal", [L, B, L])
        rank = tk("rank", [L, B])
        chosen = tk("chosen", [L, B])
        before = tk("before", [L, B])
        slot_hot = tk("slot_hot", [L, B, TOPK])
        earlier = tk("earlier", [L, L])
        later = tk("later", [L, L])
        slot_far = tk("slot_far", [L, TOPK])
        token_no = tk("token_no", [L, 1])
        cos_tab = tk("cos_tab", [L, P])
        sin_tab = tk("sin_tab", [L, P])
        topk.close()
        qT = sb("qT", [P, FH, S])
        attnT, mT = qT, qT
        kT = sb("kT", [P, FKV, S])
        vals = sb("vals", [L, NC, FKV * FD])
        x_mid = vals[:, :, 0:D]
        biased = sb("biased", [P, 2, S])
        rot = sb("rot", [P, 2, S])
        causal = sb("causal", [L, L], BF16)
        ident_bf = sb("ident_bf", [L, L], BF16)
        neg_top = sb("neg_top", [L, NC])
        prob_sum = sb("prob_sum", [L, NC])
        prob2 = sb("prob2", [L, 2, S])
        probT = normed[:].rearrange("l c d -> l (c d)")[:, 0:NC * S].rearrange("l (c s) -> l c s", c=NC)
        silu_e = biased
        silu_g = rot

        consts_zeroed, consts_ready = sem("consts_zeroed"), sem("consts_ready")
        vecs_loaded, rows_loaded, tails_loaded = sem("vecs_loaded"), sem("rows_loaded"), sem("tails_loaded")
        piece_loaded = [sem("piece_loaded0"), sem("piece_loaded1")]
        piece_hi, piece_lo = sem("piece_hi"), sem("piece_lo")
        vecs_ready = sem("vecs_ready")
        pro_full, pro_done, vtail_stored = sem("pro_full"), sem("pro_done"), sem("vtail_stored")
        ctx_loaded, ctx_hi_done, ctx_lo_done = sem("ctx_loaded"), sem("ctx_hi_done"), sem("ctx_lo_done")
        x_loaded, ln1_step, ln1_sd_done = sem("x_loaded"), sem("ln1_step"), sem("ln1_sd_done")
        xn_ready, xT_hi_done = sem("xn_ready"), sem("xT_hi_done")
        b0_full, b0_done, b1_full, b1_done = sem("b0_full"), sem("b0_done"), sem("b1_full"), sem("b1_done")
        xT_full, xT_lo_done = sem("xT_full"), sem("xT_lo_done")
        sq_done, rms_done, rms_inv = sem("sq_done"), sem("rms_done"), sem("rms_inv")
        scaled, turned, k_hi_done, q_hi_done = sem("scaled"), sem("turned"), sem("k_hi_done"), sem("q_hi_done")
        tail_step, tail_scaled, tail_turned = sem("tail_step"), sem("tail_scaled"), sem("tail_turned")
        tail_hi_done, tail_ready = sem("tail_hi_done"), sem("tail_ready")
        kq_lo_done, vtail_loaded = sem("kq_lo_done"), sem("vtail_loaded")
        s_full, s_done, shift_ready = sem("s_full"), sem("s_done"), sem("shift_ready")
        st_full, exp_done = sem("st_full"), sem("exp_done")
        pv_full, norm_step, pv_done = sem("pv_full"), sem("norm_step"), sem("pv_done")
        oT_hi_done, xres_loaded, xres_ready = sem("oT_hi_done"), sem("xres_loaded"), sem("xres_ready")
        ln2_step, ln2_sd_done, h_ready = sem("ln2_step"), sem("ln2_sd_done"), sem("h_ready")
        h_step, rows_ready, passed = sem("h_step"), sem("rows_ready"), sem("passed")
        score_ready, out_ready = sem("score_ready"), sem("out_ready")
        xh_stored, out_stored, score_stored = sem("xh_stored"), sem("out_stored"), sem("score_stored")

        topk_loaded, score_row_loaded, fvec_loaded = sem("topk_loaded"), sem("score_row_loaded"), sem("fvec_loaded")
        ring_loaded = [sem(f"ring_loaded{j}") for j in range(3)]
        rank_step, chosen_ready, before_full, hot_ready = sem("rank_step"), sem("chosen_ready"), sem("before_full"), sem("hot_ready")
        tok_full, tok_ready, rope_full, rope_ready = sem("tok_full"), sem("tok_ready"), sem("rope_full"), sem("rope_ready")
        gathered = [sem(f"gathered{c}") for c in range(NC)]
        sums_ready, root_ready, rstd_ready, normed_ready = sem("sums_ready"), sem("root_ready"), sem("rstd_ready"), sem("normed_ready")
        hT_full, hT_ready = sem("hT_full"), sem("hT_ready")
        head_full, head_biased, rot_step, head_ready = sem("head_full"), sem("head_biased"), sem("rot_step"), sem("head_ready")
        val_full, val_ready = sem("val_full"), sem("val_ready")
        att_full, top_ready, prob_ready = sem("att_full"), sem("top_ready"), sem("prob_ready")
        inv_ready, prob_scaled, pT_full, pT_ready = sem("inv_ready"), sem("prob_scaled"), sem("pT_full"), sem("pT_ready")
        attn_full, attn_ready = sem("attn_full"), sem("attn_ready")
        mid_full, mid_ready = sem("mid_full"), sem("mid_ready")
        mlp_full, silu_exp, silu_step, hid_ready = sem("mlp_full"), sem("silu_exp"), sem("silu_step"), sem("hid_ready")
        down_full, sum_ready, final_ready, scattered = sem("down_full"), sem("sum_ready"), sem("final_ready"), sem("scattered")
        gate_step, gate_exp, consts2 = sem("gate_step"), sem("gate_exp"), sem("consts2")
        blocks_read = sem("blocks_read")

        block = ctx.enter_context(nc.Block())

        def slot1(n, k):
            return 5 * n - 2 + k if not isinstance(n, int) or n else k

        def slot1_own(i, k):
            return 5 * i + 5 + k if not isinstance(i, int) or i < B - 1 else 5 * i + 3 + k

        def over_batches(eng, pre, body):
            pre()
            body(0, 1, 2, None)
            with eng.Fori(1, B - 2) as i:
                body(i, i + 1, i + 2, i - 1)
            body(B - 2, B - 1, None, B - 3)
            body(B - 1, None, None, B - 2)

        PIECES = 2 * len(W)

        @block.sync
        def _(sp):
            sp.dma_start(vecs[:], t["vecs"]).then_inc(vecs_loaded, 16)
            sp.dma_start(ctx_tail, t["ctx_tail"]).then_inc(tails_loaded, 16)

            def load_x(m):
                sp.dma_start(x_in[:], t["x"][bass.ds(m, 1)].rearrange("o t d -> t (o d)")).then_inc(x_loaded, 16)

            def load_ctx(n):
                sp.dma_start(ctx_raw[:], t["ctx"][bass.ds(n, 1)].rearrange("o p c n -> p (o c) n")).then_inc(ctx_loaded, 16)

            def load_piece(j):
                sp.dma_start(stage[:, j % 2, :], t["w_" + W[j // 2]].rearrange(
                    "(c p) o -> p c o", p=P)[:, 2 * (j % 2):2 * (j % 2) + 2, :]).then_inc(piece_loaded[j % 2], 16)

            def load_tail(n):
                sp.dma_start(v_c[TXT:TXT + 1, :, 0:VW], vtail_dram[bass.ds(n, 1)].rearrange(
                    "o (h w) -> o h w", h=NH)).then_inc(vtail_loaded, 16)

            def store(p):
                sp.wait_ge(score_ready, p + 1)
                sp.dma_start(xh_dram.rearrange("(b l) d -> b l d", b=B)[bass.ds(p, 1)].rearrange("o l d -> l (o d)"),
                             xh[:].rearrange("l a d -> l (a d)")).then_inc(xh_stored, 16)
                sp.dma_start(score_dram[bass.ds(p, 1)].rearrange("o l -> l o"), score[:, bass.ds(p, 1)]).then_inc(score_stored, 16)
                sp.wait_ge(out_ready, p + 1)
                sp.dma_start(out[bass.ds(p, 1)].rearrange("o l d -> l (o d)"), out_sb[:]).then_inc(out_stored, 16)

            def pre():
                sp.sem_inc(out_stored, 16)
                load_x(0)
                load_ctx(0)
                load_piece(0)
                load_piece(1)
                for dst, name in ((nq_row, "norm_q_w"), (w_txt, "norm_k_w"), (w_img, "norm_k_img_w"),
                                  (k_bias, "k_b"), (ki_bias, "k_img_b")):
                    sp.dma_start(dst[:], t[name].partition_broadcast(P)).then_inc(rows_loaded, 16)
                sp.dma_start(out_bias[:], t["o_b"].partition_broadcast(L)).then_inc(rows_loaded, 16)
                sp.dma_start(wr[:], t["w_router"].partition_broadcast(L)).then_inc(rows_loaded, 16)
                sp.wait_ge(rows_ready, 1)
                sp.dma_start(q_bias[:], t["q_b"].partition_broadcast(P)).then_inc(rows_loaded, 16)
                for j in range(2, PIECES):
                    sp.wait_ge(piece_hi, j - 1)
                    sp.wait_ge(piece_lo, j - 1)
                    load_piece(j)
                sp.wait_ge(xT_full, 1)
                load_x(1)
                sp.wait_ge(ctx_hi_done, 1)
                sp.wait_ge(ctx_lo_done, 1)
                load_ctx(1)
                sp.wait_ge(pro_done, 2)
                sp.dma_start(vtail_dram, v_tail.rearrange("b h w -> b (h w)")).then_inc(vtail_stored, 16)
                sp.wait_ge(vtail_stored, 16)
                sp.wait_ge(consts_ready, 3)
                load_tail(0)

            def body(i, n, m, p):
                if p is not None:
                    sp.wait_ge(b1_done, slot1_own(p, 2))
                sp.dma_start(x_res[:], t["x"][bass.ds(i, 1)].rearrange("o t d -> t (o d)")).then_inc(xres_loaded, 16)
                if m is not None:
                    sp.wait_ge(xT_full, m)
                    load_x(m)
                    sp.wait_ge(ctx_hi_done, m)
                    sp.wait_ge(ctx_lo_done, m)
                    load_ctx(m)
                if p is not None:
                    store(p)
                if n is not None:
                    sp.wait_ge(pv_full, 4 * n)
                    load_tail(n)

            over_batches(sp, pre, body)
            store(B - 1)
            sp.wait_ge(xh_stored, 16 * B)
            sp.wait_ge(score_stored, 16 * B)
            sp.wait_ge(out_stored, 16 * B + 16)

            sp.dma_start(score_row[:], score_dram.partition_broadcast(L)).then_inc(score_row_loaded, 16)
            for dst, name in ((earlier, "earlier"), (later, "later"), (slot_far, "slot_far"), (token_no, "token_no"),
                              (cos_tab, "cos_tab"), (sin_tab, "sin_tab"), (token_base, "token_base")):
                sp.dma_start(dst[:], t[name]).then_inc(topk_loaded, 16)
            sp.dma_start(fvec[:], t["fvec"]).then_inc(fvec_loaded, 16)
            sp.dma_start(bv_row[:], t["bv"].partition_broadcast(L)).then_inc(fvec_loaded, 16)
            sp.dma_start(wq, t["wq"].rearrange("(c p) n -> p c n", p=P)).then_inc(ring_loaded[0], 16)
            sp.dma_start(wk, t["wk"].rearrange("(c p) n -> p c n", p=P)).then_inc(ring_loaded[1], 16)
            sp.dma_start(wv, t["wv"].rearrange("(c p) n -> p c n", p=P)).then_inc(ring_loaded[1], 16)
            sp.dma_start(wo, t["wo"].rearrange("(c p) n -> p c n", p=P)).then_inc(ring_loaded[2], 16)
            sp.wait_ge(head_full, FH)
            sp.dma_start(w_gate, t["w_gate"].rearrange("(c p) n -> p c n", p=P)).then_inc(ring_loaded[0], 16)
            sp.wait_ge(val_full, 2 * NC)
            sp.dma_start(w_up, t["w_up"].rearrange("(c p) n -> p c n", p=P)).then_inc(ring_loaded[1], 16)
            sp.wait_ge(mid_full, NC)
            sp.dma_start(w_down, t["w_down"].rearrange("(c p) n -> p c n", p=P)).then_inc(ring_loaded[2], 16)

        @block.gpsimd
        def _(pool):
            def split_ctx(n):
                pool.wait_ge(ctx_hi_done, n + 1)
                nc.gpsimd.tensor_tensor(ctx_lo[:], ctx_raw[:], ctx_hi[:].bitcast(F32), ALU.subtract).then_inc(ctx_lo_done, 1)

            def normalise_x(m):
                pool.wait_ge(ln1_step, 3 * m + 3)
                pool.sem_inc(passed, 1)
                nc.gpsimd.tensor_scalar(xn[:], x_in[:], ln1_mv[:, 0:1], ln1_rstd[:], ALU.subtract, ALU.mult).then_inc(xn_ready, 1)

            def diagonals(i, g):
                pool.wait_ge(s_done, 8 * i + 2 * g + 2)
                nc.gpsimd.tensor_tensor(shift[:, g].rearrange("l s h q -> l (s h) q"),
                                        neg_ident[:].unsqueeze(1).to_broadcast([L, 2 * GH, L]),
                                        top[:, g].rearrange("l s h -> l (s h)").unsqueeze(2).to_broadcast([L, 2 * GH, L]),
                                        ALU.mult).then_inc(shift_ready, 1)

            def output(p):
                pool.wait_ge(score_ready, p + 1)
                nc.gpsimd.tensor_tensor(out_sb[:], xh[:, 0], xh[:, 1], ALU.add).then_inc(out_ready, 1)

            def pre():
                nc.gpsimd.memset(ident[:], 0.0)
                nc.gpsimd.memset(neg_ident[:], 0.0)
                nc.gpsimd.memset(ones_c_txt[:], 1.0)
                nc.gpsimd.memset(ones_c_tail[:], 0.0).then_inc(consts_zeroed, 1)
                pool.wait_ge(consts_zeroed, 1)
                nc.gpsimd.affine_select(out=ident[:], in_=ident[:], compare_op=ALU.not_equal, fill=1.0, base=0,
                                        pattern=[[-1, P]], channel_multiplier=1)
                nc.gpsimd.affine_select(out=neg_ident[:], in_=neg_ident[:], compare_op=ALU.not_equal, fill=-1.0, base=0,
                                        pattern=[[-1, L]], channel_multiplier=1)
                nc.gpsimd.memset(ones_c_txt[:, TAIL:TAIL + 1], 0.0)
                nc.gpsimd.memset(ones_c_tail[:, TAIL:TAIL + 1], 1.0)
                nc.gpsimd.memset(ones_img[:], 1.0)
                nc.gpsimd.memset(sq_sum[:], 1.0)
                nc.gpsimd.memset(ln_eps[:], LN_EPS)
                nc.gpsimd.memset(rms_eps[:], RMS_EPS).then_inc(consts_ready, 1)
                normalise_x(0)
                split_ctx(0)
                nc.gpsimd.memset(k_hi[:, :, NKEY - 1:NKEY].bitcast(F32), 0.0)
                nc.gpsimd.memset(k_lo[:, :, NKEY - 1:NKEY].bitcast(F32), 0.0)
                nc.gpsimd.memset(q_hi[:].bitcast(F32), 0.0)
                nc.gpsimd.memset(q_lo[:].bitcast(F32), 0.0).then_inc(consts_ready, 1)
                nc.gpsimd.memset(v_c[:], 0.0)
                nc.gpsimd.memset(v_tail[:, :, HD:VW], 1.0)
                nc.gpsimd.memset(v_a[:, :, HD:VW], 1.0)
                nc.gpsimd.memset(v_b[:, :, HD:VW], 1.0).then_inc(consts_zeroed, 1)
                pool.wait_ge(consts_zeroed, 2)
                nc.gpsimd.memset(v_c[0:TXT, :, VW + HD:2 * VW], 1.0).then_inc(consts_ready, 1)
                normalise_x(1)

            def body(i, n, m, p):
                for g in range(NG):
                    diagonals(i, g)
                if n is not None:
                    split_ctx(n)
                pool.wait_ge(xres_loaded, 16 * i + 16)
                if p is None:
                    pool.wait_ge(rows_ready, 2)
                nc.gpsimd.tensor_tensor(x_res[:], x_res[:], out_bias[:], ALU.add).then_inc(xres_ready, 1)
                if m is not None:
                    normalise_x(m)
                if p is not None:
                    output(p)

            over_batches(pool, pre, body)
            output(B - 1)

            pool.wait_ge(tok_ready, 1)
            for c in range(NC):
                nc.gpsimd.indirect_dma_start(xh_sel[:, c].rearrange("l a d -> l (a d)"), None, xh_dram,
                                             bass.IndirectOffsetOnAxis(ap=tok[:, c:c + 1], axis=0)).then_inc(gathered[c], 16)
            pool.wait_ge(rope_ready, 2)
            nc.gpsimd.memset(causal[:], 0.0)
            nc.gpsimd.memset(ident_bf[:], 0.0).then_inc(consts2, 1)
            pool.wait_ge(consts2, 1)
            nc.gpsimd.affine_select(out=causal[:], in_=causal[:], compare_op=ALU.is_ge, fill=MASKED, base=0,
                                    pattern=[[-1, L]], channel_multiplier=1)
            nc.gpsimd.affine_select(out=ident_bf[:], in_=ident_bf[:], compare_op=ALU.not_equal, fill=1.0, base=0,
                                    pattern=[[-1, L]], channel_multiplier=1).then_inc(consts2, 1)
            for c in range(NC):
                pool.wait_ge(final_ready, c + 1)
                nc.gpsimd.indirect_dma_start(out.rearrange("b l d -> (b l) d"), bass.IndirectOffsetOnAxis(ap=tok[:, c:c + 1], axis=0),
                                             keep[:, c], None).then_inc(scattered, 16)
            pool.wait_ge(scattered, 16 * NC)


        @block.scalar
        def _(act):
            def split_ctx(n):
                act.wait_ge(ctx_loaded, 16 * n + 16)
                nc.scalar.activation(ctx_hi[:], ctx_raw[:], ACT.Copy).then_inc(ctx_hi_done, 1)

            def x_hi(n):
                act.wait_ge(xT_full, n + 1)
                nc.scalar.activation(xT_hi[:], ps[:, 6, 0:KC * L].rearrange("p (c l) -> p c l", c=KC), ACT.Copy).then_inc(xT_hi_done, 1)

            def squares(n, k):
                rows = TOK_ROWS[k]
                done, slot = ((b1_done, slot1(n, k // 2)), (b0_done, 4 * n + k // 2))[k % 2]
                act.wait_ge(done, slot + 1)
                if not isinstance(n, int) or n or k:
                    act.wait_ge(sq_done, 4 * n + k)
                nc.scalar.activation(sq_junk[0:rows], proj[0:rows, k, :], ACT.Square, accum_out=sq_sum[0:rows, k:k + 1]).then_inc(sq_done, 1)

            def roots(n, m, p):
                if n is not None:
                    act.wait_ge(sq_done, 4 * n + 4)
                    nc.scalar.activation(rms[:, 0:4], sq_sum[:, 0:4], ACT.Sqrt, bias=rms_eps[:], scale=1.0 / D).then_inc(rms_done, 1)
                if m is not None:
                    act.wait_ge(ln1_step, 3 * m + 2)
                    nc.scalar.activation(ln1_sd[:], ln1_mv[:, 1:2], ACT.Sqrt, bias=ln_eps[0:L]).then_inc(ln1_sd_done, 1)
                if p is not None:
                    act.wait_ge(ln2_step, 3 * p + 3)
                    nc.scalar.activation(ln2_sd[:], ln2_mv[:, 1:2], ACT.Sqrt, bias=ln_eps[0:L]).then_inc(ln2_sd_done, 1)

            def kq_hi(n):
                act.wait_ge(turned, 4 * n + 1)
                for j in range(GH):
                    part = slice(HD * j, HD * (j + 1))
                    last = nc.scalar.activation(q_hi[part, :, j, :], ps[part, 2, 0:NG * L].rearrange("p (g l) -> p g l", g=NG), ACT.Copy)
                last.then_inc(q_hi_done, 1)
                for k in range(1, 4):
                    rows = TOK_ROWS[k]
                    act.wait_ge(turned, 4 * n + k + 1)
                    nc.scalar.activation(k_hi[:, :, KEY_AT[k]:KEY_AT[k] + rows],
                                         ps[:, 2 + k, 0:KC * rows].rearrange("p (c l) -> p c l", c=KC), ACT.Copy).then_inc(k_hi_done, 1)

            def exps(i, g):
                for c, (_, rows) in enumerate(CHUNKS):
                    k = 3 * g + c
                    act.wait_ge(st_full, 12 * i + k + 1)
                    if c == 0 and g >= 2:
                        act.wait_ge(pv_full, 4 * i + g - 1)
                    nc.scalar.activation(prob[0:rows, g % 2, c, :], ps[0:rows, 2 + k % 4, 0:GH * L], ACT.Exp).then_inc(exp_done, 1)

            def pre():
                act.wait_ge(consts_ready, 1)
                act.wait_ge(ln1_step, 2)
                nc.scalar.activation(ln1_sd[:], ln1_mv[:, 1:2], ACT.Sqrt, bias=ln_eps[0:L]).then_inc(ln1_sd_done, 1)
                split_ctx(0)

                def piece(j):
                    act.wait_ge(piece_loaded[j % 2], 16 * (j // 2) + 16)
                    nc.scalar.activation(w_hi[W[j // 2]][:, 2 * (j % 2):2 * (j % 2) + 2, :],
                                         stage[:, j % 2, :].rearrange("p (c o) -> p c o", c=2), ACT.Copy).then_inc(piece_hi, 1)

                for j in range(0, 2):
                    piece(j)
                x_hi(0)
                for j in range(2, PIECES):
                    piece(j)
                for k in range(4):
                    squares(0, k)
                act.wait_ge(pro_done, 1)
                act.wait_ge(sq_done, 4)
                nc.scalar.activation(sq_junk[0:B], tail_proj, ACT.Square, accum_out=sq_sum[0:B, 4:5]).then_inc(tail_step, 1)
                act.wait_ge(tail_step, 1)
                nc.scalar.activation(rms[:, 4:5], sq_sum[:, 4:5], ACT.Sqrt, bias=rms_eps[:], scale=1.0 / D)
                roots(0, 1, None)
                act.wait_ge(consts_ready, 2)
                kq_hi(0)
                act.wait_ge(tail_turned, 1)
                nc.scalar.activation(k_tail_hi[:], ps[:, 7, 0:KC * B].rearrange("p (c b) -> p c b", c=KC), ACT.Copy).then_inc(tail_hi_done, 1)

            def body(i, n, m, p):
                if n is not None:
                    x_hi(n)
                act.wait_ge(b0_full, 4 * i + 3)
                nc.scalar.activation(v_a[:, :, 0:HD], bank0.rearrange("p (h d) -> p h d", h=NH), ACT.Copy).then_inc(b0_done, 1)
                act.wait_ge(b0_full, 4 * i + 4)
                nc.scalar.activation(v_c[0:TXT, :, VW:VW + HD], bank0[0:TXT].rearrange("p (h d) -> p h d", h=NH), ACT.Copy).then_inc(b0_done, 1)
                if n is not None:
                    split_ctx(n)
                exps(i, 0)
                exps(i, 1)
                if n is not None:
                    squares(n, 0)
                    squares(n, 1)
                exps(i, 2)
                if n is not None:
                    squares(n, 2)
                    squares(n, 3)
                roots(n, m, p)
                exps(i, 3)
                if n is not None:
                    kq_hi(n)
                act.wait_ge(b1_full, slot1_own(i, 1))
                nc.scalar.activation(oT_hi[:], bank1[:, 0:KC * L].rearrange("p (c l) -> p c l", c=KC), ACT.Copy).then_inc(oT_hi_done, 1)

            over_batches(act, pre, body)
            roots(None, None, B - 1)

            def token_roots(k):
                act.wait_ge(sums_ready, k + 1)
                nc.scalar.activation(rstd[:], sums[:], ACT.Sqrt, bias=rms_eps[0:L], scale=1.0 / D).then_inc(root_ready, 1)

            def hT_scaled(k, at):
                act.wait_ge(fvec_loaded, 32)
                for kc in range(KC):
                    act.wait_ge(hT_full, KC * k + kc + 1)
                    nc.scalar.activation(hT[:, kc, :], ps[:, 4 + kc, 0:S], ACT.Copy, scale=fvec[:, at + kc:at + kc + 1]).then_inc(hT_ready, 1)

            for k, table in enumerate((cos, sin)):
                act.wait_ge(rope_full, k + 1)
                nc.scalar.activation(table[:], ps[:, 2 + k, 0:S], ACT.Copy).then_inc(rope_ready, 1)
            token_roots(0)
            hT_scaled(0, FH + FKV)
            for h in range(FH + FKV):
                act.wait_ge(head_full, h + 1)
                if h >= 2:
                    act.wait_ge(head_ready, h - 1)
                nc.scalar.activation(biased[:, h % 2, :], ps[:, h % 2, 0:S], ACT.Identity, bias=fvec[:, h:h + 1]).then_inc(head_biased, 1)
            act.wait_ge(gate_step, 1)
            nc.scalar.activation(gate_e[:], sel_score[:], ACT.Exp, scale=-1.0).then_inc(gate_exp, 1)

            def turn_evac(k):
                c = k % NC
                act.wait_ge(pT_full, k + 1)
                if c == 0 and k:
                    act.wait_ge(attn_full, k // NC)
                nc.scalar.activation(probT[:, 0:c + 1, c * L:(c + 1) * L],
                                     ps[0:L, 4 + k % 2, 0:(c + 1) * L].rearrange("t (b q) -> t b q", b=c + 1), ACT.Copy).then_inc(pT_ready, 1)

            for k in range(FH * NC + 2):
                if k < FH * NC:
                    c = k % NC
                    n_keys = (c + 1) * L
                    act.wait_ge(top_ready, k + 1)
                    if k >= 2:
                        act.wait_ge(pT_full, k - 1)
                    nc.scalar.activation(prob2[:, k % 2, 0:n_keys], ps[0:L, c, 0:n_keys], ACT.Exp, bias=neg_top[:, c:c + 1],
                                         accum_out=prob_sum[:, c:c + 1]).then_inc(prob_ready, 1)
                if k >= 2:
                    turn_evac(k - 2)
            token_roots(1)
            hT_scaled(1, FH + FKV + KC)
            for j in range(FC):
                act.wait_ge(mlp_full, j + 1)
                if j >= 2:
                    act.wait_ge(hid_ready, j - 1)
                nc.scalar.activation(silu_e[:, j % 2, :], ps[:, 2 * (j % 2), 0:S], ACT.Exp, scale=-1.0).then_inc(silu_exp, 1)

        @block.vector
        def _(dve):
            def ln1(m):
                dve.wait_ge(x_loaded, 16 * m + 16)
                nc.vector.bn_stats(ln1_stats[:], x_in[:]).then_inc(ln1_step, 1)
                dve.wait_ge(ln1_step, 3 * m + 1)
                dve.sem_inc(passed, 1)
                nc.vector.bn_aggr(ln1_mv[:], ln1_stats[:]).then_inc(ln1_step, 1)

            def ln1_finish(m):
                dve.wait_ge(ln1_sd_done, m + 1)
                nc.vector.reciprocal(ln1_rstd[:], ln1_sd[:]).then_inc(ln1_step, 1)

            def x_rest(n):
                dve.wait_ge(xT_hi_done, n + 1)
                nc.vector.tensor_tensor(xT_lo[:], ps[:, 6, 0:KC * L].rearrange("p (c l) -> p c l", c=KC),
                                        xT_hi[:].bitcast(F32), ALU.subtract).then_inc(xT_lo_done, 1)

            def add_bias(n, k):
                rows, bias = TOK_ROWS[k], (q_bias, k_bias, ki_bias, ki_bias)[k]
                full, done, bank, slot = ((b1_full, b1_done, bank1, slot1(n, k // 2)), (b0_full, b0_done, bank0, 4 * n + k // 2))[k % 2]
                dve.wait_ge(full, slot + 1)
                nc.vector.tensor_tensor(proj[0:rows, k, :], bank[0:rows], bias[0:rows], ALU.add).then_inc(done, 1)

            def rms_scale(n):
                dve.wait_ge(rms_done, n + 1)
                nc.vector.reciprocal(rstd1[:], rms[:]).then_inc(rms_inv, 1)
                dve.wait_ge(rms_inv, n + 1)
                nc.vector.tensor_scalar(proj[0:L, 0, :], proj[0:L, 0, :], rstd1[0:L, 0:1], None, ALU.mult).then_inc(scaled, 1)
                for k in range(1, 4):
                    rows = TOK_ROWS[k]
                    nc.vector.scalar_tensor_tensor(proj[0:rows, k, :], proj[0:rows, k, :], rstd1[0:rows, k:k + 1],
                                                   (w_txt if k == 1 else w_img)[0:rows], ALU.mult, ALU.mult).then_inc(scaled, 1)

            def q_rest(n):
                dve.wait_ge(q_hi_done, n + 1)
                for j in range(GH):
                    part = slice(HD * j, HD * (j + 1))
                    nc.vector.tensor_tensor(q_lo[part, :, j, :], ps[part, 2, 0:NG * L].rearrange("p (g l) -> p g l", g=NG),
                                            q_hi[part, :, j, :].bitcast(F32), ALU.subtract)

            def k_rest(n, k):
                rows = TOK_ROWS[k]
                cols = slice(KEY_AT[k], KEY_AT[k] + rows)
                dve.wait_ge(k_hi_done, 3 * n + k)
                return nc.vector.tensor_tensor(k_lo[:, :, cols], ps[:, 2 + k, 0:KC * rows].rearrange("p (c l) -> p c l", c=KC),
                                               k_hi[:, :, cols].bitcast(F32), ALU.subtract)

            def tail_keys(n):
                nc.vector.tensor_copy(k_hi[:, :, TAIL:TAIL + 1], k_tail_hi[:, :, bass.ds(n, 1)])
                nc.vector.tensor_copy(k_lo[:, :, TAIL:TAIL + 1], k_tail_lo[:, :, bass.ds(n, 1)]).then_inc(kq_lo_done, 1)

            def pair_max(i, p):
                dve.wait_ge(s_full, 8 * i + p + 1)
                bank = 2 + 2 * (p % 2)
                heads = slice(2 * (p % 2), 2 * (p % 2) + 2)
                nc.vector.tensor_reduce(top[:, p // 2, 0, heads], ps[0:L, bank:bank + 2, 0:TXT], AX.X, ALU.max)
                nc.vector.tensor_reduce(top[:, p // 2, 1, heads], ps[0:L, bank:bank + 2, TAIL:CTX], AX.X, ALU.max).then_inc(s_done, 1)

            def normalise(i, g):
                dve.wait_ge(pv_full, 4 * i + g + 1)
                pv = ps[0:L, 6 + g % 2, 0:GH * 2 * VW].rearrange("l (h s w) -> l h s w", h=GH, s=2)
                nc.vector.reciprocal(rec[:], pv[:, :, :, HD]).then_inc(norm_step, 1)
                dve.wait_ge(norm_step, 8 * i + 2 * g + 1)
                for s in range(2):
                    last = nc.vector.tensor_tensor(o_parts[:, s], pv[:, :, s, 0:HD],
                                                   rec[:, :, s:s + 1].to_broadcast([L, GH, HD]), ALU.mult)
                last.then_inc(norm_step, 1)
                dve.wait_ge(norm_step, 8 * i + 2 * g + 2)
                nc.vector.tensor_tensor(o[:, g * P:(g + 1) * P].rearrange("l (h d) -> l h d", h=GH),
                                        o_parts[:, 0], o_parts[:, 1], ALU.add).then_inc(pv_done, 1)

            def ln2(p):
                dve.wait_ge(b1_done, slot1_own(p, 2))
                nc.vector.bn_stats(ln2_stats[:], xh[:, 0]).then_inc(ln2_step, 1)
                dve.wait_ge(ln2_step, 3 * p + 1)
                dve.sem_inc(passed, 1)
                nc.vector.bn_aggr(ln2_mv[:], ln2_stats[:]).then_inc(ln2_step, 2)

            def ln2_finish(p):
                dve.wait_ge(ln2_sd_done, p + 1)
                nc.vector.reciprocal(ln2_rstd[:], ln2_sd[:]).then_inc(h_step, 1)
                dve.wait_ge(h_step, p + 1)
                nc.vector.tensor_scalar(xh[:, 1], xh[:, 0], ln2_mv[:, 0:1], ln2_rstd[:], ALU.subtract, ALU.mult).then_inc(h_ready, 1)
                dve.wait_ge(h_ready, p + 1)
                dve.wait_ge(out_stored, 16 * p + 16)
                nc.vector.scalar_tensor_tensor(score_junk[:], xh[:, 1], 1.0, wr[:], ALU.mult, ALU.mult,
                                               accum_out=score[:, bass.ds(p, 1)]).then_inc(score_ready, 1)

            def pre():
                ln1(0)
                ln1_finish(0)
                dve.wait_ge(vecs_loaded, 16)
                nc.vector.tensor_tensor(vbias_cols, vecs[:, 0, :].unsqueeze(2).to_broadcast([P, KC, L]),
                                        vecs[:, 1, :].unsqueeze(2).to_broadcast([P, KC, L]), ALU.add).then_inc(vecs_ready, 1)

                def piece(j):
                    dve.wait_ge(piece_hi, j + 1)
                    c2 = slice(2 * (j % 2), 2 * (j % 2) + 2)
                    nc.vector.tensor_tensor(w_lo[W[j // 2]][:, c2, :], stage[:, j % 2, :].rearrange("p (c o) -> p c o", c=2),
                                            w_hi[W[j // 2]][:, c2, :].bitcast(F32), ALU.subtract).then_inc(piece_lo, 1)

                for j in range(2):
                    piece(j)
                x_rest(0)
                dve.wait_ge(rows_loaded, 16 * 7)
                nc.vector.scalar_tensor_tensor(w_txt[:], nq_row[:], SCALE, w_txt[:], ALU.mult, ALU.mult)
                nc.vector.scalar_tensor_tensor(w_img[:], nq_row[:], SCALE, w_img[:], ALU.mult, ALU.mult).then_inc(rows_ready, 1)
                for j in range(2, 6):
                    piece(j)
                dve.wait_ge(rows_loaded, 16 * 8)
                add_bias(0, 1)
                add_bias(0, 0)
                for j in range(6, PIECES):
                    piece(j)
                add_bias(0, 2)
                add_bias(0, 3)
                ln1(1)
                dve.wait_ge(pro_full, 1)
                nc.vector.tensor_tensor(tail_proj, ps[0:B, 7, :], ki_bias[0:B], ALU.add).then_inc(pro_done, 1)
                dve.wait_ge(pro_full, 2)
                dve.wait_ge(consts_ready, 3)
                nc.vector.tensor_copy(v_tail[:, :, 0:HD], ps[0:B, 6, :].rearrange("b (h d) -> b h d", h=NH)).then_inc(pro_done, 1)
                dve.wait_ge(rows_ready, 1)
                rms_scale(0)
                nc.vector.scalar_tensor_tensor(tail_proj, tail_proj, rstd1[0:B, 4:5], w_img[0:B], ALU.mult, ALU.mult).then_inc(tail_scaled, 1)
                ln1_finish(1)
                dve.wait_ge(pro_full, 3)
                nc.vector.tensor_tensor(out_bias[:], ps[0:L, 7, :], out_bias[:], ALU.add).then_inc(rows_ready, 1)
                q_rest(0)
                for k in range(1, 4):
                    k_rest(0, k)
                dve.wait_ge(tail_hi_done, 1)
                nc.vector.tensor_tensor(k_tail_lo[:], ps[:, 7, 0:KC * B].rearrange("p (c b) -> p c b", c=KC),
                                        k_tail_hi[:].bitcast(F32), ALU.subtract).then_inc(tail_ready, 1)
                dve.wait_ge(tail_ready, 1)
                tail_keys(0)

            def body(i, n, m, p):
                pair_max(i, 0)
                if n is not None:
                    x_rest(n)
                pair_max(i, 1)
                pair_max(i, 2)
                if p is not None:
                    ln2(p)
                for k in range(3, 6):
                    pair_max(i, k)
                dve.wait_ge(b1_full, 5 * i + 3)
                nc.vector.tensor_copy(v_b[:, :, 0:HD], bank1.rearrange("p (h d) -> p h d", h=NH)).then_inc(b1_done, 1)
                pair_max(i, 6)
                pair_max(i, 7)
                if m is not None:
                    ln1(m)
                if n is not None:
                    add_bias(n, 0)
                normalise(i, 0)
                if n is not None:
                    for k in range(1, 4):
                        add_bias(n, k)
                normalise(i, 1)
                if m is not None:
                    ln1_finish(m)
                if n is not None:
                    rms_scale(n)
                if p is not None:
                    ln2_finish(p)
                normalise(i, 2)
                if n is not None:
                    q_rest(n)
                normalise(i, 3)
                if n is not None:
                    for k in range(1, 4):
                        k_rest(n, k)
                    tail_keys(n)
                dve.wait_ge(oT_hi_done, i + 1)
                nc.vector.tensor_tensor(oT_lo[:], bank1[:, 0:KC * L].rearrange("p (c l) -> p c l", c=KC),
                                        oT_hi[:].bitcast(F32), ALU.subtract).then_inc(b1_done, 1)
                dve.wait_ge(b1_full, slot1_own(i, 2))
                dve.wait_ge(xres_ready, i + 1)
                if p is not None:
                    dve.wait_ge(xh_stored, 16 * i)
                    dve.wait_ge(out_ready, i)
                nc.vector.tensor_tensor(xh[:, 0], bank1[0:L], x_res[:], ALU.add).then_inc(b1_done, 1)

            over_batches(dve, pre, body)
            ln2(B - 1)
            ln2_finish(B - 1)

            dve.wait_ge(score_row_loaded, 16)
            dve.wait_ge(topk_loaded, 16 * 7)
            own = score[:].unsqueeze(2).to_broadcast([L, B, L])
            nc.vector.tensor_tensor(equal[:], score_row[:], own, ALU.is_equal).then_inc(rank_step, 1)
            nc.vector.tensor_tensor(above[:], score_row[:], own, ALU.is_gt).then_inc(rank_step, 1)
            dve.wait_ge(rank_step, 1)
            nc.vector.tensor_tensor(equal[:], equal[:], earlier[:].unsqueeze(1).to_broadcast([L, B, L]), ALU.mult).then_inc(rank_step, 1)
            dve.wait_ge(rank_step, 3)
            nc.vector.tensor_tensor(above[:], above[:], equal[:], ALU.add).then_inc(rank_step, 1)
            dve.wait_ge(rank_step, 4)
            nc.vector.tensor_reduce(rank[:], above[:], AX.X, ALU.add).then_inc(rank_step, 1)
            dve.wait_ge(rank_step, 5)
            nc.vector.tensor_scalar(chosen[:], rank[:], TOPK - 0.5, None, ALU.is_lt).then_inc(chosen_ready, 1)
            dve.wait_ge(before_full, 1)
            nc.vector.scalar_tensor_tensor(before[:], chosen[:], -FAR, ps[0:L, 0, 0:B], ALU.mult, ALU.add).then_inc(rank_step, 1)
            dve.wait_ge(rank_step, 6)
            nc.vector.tensor_tensor(slot_hot[:], before[:].unsqueeze(2).to_broadcast([L, B, TOPK]),
                                    slot_far[:].unsqueeze(1).to_broadcast([L, B, TOPK]), ALU.is_equal).then_inc(hot_ready, 1)
            dve.wait_ge(tok_full, 1)
            nc.vector.tensor_tensor(tok[:], ps[0:L, 1, 0:NC], token_base[:], ALU.add).then_inc(tok_ready, 1)

            def normalise_tokens(k, src):
                dve.wait_ge(root_ready, k + 1)
                nc.vector.reciprocal(rstd[:], rstd[:]).then_inc(rstd_ready, 1)
                dve.wait_ge(rstd_ready, k + 1)
                for c in range(NC):
                    nc.vector.tensor_scalar(normed[:, c], src(c), rstd[:, c:c + 1], None, ALU.mult).then_inc(normed_ready, 1)

            for c in range(NC):
                dve.wait_ge(gathered[c], 16)
                last = nc.vector.scalar_tensor_tensor(normed[:, c], xh_sel[:, c, 1], 1.0, xh_sel[:, c, 1], ALU.mult, ALU.mult,
                                                      accum_out=sums[:, c:c + 1])
            last.then_inc(sums_ready, 1)
            dve.wait_ge(sums_ready, 1)
            for c in range(NC):
                last = nc.vector.scalar_tensor_tensor(normed[:, c], xh_sel[:, c, 1], 1.0, wr[:], ALU.mult, ALU.mult,
                                                      accum_out=sel_score[:, c:c + 1])
            last.then_inc(gate_step, 1)
            dve.wait_ge(gate_step, 1)
            normalise_tokens(0, lambda c: xh_sel[:, c, 1])
            dve.wait_ge(rope_ready, 2)
            for h in range(FH + FKV):
                dve.wait_ge(head_biased, h + 1)
                b = biased[:, h % 2, :]
                dst = qT[:, h, :] if h < FH else kT[:, h - FH, :]
                if h >= 2:
                    dve.wait_ge(head_ready, h - 1)
                r = rot[:, h % 2, :]
                scale = 1.0 if h < FH else FSCALE
                nc.vector.scalar_tensor_tensor(r[0:HALF], b[HALF:P], scale, sin[HALF:P], ALU.mult, ALU.mult)
                nc.vector.scalar_tensor_tensor(r[HALF:P], b[0:HALF], scale, sin[0:HALF], ALU.mult, ALU.mult)
                nc.vector.scalar_tensor_tensor(dst, b, scale, cos[:], ALU.mult, ALU.mult).then_inc(rot_step, 1)
                dve.wait_ge(rot_step, h + 1)
                nc.vector.tensor_tensor(dst, dst, r, ALU.add).then_inc(head_ready, 1)
            dve.wait_ge(fvec_loaded, 32)
            for k in range(2 * NC):
                dve.wait_ge(val_full, k + 1)
                half = slice(512 * (k % 2), 512 * (k % 2) + 512)
                nc.vector.tensor_tensor(vals[:, k // 2, half], ps[0:L, 2 + k % 2, :], bv_row[:, half], ALU.add).then_inc(val_ready, 1)
            dve.wait_ge(gate_exp, 1)
            nc.vector.tensor_scalar(gate_e[:], gate_e[:], 1.0, None, ALU.add).then_inc(gate_step, 1)
            dve.wait_ge(gate_step, 2)
            nc.vector.reciprocal(gate[:], gate_e[:]).then_inc(gate_step, 1)
            dve.wait_ge(gate_step, 3)
            nc.vector.tensor_scalar(gate_e[:], gate[:], -1.0, 1.0, ALU.mult, ALU.add).then_inc(gate_step, 1)
            dve.wait_ge(gate_step, 4)
            for c in range(NC):
                last = nc.vector.scalar_tensor_tensor(keep[:, c], xh_sel[:, c, 1], gate_e[:, c:c + 1], xh_sel[:, c, 0], ALU.mult, ALU.add)
            last.then_inc(gate_step, 1)

            def scale_probs(k):
                c = k % NC
                dve.wait_ge(prob_ready, k + 1)
                nc.vector.reciprocal(prob_sum[:, c:c + 1], prob_sum[:, c:c + 1]).then_inc(inv_ready, 1)
                dve.wait_ge(inv_ready, k + 1)
                part = prob2[:, k % 2, 0:(c + 1) * L]
                nc.vector.tensor_scalar(part, part, prob_sum[:, c:c + 1], None, ALU.mult).then_inc(prob_scaled, 1)

            for k in range(FH * NC + 3):
                c = k % NC
                if k < FH * NC:
                    dve.wait_ge(att_full, k + 1)
                    nc.vector.tensor_reduce(neg_top[:, c:c + 1], ps[0:L, c, 0:(c + 1) * L], AX.X, ALU.max, negate=True).then_inc(top_ready, 1)
                if 1 <= k <= FH * NC:
                    scale_probs(k - 1)
                if c == 2 and k >= NC:
                    h = k // NC - 1
                    dve.wait_ge(attn_full, h + 1)
                    nc.vector.tensor_copy(attnT[:, h, :], ps[:, 6 + h % 2, 0:S]).then_inc(attn_ready, 1)
            for c in range(NC):
                dve.wait_ge(mid_full, c + 1)
                nc.vector.tensor_tensor(x_mid[:, c], ps[0:L, c, :], xh_sel[:, c, 1], ALU.add).then_inc(mid_ready, 1)
            for c in range(NC):
                dve.wait_ge(mid_ready, c + 1)
                last = nc.vector.scalar_tensor_tensor(normed[:, c], x_mid[:, c], 1.0, x_mid[:, c], ALU.mult, ALU.mult,
                                                      accum_out=sums[:, c:c + 1])
            last.then_inc(sums_ready, 1)
            dve.wait_ge(sums_ready, 2)
            normalise_tokens(1, lambda c: x_mid[:, c])
            for j in range(FC):
                e = silu_e[:, j % 2, :]
                g, u = (ps[:, 2 * (j % 2) + a, 0:S] for a in range(2))
                dve.wait_ge(silu_exp, j + 1)
                nc.vector.tensor_scalar(e, e, 1.0, None, ALU.add).then_inc(silu_step, 1)
                dve.wait_ge(silu_step, 3 * j + 1)
                nc.vector.reciprocal(e, e).then_inc(silu_step, 1)
                dve.wait_ge(silu_step, 3 * j + 2)
                nc.vector.tensor_tensor(silu_g[:, j % 2, :], g, e, ALU.mult).then_inc(silu_step, 1)
                dve.wait_ge(silu_step, 3 * j + 3)
                nc.vector.tensor_tensor(mT[:, j, :], u, silu_g[:, j % 2, :], ALU.mult).then_inc(hid_ready, 1)
            dve.wait_ge(gate_step, 5)
            for c in range(NC):
                dve.wait_ge(down_full, c + 1)
                nc.vector.tensor_tensor(x_mid[:, c], ps[0:L, 4 + c, :], x_mid[:, c], ALU.add).then_inc(sum_ready, 1)
                dve.wait_ge(sum_ready, c + 1)
                nc.vector.scalar_tensor_tensor(keep[:, c], x_mid[:, c], gate[:, c:c + 1], keep[:, c], ALU.mult, ALU.add).then_inc(final_ready, 1)

        @block.tensor
        def _(pe):
            def mm3(o_, a_hi, a_lo, b_hi, b_lo, start, stop):
                nc.tensor.matmul(o_, a_hi, b_hi, start=start, stop=False)
                nc.tensor.matmul(o_, a_hi, b_lo, start=False, stop=False)
                return nc.tensor.matmul(o_, a_lo, b_hi, start=False, stop=stop)

            def project(o_, a_hi, a_lo, cols, w, chunks=range(KC)):
                for kc in chunks:
                    last = mm3(o_, a_hi[:, kc, cols], a_lo[:, kc, cols], w_hi[w][:, kc, :], w_lo[w][:, kc, :], kc == 0, kc == KC - 1)
                return last

            def transpose_x(n):
                pe.wait_ge(xn_ready, n + 1)
                for c in range(KC):
                    last = nc.tensor.transpose(ps[:, 6, c * L:(c + 1) * L], xn[:, c * P:(c + 1) * P], ident[0:L, 0:L])
                last.then_inc(xT_full, 1)

            def queries(n):
                pe.wait_ge(xT_lo_done, n + 1)
                if not isinstance(n, int) or n:
                    pe.wait_ge(b1_done, slot1(n, 0))
                project(bank1[0:L], xT_hi, xT_lo, slice(0, L), "q").then_inc(b1_full, 1)

            def keys(n, k):
                cols, w, rows = ((slice(0, TXT), "k", TXT), (slice(TXT, TXT + P), "k_img", P), (slice(TXT + P, CTXC), "k_img", P))[k]
                if k == 0:
                    pe.wait_ge(ctx_lo_done, n + 1)
                if not isinstance(n, int) or n or k:
                    if k % 2:
                        pe.wait_ge(b1_done, slot1(n, 1))
                    else:
                        pe.wait_ge(b0_done, 4 * n + k // 2)
                project((bank0, bank1)[k % 2][0:rows], ctx_hi, ctx_lo, cols, w).then_inc((b0_full, b1_full)[k % 2], 1)

            def turn(n, k):
                rows = TOK_ROWS[k]
                pe.wait_ge(scaled, 4 * n + k + 1)
                for c in range(KC):
                    last = nc.tensor.transpose(ps[:, 2 + k, c * rows:(c + 1) * rows], proj[0:rows, k, c * P:(c + 1) * P], ident[0:rows, 0:rows])
                last.then_inc(turned, 1)

            def values(i, k, part):
                cols, w, rows = ((slice(TXT, TXT + P), "v_img", P), (slice(TXT + P, CTXC), "v_img", P), (slice(0, TXT), "v", TXT))[k]
                if part == 0:
                    if k == 1:
                        pe.wait_ge(b1_done, 5 * i + 2)
                    else:
                        pe.wait_ge(b0_done, 4 * i + 2 + k // 2)
                last = project((bank0, bank1)[k % 2][0:rows], ctx_hi, ctx_lo, cols, w, range(2 * part, 2 * part + 2))
                if part == 1:
                    last.then_inc((b0_full, b1_full)[k % 2], 1)

            def scores(i, p):
                if p == 0:
                    pe.wait_ge(kq_lo_done, i + 1)
                if p >= 2:
                    pe.wait_ge(s_done, 8 * i + p - 1)
                for e in range(2):
                    g, j = p // 2, 2 * (p % 2) + e
                    last = nc.tensor.matmul(ps[0:L, 2 + 2 * (p % 2) + e, 0:NKEY], q_hi[:, g, j, :], k_hi[:, g, :], start=True, stop=True)
                last.then_inc(s_full, 1)

            def scores_T(i, g):
                pe.wait_ge(shift_ready, 4 * i + g + 1)
                for c, (at, rows) in enumerate(CHUNKS):
                    k = 3 * g + c
                    if k == 0:
                        pe.wait_ge(s_done, 8 * i + 7)
                    if k == 2:
                        pe.wait_ge(s_done, 8 * i + 8)
                    if k >= 4:
                        pe.wait_ge(exp_done, 12 * i + k - 3)
                    o_ = ps[0:rows, 2 + k % 4, 0:GH * L]
                    cols = slice(at, at + rows)
                    q = [x[:, g].rearrange("p h q -> p (h q)") for x in (q_hi, q_lo)]
                    sh = [shift[:, g, s].rearrange("l h q -> l (h q)") for s in range(2)]
                    mm3(o_, k_hi[:, g, cols], k_lo[:, g, cols], q[0], q[1], True, False)
                    if c == 0:
                        nc.tensor.matmul(o_, ones_c_txt[:], sh[0], start=False, stop=False)
                        last = nc.tensor.matmul(o_, ones_c_tail[:], sh[1], start=False, stop=True)
                    else:
                        last = nc.tensor.matmul(o_, ones_img[:], sh[1], start=False, stop=True)
                    last.then_inc(st_full, 1)

            def weighted_values(i, g, n):
                pe.wait_ge(exp_done, 12 * i + 3 * g + 3)
                if g == 0:
                    pe.wait_ge(vtail_loaded, 16 * i + 16)
                    pe.wait_ge(b0_done, 4 * i + 4)
                    pe.wait_ge(b1_done, 5 * i + 3)
                    if n is not None:
                        pe.wait_ge(xT_lo_done, n + 1)
                if g >= 2:
                    pe.wait_ge(pv_done, 4 * i + g - 1)
                for j in range(GH):
                    h, at = GH * g + j, 2 * VW * j
                    qs = slice(L * j, L * (j + 1))
                    bank = ps[0:L, 6 + g % 2, :]
                    nc.tensor.matmul(bank[:, at:at + 2 * VW], prob[0:CHUNK_C, g % 2, 0, qs], v_c[:, h, :], start=True, stop=False)
                    nc.tensor.matmul(bank[:, at:at + VW], prob[:, g % 2, 1, qs], v_a[:, h, :], start=False, stop=False)
                    last = nc.tensor.matmul(bank[:, at:at + VW], prob[:, g % 2, 2, qs], v_b[:, h, :], start=False, stop=True)
                last.then_inc(pv_full, 1)

            def pre():
                pe.wait_ge(consts_ready, 1)
                transpose_x(0)
                pe.wait_ge(piece_lo, 2)
                keys(0, 0)
                pe.wait_ge(piece_lo, 4)
                queries(0)
                pe.wait_ge(piece_lo, 6)
                keys(0, 1)
                keys(0, 2)
                pe.wait_ge(tails_loaded, 16)
                for bank, w, pieces in ((7, "k_img", 6), (6, "v_img", 8)):
                    pe.wait_ge(piece_lo, pieces)
                    for kc in range(KC):
                        for part in (w_hi, w_lo):
                            last = nc.tensor.matmul(ps[0:B, bank, :], ctx_tail[:, kc, :], part[w][:, kc, :].bitcast(F32),
                                                    start=kc == 0 and part is w_hi, stop=kc == KC - 1 and part is w_lo)
                    last.then_inc(pro_full, 1)
                pe.wait_ge(piece_lo, PIECES)
                pe.wait_ge(vecs_ready, 1)
                pe.wait_ge(pro_done, 1)
                for kc in range(KC):
                    for part in (w_hi, w_lo):
                        last = nc.tensor.matmul(ps[0:L, 7, :], vbias_cols[:, kc, :], part["o"][:, kc, :].bitcast(F32),
                                                start=kc == 0 and part is w_hi, stop=kc == KC - 1 and part is w_lo)
                last.then_inc(pro_full, 1)
                for k in range(4):
                    turn(0, k)
                pe.wait_ge(tail_scaled, 1)
                pe.wait_ge(rows_ready, 2)
                for c in range(KC):
                    last = nc.tensor.transpose(ps[:, 7, c * B:(c + 1) * B], tail_proj[:, c * P:(c + 1) * P], ident[0:B, 0:B])
                last.then_inc(tail_turned, 1)
                values(0, 0, 0)

            def body(i, n, m, p):
                if n is not None:
                    if p is None:
                        pe.wait_ge(pro_done, 2)
                    else:
                        pe.wait_ge(pv_done, 4 * i)
                    transpose_x(n)
                scores(i, 0)
                scores(i, 1)
                values(i, 0, 1)
                for k in (1, 2):
                    for part in range(2):
                        scores(i, 2 * k + part)
                        values(i, k, part)
                scores(i, 6)
                scores(i, 7)
                scores_T(i, 0)
                scores_T(i, 1)
                if n is not None:
                    queries(n)
                weighted_values(i, 0, n)
                if n is not None:
                    keys(n, 0)
                scores_T(i, 2)
                if n is not None:
                    keys(n, 1)
                    keys(n, 2)
                weighted_values(i, 1, n)
                scores_T(i, 3)
                weighted_values(i, 2, n)
                if n is not None:
                    pe.wait_ge(exp_done, 12 * i + 10)
                    turn(n, 0)
                    turn(n, 1)
                weighted_values(i, 3, n)
                if n is not None:
                    turn(n, 2)
                    turn(n, 3)
                pe.wait_ge(pv_done, 4 * i + 4)
                pe.wait_ge(b1_done, slot1_own(i, 0))
                for c in range(KC):
                    last = nc.tensor.transpose(bank1[:, c * L:(c + 1) * L], o[:, c * P:(c + 1) * P], ident[0:L, 0:L])
                last.then_inc(b1_full, 1)
                if n is not None:
                    values(n, 0, 0)
                pe.wait_ge(b1_done, slot1_own(i, 1))
                project(bank1[0:L], oT_hi, oT_lo, slice(0, L), "o").then_inc(b1_full, 1)

            over_batches(pe, pre, body)

            pe.wait_ge(chosen_ready, 1)
            nc.tensor.matmul(ps[0:L, 0, 0:B], later[:], chosen[:], start=True, stop=True).then_inc(before_full, 1)
            pe.wait_ge(hot_ready, 1)
            hot = slot_hot[:].rearrange("l b k -> l (b k)")
            for c in range(NC):
                last = nc.tensor.matmul(ps[0:L, 1, c:c + 1], hot[:, c * L:(c + 1) * L], token_no[:], start=True, stop=True)
            last.then_inc(tok_full, 1)
            for k, table in enumerate((cos_tab, sin_tab)):
                nc.tensor.matmul(ps[:, 2 + k, 0:S], table[:], hot, start=True, stop=True).then_inc(rope_full, 1)

            def turn_tokens(k):
                pe.wait_ge(normed_ready, NC * k + NC)
                for kc in range(KC):
                    for c in range(NC):
                        last = nc.tensor.transpose(ps[:, 4 + kc, c * L:(c + 1) * L], normed[:, c, kc * P:(kc + 1) * P], ident[0:L, 0:L])
                    last.then_inc(hT_full, 1)

            turn_tokens(0)
            pe.wait_ge(hT_ready, KC)
            for h in range(FH + FKV):
                w, hh = (wq, h) if h < FH else (wk, h - FH)
                if h == 0:
                    pe.wait_ge(ring_loaded[0], 16)
                if h == FH:
                    pe.wait_ge(ring_loaded[1], 32)
                if h >= 2:
                    pe.wait_ge(head_biased, h - 1)
                for kc in range(KC):
                    last = nc.tensor.matmul(ps[:, h % 2, 0:S], w[:, kc, hh * FD:(hh + 1) * FD], hT[:, kc, :], start=kc == 0, stop=kc == KC - 1)
                last.then_inc(head_full, 1)
            for k in range(2 * NC):
                if k >= 2:
                    pe.wait_ge(val_ready, k - 1)
                c, half = k // 2, slice(512 * (k % 2), 512 * (k % 2) + 512)
                for kc in range(KC):
                    last = nc.tensor.matmul(ps[0:L, 2 + k % 2, :], hT[:, kc, c * L:(c + 1) * L], wv[:, kc, half], start=kc == 0, stop=kc == KC - 1)
                last.then_inc(val_full, 1)

            def att(k):
                h, c = k // NC, k % NC
                if c == 0:
                    pe.wait_ge(head_ready, FH + h // 2 + 1)
                if k >= NC:
                    pe.wait_ge(prob_ready, k - NC + 1)
                o_ = ps[0:L, c, 0:(c + 1) * L]
                nc.tensor.matmul(o_, qT[:, h, c * L:(c + 1) * L], kT[:, h // 2, 0:(c + 1) * L], start=True, stop=False)
                nc.tensor.matmul(o_[:, c * L:(c + 1) * L], ident_bf[:], causal[:], start=False, stop=True).then_inc(att_full, 1)

            def turn_probs(k):
                c = k % NC
                pe.wait_ge(prob_scaled, k + 1)
                if k >= 2:
                    pe.wait_ge(pT_ready, k - 1)
                for b in range(c + 1):
                    last = nc.tensor.transpose(ps[0:L, 4 + k % 2, b * L:(b + 1) * L], prob2[:, k % 2, b * L:(b + 1) * L], ident[0:L, 0:L])
                last.then_inc(pT_full, 1)

            def weigh(h):
                pe.wait_ge(pT_ready, NC * h + NC)
                if h >= 2:
                    pe.wait_ge(attn_ready, h - 1)
                for b in range(NC):
                    last = nc.tensor.matmul(ps[:, 6 + h % 2, b * L:S], vals[:, b, (h // 2) * FD:(h // 2 + 1) * FD], probT[:, b, b * L:S],
                                            start=b == 0, stop=b == NC - 1)
                last.then_inc(attn_full, 1)

            pe.wait_ge(consts2, 2)
            pe.wait_ge(val_ready, 2 * NC)
            for k in range(FH * NC + 3):
                if k < FH * NC:
                    att(k)
                if 2 <= k < FH * NC + 2:
                    turn_probs(k - 2)
                if k >= NC and k % NC == 2:
                    weigh(k // NC - 1)
            pe.wait_ge(ring_loaded[2], 16)
            pe.wait_ge(attn_ready, FH)
            for c in range(NC):
                for h in range(FH):
                    last = nc.tensor.matmul(ps[0:L, c, :], attnT[:, h, c * L:(c + 1) * L], wo[:, h, :], start=h == 0, stop=h == FH - 1)
                last.then_inc(mid_full, 1)
            turn_tokens(1)
            pe.wait_ge(hT_ready, 2 * KC)
            pe.wait_ge(mid_ready, NC)
            pe.wait_ge(ring_loaded[0], 32)
            pe.wait_ge(ring_loaded[1], 48)

            def down(j):
                pe.wait_ge(hid_ready, j + 1)
                if j == 0:
                    pe.wait_ge(ring_loaded[2], 32)
                for c in range(NC):
                    last = nc.tensor.matmul(ps[0:L, 4 + c, :], mT[:, j, c * L:(c + 1) * L], w_down[:, j, :], start=j == 0, stop=j == FC - 1)
                    if j == FC - 1:
                        last.then_inc(down_full, 1)

            for j in range(FC + 2):
                if j < FC:
                    if j >= 2:
                        pe.wait_ge(hid_ready, j - 1)
                    for a, w in enumerate((w_gate, w_up)):
                        for kc in range(KC):
                            last = nc.tensor.matmul(ps[:, 2 * (j % 2) + a, 0:S], w[:, kc, j * P:(j + 1) * P], hT[:, kc, :], start=kc == 0, stop=kc == KC - 1)
                    last.then_inc(mlp_full, 1)
                if j >= 2:
                    down(j - 2)


def kernel(**inputs):
    import numpy as np
    import concourse.bacc as bacc
    from concourse.bass_utils import run_bass_kernel_spmd as run

    nc = bacc.Bacc("TRN2", target_bir_lowering=False, num_devices=1)
    a = {k: np.asarray(v) for k, v in inputs.items()}
    c, f = np.ascontiguousarray, np.float32

    def columns(v):
        return v.reshape(KC, P).T

    x_ = "L0_xattn_"
    ctxT = a["ctx_2048"].transpose(0, 2, 1)
    order = np.concatenate([np.arange(IMG, CTX), np.arange(IMG_MAIN)])
    arrays = {
        "x": c(a["x"]),
        "ctx": c(ctxT[:, :, order].reshape(B, KC, P, CTXC).transpose(0, 2, 1, 3)),
        "ctx_tail": c(ctxT[:, :, IMG_MAIN].T.reshape(KC, P, B).transpose(1, 0, 2)),
        "vecs": c(np.stack([columns(a[x_ + n]) for n in ("v_b", "v_img_b")], 1)),
        "w_router": c(a["L0_ffn_w_router"]),
    }
    for n in ("q_b", "k_b", "k_img_b", "norm_q_w", "norm_k_w", "norm_k_img_w", "o_b"):
        arrays[n] = c(a[x_ + n])
    f_ = "L0_ffn_"
    arrays["fvec"] = c(np.concatenate([a[f_ + "bq"].reshape(FH, FD).T, a[f_ + "bk"].reshape(FKV, FD).T,
                                       columns(a[f_ + "ln1_w"]), columns(a[f_ + "ln2_w"])], 1))
    arrays["bv"] = c(a[f_ + "bv"])
    for w in ("wq", "wk", "wv", "wo", "w_gate", "w_up", "w_down"):
        arrays[w] = c(a[f_ + w])
    token = np.arange(L)
    arrays["earlier"] = (token[None, :] < token[:, None]).astype(f)
    arrays["later"] = (token[None, :] > token[:, None]).astype(f)
    arrays["slot_far"] = np.broadcast_to(np.arange(TOPK, dtype=f) - f(FAR), (L, TOPK)).copy()
    arrays["token_no"] = token.astype(f)[:, None].copy()
    arrays["token_base"] = (L * (BPC * np.arange(NC)[None, :] + token[:, None] // TOPK)).astype(f)
    freq = f(1.0) / np.power(f(10000.0), np.arange(0, FD, 2, dtype=f) / f(FD))
    angle = token.astype(f)[:, None] * freq
    arrays["cos_tab"] = np.concatenate([np.cos(angle), np.cos(angle)], 1).astype(f)
    arrays["sin_tab"] = np.concatenate([np.sin(angle), -np.sin(angle)], 1).astype(f)
    for w in ("q", "k", "v", "k_img", "v_img", "o"):
        arrays["w_" + w] = c(a[x_ + w + "_w"].T)
    feeds, t = {}, {}
    for k, v in arrays.items():
        feeds[f"in_{k}_dram"] = v
        t[k] = nc.dram_tensor(f"in_{k}_dram", v.shape, mybir.dt.from_np(v.dtype), kind="ExternalInput").ap()
    out = nc.dram_tensor("out_dram", (B, L, D), F32, kind="ExternalOutput").ap()
    build(nc, t, out)
    r = run(nc, [feeds], core_ids=[0])
    return r.results[0]["out_dram"]
```

```python
from contextlib import ExitStack

import concourse.bass as bass
from concourse import mybir

ACT = mybir.ActivationFunctionType
ALU = mybir.AluOpType
AX = mybir.AxisListType
F32 = mybir.dt.float32
F32R = mybir.dt.float32r
BF16 = mybir.dt.bfloat16

B, L, D = 32, 112, 512
IMG, CTX = 257, 375
TXT = CTX - IMG
NH, HD = 16, 32
P = 128
KC = D // P
GH = P // HD
NG = NH // GH
IMG_MAIN = IMG - 1
TAIL = TXT
NKEY = CTX + 1
CHUNK_C = TXT + 1
CTXC = TXT + IMG_MAIN
TOK_ROWS = (L, TXT, P, P)
KEY_AT = (None, 0, TAIL + 1, TAIL + 1 + P)
VW = HD + 1
LN_EPS, RMS_EPS = 1e-5, 1e-6
SCALE = HD ** -0.5
CHUNKS = [(0, CHUNK_C), (CHUNK_C, P), (CHUNK_C + P, P)]
TOPK = max(1, int(L * 0.125))
S = B * TOPK
NC = S // L
BPC = B // NC
FH, FKV, FD = 16, 8, 128
FF = 2048
FC = FF // P
FSCALE = FD ** -0.5
HALF = FD // 2
LAG = 3
MASKED = -1e30
FAR = 1000.0


def build(nc, t, out):
    with ExitStack() as ctx:
        def sb(name, shape, dt=F32):
            return ctx.enter_context(nc.sbuf_tensor(name, shape, dt))

        def sem(name):
            return ctx.enter_context(nc.semaphore(name))

        ps = ctx.enter_context(nc.psum_tensor("ps", [P, 8, 512], F32))
        bank0, bank1 = ps[:, 0, :], ps[:, 1, :]
        vtail_dram = nc.dram_tensor("vtail_dram", (B, NH * VW), F32, kind="Internal").ap()
        xh_dram = nc.dram_tensor("xh_dram", (B * L, 2 * D), F32, kind="Internal").ap()
        score_dram = nc.dram_tensor("score_dram", (B, L), F32, kind="Internal").ap()

        ident = sb("ident", [P, P])
        ln_eps = sb("ln_eps", [P, 1])
        rms_eps = sb("rms_eps", [P, 1])
        wr = sb("wr", [L, D])
        rank = sb("rank", [L, B])

        phase1 = ExitStack()

        def p1(name, shape, dt=F32):
            return phase1.enter_context(nc.sbuf_tensor(name, shape, dt))

        W = ["k", "q", "k_img", "v_img", "v", "o"]
        w_hi, w_lo = {}, {}
        for w in W:
            w_hi[w] = p1(f"w_{w}_hi", [P, KC, D], F32R)
            w_lo[w] = p1(f"w_{w}_lo", [P, KC, D], F32R)
        neg_ident = p1("neg_ident", [L, L], BF16)
        strip = p1("strip", [L, TAIL + P + 1], BF16)
        ones_c_tail, ones_img, ones_c_txt = strip[:, 0:CHUNK_C], strip[:, TAIL:TAIL + P], strip[:, P:P + CHUNK_C]
        vecs = p1("vecs", [P, 2, KC])
        q_bias, k_bias, ki_bias = (p1(n, [P, D]) for n in ("q_bias", "k_bias", "ki_bias"))
        nq_row = q_bias
        w_txt = p1("w_txt", [P, D])
        w_img = p1("w_img", [P, D])
        out_bias = p1("out_bias", [L, D])
        k_tail_hi = p1("k_tail_hi", [P, KC, B], F32R)
        k_tail_lo = p1("k_tail_lo", [P, KC, B], F32R)
        ctx_raw = p1("ctx_raw", [P, KC, CTXC])
        ctx_hi = p1("ctx_hi", [P, KC, CTXC], F32R)
        ctx_lo = p1("ctx_lo", [P, KC, CTXC], F32R)
        x_in = p1("x_in", [L, D])
        xn = x_in
        ln1_stats = p1("ln1_stats", [L, 6])
        ln1_mv = p1("ln1_mv", [L, 2])
        ln1_sd = p1("ln1_sd", [L, 1])
        ln1_rstd = p1("ln1_rstd", [L, 1])
        xT_hi = p1("xT_hi", [P, KC, L], F32R)
        xT_lo = p1("xT_lo", [P, KC, L], F32R)
        proj = p1("proj", [P, 4, D])
        sq_junk = p1("sq_junk", [P, D], BF16)
        sq_sum = p1("sq_sum", [P, 5])
        rms = p1("rms", [P, 5])
        rstd1 = p1("rstd1", [P, 5])
        k_hi = p1("k_hi", [P, KC, NKEY], F32R)
        k_lo = p1("k_lo", [P, KC, NKEY], F32R)
        q_hi = p1("q_hi", [P, NG, GH, L], F32R)
        q_lo = p1("q_lo", [P, NG, GH, L], F32R)
        v_c = p1("v_c", [CHUNK_C, NH, 2 * VW])
        v_a = p1("v_a", [P, NH, VW])
        v_b = p1("v_b", [P, NH, VW])
        score_now = p1("score_now", [L, 1])
        score_row = p1("score_row", [L, L])
        earlier = p1("earlier", [L, L], BF16)
        top = p1("top", [L, NG, 2, GH])
        shift = p1("shift", [L, NG, 2, GH, L], BF16)
        prob = p1("prob", [P, 2, 3, GH * L])
        prob_flat = prob[:].rearrange("p a c n -> p (a c n)")
        stage = prob_flat[:, 0:4 * D].rearrange("p (a n) -> p a n", a=2)
        vbias_cols = prob_flat[:, 4 * D:4 * D + KC * L].rearrange("p (c l) -> p c l", c=KC)
        ctx_tail = prob_flat[:, 4 * D + KC * L:4 * D + KC * (L + B)].rearrange("p (c b) -> p c b", c=KC)
        rec = p1("rec", [L, GH, 2])
        o_txt = p1("o_txt", [L, GH, HD])
        equal = o_txt[:].rearrange("l h d -> l (h d)")[:, 0:L]
        o = p1("o", [L, D])
        tail_proj = o[0:B]
        oT_hi, oT_lo = xT_hi, xT_lo
        x_res = p1("x_res", [L, D])
        xh = p1("xh", [L, 2, D])
        ln2_stats = p1("ln2_stats", [L, 6])
        ln2_mv = p1("ln2_mv", [L, 2])
        ln2_sd = p1("ln2_sd", [L, 1])
        ln2_rstd = p1("ln2_rstd", [L, 1])
        out_sb = p1("out_sb", [L, D])
        score_junk = out_sb
        v_tail = xh[0:B].rearrange("b a d -> b (a d)")[:, 0:NH * VW].rearrange("b (h w) -> b h w", h=NH)

        phase1.close()
        raw_weights = ExitStack()
        ring = [raw_weights.enter_context(nc.sbuf_tensor(f"ring{j}", [P, 4 * FF], F32)) for j in range(3)]
        raw_weights.close()
        ring_lo = [sb(f"ring_lo{j}", [P, 4 * FF], F32R) for j in range(3)]
        def parts(rings):
            whole = [r[:].rearrange("p (c n) -> p c n", c=KC) for r in rings]
            half = [rings[1][:, 2 * FF * e:2 * FF * (e + 1)].rearrange("p (c n) -> p c n", c=KC) for e in range(2)]
            return whole[0], half[0], half[1], whole[0], whole[1], rings[2][:].rearrange("p (c n) -> p c n", c=FC)

        wq, wk, wv, w_gate, w_up, w_down = parts(ring)
        wq_lo, wk_lo, wv_lo, w_gate_lo, w_up_lo, w_down_lo = parts(ring_lo)
        wo = ring[2][:].rearrange("p (c n) -> p c n", c=FH)
        wv_hi = ring_lo[0][:, 0:2 * FF].rearrange("p (c n) -> p c n", c=KC)
        fvec = sb("fvec", [P, FH + FKV + 2 * KC])
        bv_row = sb("bv_row", [L, FKV * FD])
        tok = sb("tok", [L, NC], mybir.dt.int32)
        token_base = sb("token_base", [L, NC])
        xh_sel = sb("xh_sel", [L, NC, 2, D])
        sel_score = sb("sel_score", [L, NC])
        gate_e = sb("gate_e", [L, NC])
        gate = sb("gate", [L, NC])
        keep = xh_sel[:, :, 0, :]
        sums = sb("sums", [L, NC])
        rstd = sb("rstd", [L, NC])
        hT_hi = sb("hT_hi", [P, KC, S], F32R)
        over_normed = ExitStack()
        hT_lo = over_normed.enter_context(nc.sbuf_tensor("hT_lo", [P, KC, S], F32R))
        over_normed.close()
        normed = sb("normed", [L, NC, D])
        cos = sb("cos", [P, S])
        sin = sb("sin", [P, S])
        topk = ExitStack()

        def tk(name, shape, dt=F32):
            return topk.enter_context(nc.sbuf_tensor(name, shape, dt))

        chosen = tk("chosen", [L, B])
        before = tk("before", [L, B])
        slot_hot = tk("slot_hot", [L, B, TOPK])
        later = tk("later", [L, L])
        slot_far = tk("slot_far", [L, TOPK])
        token_no = tk("token_no", [L, 1])
        cos_tab = tk("cos_tab", [L, P])
        sin_tab = tk("sin_tab", [L, P])
        topk.close()
        qk = ExitStack()
        qT = qk.enter_context(nc.sbuf_tensor("qT", [P, FH, S], F32))
        kT = qk.enter_context(nc.sbuf_tensor("kT", [P, FKV, S], F32))
        qk.close()
        attnT = qT
        mlp = ExitStack()
        m_prod = mlp.enter_context(nc.sbuf_tensor("m_prod", [P, 2, S], F32))
        m_hi = mlp.enter_context(nc.sbuf_tensor("m_hi", [P, 2, S], F32R))
        m_lo = mlp.enter_context(nc.sbuf_tensor("m_lo", [P, 2, S], F32R))
        down_hi = mlp.enter_context(nc.sbuf_tensor("down_hi", [P, 3, D], F32R))
        mlp.enter_context(nc.sbuf_tensor("mlp_gap", [P, FH * S - 6 * S - 3 * D], F32))
        gate_up_hi = mlp.enter_context(nc.sbuf_tensor("gate_up_hi", [P, 3, 2, KC, P], F32R))
        mlp.close()
        sb("qk_space", [P, (FH + FKV) * S])
        over_vals = ExitStack()
        head_hi = over_vals.enter_context(nc.sbuf_tensor("head_hi", [P, 4, KC, FD], F32R))
        over_vals.close()
        vals = sb("vals", [L, NC, FKV * FD])
        x_mid = vals[:, :, 0:D]
        rows4 = sb("rows4", [P, LAG + 1, S])
        biased, rot = rows4[:, 0:2], rows4[:, 2:4]
        causal = sb("causal", [L, L], BF16)
        ident_bf = sb("ident_bf", [L, L], BF16)
        neg_top = sb("neg_top", [L, NC])
        prob_sum = sb("prob_sum", [L, NC])
        prob2 = rows4[0:L]
        probT = normed[:].rearrange("l c d -> l (c d)")[:, 0:NC * S].rearrange("l (c s) -> l c s", c=NC)
        silu_e = biased
        silu_g = rot

        consts_zeroed, consts_ready = sem("consts_zeroed"), sem("consts_ready")
        vecs_loaded, rows_loaded, tails_loaded = sem("vecs_loaded"), sem("rows_loaded"), sem("tails_loaded")
        piece_loaded = [sem("piece_loaded0"), sem("piece_loaded1")]
        piece_hi, piece_lo = sem("piece_hi"), sem("piece_lo")
        vecs_ready = sem("vecs_ready")
        pro_full, pro_done, vtail_stored = sem("pro_full"), sem("pro_done"), sem("vtail_stored")
        ctx_loaded, ctx_hi_done, ctx_lo_done = sem("ctx_loaded"), sem("ctx_hi_done"), sem("ctx_lo_done")
        x_loaded, ln1_step, ln1_sd_done = sem("x_loaded"), sem("ln1_step"), sem("ln1_sd_done")
        xn_ready, xT_hi_done = sem("xn_ready"), sem("xT_hi_done")
        b0_full, b0_done, b1_full, b1_done = sem("b0_full"), sem("b0_done"), sem("b1_full"), sem("b1_done")
        xT_full, xT_lo_done = sem("xT_full"), sem("xT_lo_done")
        sq_done, rms_done, rms_inv = sem("sq_done"), sem("rms_done"), sem("rms_inv")
        scaled, turned, k_hi_done, q_hi_done = sem("scaled"), sem("turned"), sem("k_hi_done"), sem("q_hi_done")
        tail_step, tail_scaled, tail_turned = sem("tail_step"), sem("tail_scaled"), sem("tail_turned")
        tail_hi_done, tail_ready = sem("tail_hi_done"), sem("tail_ready")
        tail_split, bias_split = sem("tail_split"), sem("bias_split")
        kq_lo_done, vtail_loaded = sem("kq_lo_done"), sem("vtail_loaded")
        s_full, s_done, shift_ready = sem("s_full"), sem("s_done"), sem("shift_ready")
        st_full, exp_done = sem("st_full"), sem("exp_done")
        pv_full, norm_step, pv_done = sem("pv_full"), sem("norm_step"), sem("pv_done")
        oT_hi_done, xres_loaded, xres_ready = sem("oT_hi_done"), sem("xres_loaded"), sem("xres_ready")
        ln2_step, ln2_sd_done, h_ready = sem("ln2_step"), sem("ln2_sd_done"), sem("h_ready")
        h_step, rows_ready, passed = sem("h_step"), sem("rows_ready"), sem("passed")
        score_ready, out_ready = sem("score_ready"), sem("out_ready")
        xh_stored, out_stored, score_stored = sem("xh_stored"), sem("out_stored"), sem("score_stored")

        topk_loaded, score_row_loaded, fvec_loaded = sem("topk_loaded"), sem("score_row_loaded"), sem("fvec_loaded")
        ring_loaded = [sem(f"ring_loaded{j}") for j in range(3)]
        rank_step, rank_done, chosen_ready, before_full, hot_ready = sem("rank_step"), sem("rank_done"), sem("chosen_ready"), sem("before_full"), sem("hot_ready")
        tok_full, tok_ready, rope_full, rope_ready = sem("tok_full"), sem("tok_ready"), sem("rope_full"), sem("rope_ready")
        gathered = [sem(f"gathered{c}") for c in range(NC)]
        sums_ready, root_ready, rstd_ready, normed_ready = sem("sums_ready"), sem("root_ready"), sem("rstd_ready"), sem("normed_ready")
        hT_full, hT_ready = sem("hT_full"), sem("hT_ready")
        head_full, head_biased, rot_step, head_ready = sem("head_full"), sem("head_biased"), sem("rot_step"), sem("head_ready")
        val_full, val_ready = sem("val_full"), sem("val_ready")
        att_full, top_ready, prob_ready = sem("att_full"), sem("top_ready"), sem("prob_ready")
        inv_ready, prob_scaled, pT_full, pT_ready = sem("inv_ready"), sem("prob_scaled"), sem("pT_full"), sem("pT_ready")
        attn_full, attn_ready = sem("attn_full"), sem("attn_ready")
        mid_full, mid_ready = sem("mid_full"), sem("mid_ready")
        mlp_full, silu_exp, silu_step, hid_ready = sem("mlp_full"), sem("silu_exp"), sem("silu_step"), sem("hid_ready")
        down_full, sum_ready, final_ready, scattered = sem("down_full"), sem("sum_ready"), sem("final_ready"), sem("scattered")
        gate_step, gate_exp, consts2 = sem("gate_step"), sem("gate_exp"), sem("consts2")
        hT_hi_done, w_hi_done, w_lo_done = sem("hT_hi_done"), sem("w_hi_done"), sem("w_lo_done")
        gate_up_hi_done, gate_up_lo_done = sem("gate_up_hi_done"), sem("gate_up_lo_done")
        down_hi_done, down_lo_done, down_step = sem("down_hi_done"), sem("down_lo_done"), sem("down_step")
        m_hi_done, m_lo_done = sem("m_hi_done"), sem("m_lo_done")

        block = ctx.enter_context(nc.Block())

        def slot1(n, k):
            return 5 * n - 2 + k if not isinstance(n, int) or n else k

        def slot1_own(i, k):
            return 5 * i + 5 + k if not isinstance(i, int) or i < B - 1 else 5 * i + 3 + k

        def over_batches(eng, pre, body):
            pre()
            body(0, 1, 2, None)
            body(1, 2, 3, 0)
            with eng.Fori(2, B - 2) as i:
                body(i, i + 1, i + 2, i - 1)
            body(B - 2, B - 1, None, B - 3)
            body(B - 1, None, None, B - 2)

        PIECES = 2 * len(W)

        def head_weights(h):
            if h < FH + FKV:
                w, lo, cols = (wq, wq_lo, slice(h * FD, (h + 1) * FD)) if h < FH else (wk, wk_lo, slice((h - FH) * FD, (h - FH + 1) * FD))
                return w[:, :, cols], lo[:, :, cols], head_hi[:, h % 4]
            cols = slice(512 * (h - FH - FKV), 512 * (h - FH - FKV + 1))
            return wv[:, :, cols], wv_lo[:, :, cols], wv_hi[:, :, cols]

        @block.sync
        def _(sp):
            sp.dma_start(vecs[:], t["vecs"]).then_inc(vecs_loaded, 16)
            sp.dma_start(ctx_tail, t["ctx_tail"]).then_inc(tails_loaded, 16)

            def load_x(m):
                sp.dma_start(x_in[:], t["x"][bass.ds(m, 1)].rearrange("o t d -> t (o d)")).then_inc(x_loaded, 16)

            def load_ctx(n):
                sp.dma_start(ctx_raw[:], t["ctx"][bass.ds(n, 1)].rearrange("o p c n -> p (o c) n")).then_inc(ctx_loaded, 16)

            def load_piece(j):
                sp.dma_start(stage[:, j % 2, :], t["w_" + W[j // 2]].rearrange(
                    "(c p) o -> p c o", p=P)[:, 2 * (j % 2):2 * (j % 2) + 2, :]).then_inc(piece_loaded[j % 2], 16)

            def load_tail(n):
                sp.dma_start(v_c[TXT:TXT + 1, :, 0:VW], vtail_dram[bass.ds(n, 1)].rearrange(
                    "o (h w) -> o h w", h=NH)).then_inc(vtail_loaded, 16)

            def store(p):
                sp.wait_ge(score_ready, p + 1)
                sp.dma_start(score_dram[bass.ds(p, 1)].rearrange("o l -> l o"), score_now[:]).then_inc(score_stored, 16)
                sp.dma_start(xh_dram.rearrange("(b l) d -> b l d", b=B)[bass.ds(p, 1)].rearrange("o l d -> l (o d)"),
                             xh[:].rearrange("l a d -> l (a d)")).then_inc(xh_stored, 16)
                sp.wait_ge(score_stored, 16 * p + 16)
                if not isinstance(p, int) or p:
                    sp.wait_ge(rank_done, p)
                sp.dma_start(score_row[:], score_dram[bass.ds(p, 1)].rearrange("o l -> (o l)").partition_broadcast(L)).then_inc(score_row_loaded, 16)
                sp.wait_ge(out_ready, p + 1)
                sp.dma_start(out[bass.ds(p, 1)].rearrange("o l d -> l (o d)"), out_sb[:]).then_inc(out_stored, 16)

            def pre():
                sp.sem_inc(out_stored, 16)
                load_x(0)
                load_ctx(0)
                load_piece(0)
                load_piece(1)
                for dst, name in ((nq_row, "norm_q_w"), (w_txt, "norm_k_w"), (w_img, "norm_k_img_w"),
                                  (k_bias, "k_b"), (ki_bias, "k_img_b")):
                    sp.dma_start(dst[:], t[name].partition_broadcast(P)).then_inc(rows_loaded, 16)
                sp.dma_start(out_bias[:], t["o_b"].partition_broadcast(L)).then_inc(rows_loaded, 16)
                sp.dma_start(wr[:], t["w_router"].partition_broadcast(L)).then_inc(rows_loaded, 16)
                sp.wait_ge(rows_ready, 1)
                sp.dma_start(q_bias[:], t["q_b"].partition_broadcast(P)).then_inc(rows_loaded, 16)
                for j in range(2, PIECES):
                    sp.wait_ge(piece_hi, j - 1)
                    sp.wait_ge(piece_lo, j - 1)
                    load_piece(j)
                sp.wait_ge(xT_full, 1)
                load_x(1)
                sp.wait_ge(ctx_hi_done, 1)
                sp.wait_ge(ctx_lo_done, 1)
                load_ctx(1)
                sp.wait_ge(pro_done, 2)
                sp.dma_start(vtail_dram, v_tail.rearrange("b h w -> b (h w)")).then_inc(vtail_stored, 16)
                sp.wait_ge(vtail_stored, 16)
                sp.wait_ge(consts_ready, 3)
                load_tail(0)

            def body(i, n, m, p):
                if p is not None:
                    sp.wait_ge(b1_done, slot1_own(p, 2))
                sp.dma_start(x_res[:], t["x"][bass.ds(i, 1)].rearrange("o t d -> t (o d)")).then_inc(xres_loaded, 16)
                if n is None:
                    sp.wait_ge(b0_full, 4 * i + 2)
                    sp.dma_start(wq, t["wq"].rearrange("(c p) n -> p c n", p=P)).then_inc(ring_loaded[0], 16)
                    sp.wait_ge(b1_full, 5 * i + 3)
                    sp.dma_start(wk, t["wk"].rearrange("(c p) n -> p c n", p=P)).then_inc(ring_loaded[1], 16)
                    sp.dma_start(wv, t["wv"].rearrange("(c p) n -> p c n", p=P)).then_inc(ring_loaded[1], 16)
                if m is not None:
                    sp.wait_ge(xT_full, m)
                    load_x(m)
                    sp.wait_ge(ctx_hi_done, m)
                    sp.wait_ge(ctx_lo_done, m)
                    load_ctx(m)
                if p is not None:
                    store(p)
                if n is not None:
                    sp.wait_ge(pv_full, 4 * n)
                    load_tail(n)

            over_batches(sp, pre, body)
            store(B - 1)
            sp.wait_ge(xh_stored, 16 * B)
            sp.wait_ge(score_stored, 16 * B)
            sp.wait_ge(out_stored, 16 * B + 16)

            for dst, name in ((later, "later"), (slot_far, "slot_far"), (token_no, "token_no"),
                              (cos_tab, "cos_tab"), (sin_tab, "sin_tab"), (token_base, "token_base")):
                sp.dma_start(dst[:], t[name]).then_inc(topk_loaded, 16)
            sp.dma_start(fvec[:], t["fvec"]).then_inc(fvec_loaded, 16)
            sp.dma_start(bv_row[:], t["bv"].partition_broadcast(L)).then_inc(fvec_loaded, 16)
            sp.dma_start(wo, t["wo"].rearrange("(c p) n -> p c n", p=P)).then_inc(ring_loaded[2], 16)
            sp.wait_ge(val_full, 2 * NC)
            sp.dma_start(w_gate, t["w_gate"].rearrange("(c p) n -> p c n", p=P)).then_inc(ring_loaded[0], 16)
            sp.dma_start(w_up, t["w_up"].rearrange("(c p) n -> p c n", p=P)).then_inc(ring_loaded[1], 16)
            sp.wait_ge(mid_full, NC)
            sp.dma_start(w_down, t["w_down"].rearrange("(c p) n -> p c n", p=P)).then_inc(ring_loaded[2], 16)

        @block.gpsimd
        def _(pool):
            def split_ctx(n):
                pool.wait_ge(ctx_hi_done, n + 1)
                nc.gpsimd.tensor_tensor(ctx_lo[:], ctx_raw[:], ctx_hi[:].bitcast(F32), ALU.subtract).then_inc(ctx_lo_done, 1)

            def normalise_x(m):
                pool.wait_ge(ln1_step, 3 * m + 3)
                pool.sem_inc(passed, 1)
                nc.gpsimd.tensor_scalar(xn[:], x_in[:], ln1_mv[:, 0:1], ln1_rstd[:], ALU.subtract, ALU.mult).then_inc(xn_ready, 1)

            def diagonals(i, g):
                pool.wait_ge(s_done, 8 * i + 2 * g + 2)
                nc.gpsimd.tensor_tensor(shift[:, g].rearrange("l s h q -> l (s h) q"),
                                        neg_ident[:].unsqueeze(1).to_broadcast([L, 2 * GH, L]),
                                        top[:, g].rearrange("l s h -> l (s h)").unsqueeze(2).to_broadcast([L, 2 * GH, L]),
                                        ALU.mult).then_inc(shift_ready, 1)

            def output(p):
                pool.wait_ge(score_ready, p + 1)
                nc.gpsimd.tensor_tensor(out_sb[:], xh[:, 0], xh[:, 1], ALU.add).then_inc(out_ready, 1)

            def pre():
                nc.gpsimd.memset(ident[:], 0.0)
                nc.gpsimd.memset(neg_ident[:], 0.0)
                nc.gpsimd.memset(earlier[:], 1.0)
                nc.gpsimd.memset(strip[:], 0.0).then_inc(consts_zeroed, 1)
                pool.wait_ge(consts_zeroed, 1)
                nc.gpsimd.affine_select(out=ident[:], in_=ident[:], compare_op=ALU.not_equal, fill=1.0, base=0,
                                        pattern=[[-1, P]], channel_multiplier=1)
                nc.gpsimd.affine_select(out=neg_ident[:], in_=neg_ident[:], compare_op=ALU.not_equal, fill=-1.0, base=0,
                                        pattern=[[-1, L]], channel_multiplier=1)
                nc.gpsimd.affine_select(out=earlier[:], in_=earlier[:], compare_op=ALU.is_ge, fill=0.0, base=-1,
                                        pattern=[[-1, L]], channel_multiplier=1)
                nc.gpsimd.memset(ones_img, 1.0)
                nc.gpsimd.memset(sq_sum[:], 1.0)
                nc.gpsimd.memset(ln_eps[:], LN_EPS)
                nc.gpsimd.memset(rms_eps[:], RMS_EPS).then_inc(consts_ready, 1)
                normalise_x(0)
                split_ctx(0)
                nc.gpsimd.memset(k_hi[:, :, NKEY - 1:NKEY].bitcast(F32), 0.0)
                nc.gpsimd.memset(k_lo[:, :, NKEY - 1:NKEY].bitcast(F32), 0.0)
                nc.gpsimd.memset(q_hi[:].bitcast(F32), 0.0)
                nc.gpsimd.memset(q_lo[:].bitcast(F32), 0.0).then_inc(consts_ready, 1)
                nc.gpsimd.memset(v_c[:], 0.0)
                nc.gpsimd.memset(v_tail[:, :, HD:VW], 1.0)
                nc.gpsimd.memset(v_a[:, :, HD:VW], 1.0)
                nc.gpsimd.memset(v_b[:, :, HD:VW], 1.0).then_inc(consts_zeroed, 1)
                pool.wait_ge(consts_zeroed, 2)
                nc.gpsimd.memset(v_c[0:TXT, :, VW + HD:2 * VW], 1.0).then_inc(consts_ready, 1)
                normalise_x(1)

            def body(i, n, m, p):
                for g in range(NG):
                    diagonals(i, g)
                if n is not None:
                    split_ctx(n)
                pool.wait_ge(xres_loaded, 16 * i + 16)
                if p is None:
                    pool.wait_ge(rows_ready, 2)
                nc.gpsimd.tensor_tensor(x_res[:], x_res[:], out_bias[:], ALU.add).then_inc(xres_ready, 1)
                if m is not None:
                    normalise_x(m)
                if p is not None:
                    output(p)

            over_batches(pool, pre, body)
            output(B - 1)

            def weights_lo(h):
                pool.wait_ge(w_hi_done, h + 1)
                w, lo, hi = head_weights(h)
                nc.gpsimd.tensor_tensor(lo, w, hi.bitcast(F32), ALU.subtract).then_inc(w_lo_done, 1)

            for h in range(4):
                weights_lo(h)
            pool.wait_ge(tok_ready, 1)
            for c in range(NC):
                nc.gpsimd.indirect_dma_start(xh_sel[:, c].rearrange("l a d -> l (a d)"), None, xh_dram,
                                             bass.IndirectOffsetOnAxis(ap=tok[:, c:c + 1], axis=0)).then_inc(gathered[c], 16)
            pool.wait_ge(rope_ready, 2)
            nc.gpsimd.memset(causal[:], 0.0)
            nc.gpsimd.memset(ident_bf[:], 0.0).then_inc(consts2, 1)
            pool.wait_ge(consts2, 1)
            nc.gpsimd.affine_select(out=causal[:], in_=causal[:], compare_op=ALU.is_ge, fill=MASKED, base=0,
                                    pattern=[[-1, L]], channel_multiplier=1)
            nc.gpsimd.affine_select(out=ident_bf[:], in_=ident_bf[:], compare_op=ALU.not_equal, fill=1.0, base=0,
                                    pattern=[[-1, L]], channel_multiplier=1).then_inc(consts2, 1)
            for h in range(4, FH + FKV + 2):
                weights_lo(h)

            def gate_up_rest(j):
                pool.wait_ge(gate_up_hi_done, j + 1)
                for e, (w, lo) in enumerate(((w_gate, w_gate_lo), (w_up, w_up_lo))):
                    cols = slice(j * P, (j + 1) * P)
                    last = nc.gpsimd.tensor_tensor(lo[:, :, cols], w[:, :, cols], gate_up_hi[:, j % 3, e].bitcast(F32), ALU.subtract)
                last.then_inc(gate_up_lo_done, 1)

            gate_up_rest(0)
            gate_up_rest(1)
            for j in range(FC):
                if j + 2 < FC:
                    gate_up_rest(j + 2)
                pool.wait_ge(down_hi_done, j + 1)
                nc.gpsimd.tensor_tensor(w_down_lo[:, j, :], w_down[:, j, :], down_hi[:, j % 3].bitcast(F32), ALU.subtract).then_inc(down_lo_done, 1)
            for c in range(NC):
                pool.wait_ge(final_ready, c + 1)
                nc.gpsimd.indirect_dma_start(out.rearrange("b l d -> (b l) d"), bass.IndirectOffsetOnAxis(ap=tok[:, c:c + 1], axis=0),
                                             keep[:, c], None).then_inc(scattered, 16)
            pool.wait_ge(scattered, 16 * NC)


        @block.scalar
        def _(act):
            def split_ctx(n):
                act.wait_ge(ctx_loaded, 16 * n + 16)
                nc.scalar.activation(ctx_hi[:], ctx_raw[:], ACT.Copy).then_inc(ctx_hi_done, 1)

            def x_hi(n):
                act.wait_ge(xT_full, n + 1)
                nc.scalar.activation(xT_hi[:], ps[:, 6, 0:KC * L].rearrange("p (c l) -> p c l", c=KC), ACT.Copy).then_inc(xT_hi_done, 1)

            def squares(n, k):
                rows = TOK_ROWS[k]
                done, slot = ((b1_done, slot1(n, k // 2)), (b0_done, 4 * n + k // 2))[k % 2]
                act.wait_ge(done, slot + 1)
                if not isinstance(n, int) or n or k:
                    act.wait_ge(sq_done, 4 * n + k)
                nc.scalar.activation(sq_junk[0:rows], proj[0:rows, k, :], ACT.Square, accum_out=sq_sum[0:rows, k:k + 1]).then_inc(sq_done, 1)

            def roots(n, m, p):
                if n is not None:
                    act.wait_ge(sq_done, 4 * n + 4)
                    nc.scalar.activation(rms[:, 0:4], sq_sum[:, 0:4], ACT.Sqrt, bias=rms_eps[:], scale=1.0 / D).then_inc(rms_done, 1)
                if m is not None:
                    act.wait_ge(ln1_step, 3 * m + 2)
                    nc.scalar.activation(ln1_sd[:], ln1_mv[:, 1:2], ACT.Sqrt, bias=ln_eps[0:L]).then_inc(ln1_sd_done, 1)
                if p is not None:
                    act.wait_ge(ln2_step, 3 * p + 3)
                    nc.scalar.activation(ln2_sd[:], ln2_mv[:, 1:2], ACT.Sqrt, bias=ln_eps[0:L]).then_inc(ln2_sd_done, 1)

            def kq_hi(n):
                act.wait_ge(turned, 4 * n + 1)
                for j in range(GH):
                    part = slice(HD * j, HD * (j + 1))
                    last = nc.scalar.activation(q_hi[part, :, j, :], ps[part, 2, 0:NG * L].rearrange("p (g l) -> p g l", g=NG), ACT.Copy)
                last.then_inc(q_hi_done, 1)
                for k in range(1, 4):
                    rows = TOK_ROWS[k]
                    act.wait_ge(turned, 4 * n + k + 1)
                    nc.scalar.activation(k_hi[:, :, KEY_AT[k]:KEY_AT[k] + rows],
                                         ps[:, 2 + k, 0:KC * rows].rearrange("p (c l) -> p c l", c=KC), ACT.Copy).then_inc(k_hi_done, 1)

            def exps(i, g):
                for c, (_, rows) in enumerate(CHUNKS):
                    k = 3 * g + c
                    act.wait_ge(st_full, 12 * i + k + 1)
                    if c == 0 and g >= 2:
                        act.wait_ge(pv_full, 4 * i + g - 1)
                    nc.scalar.activation(prob[0:rows, g % 2, c, :], ps[0:rows, 2 + k % 4, 0:GH * L], ACT.Exp).then_inc(exp_done, 1)

            def pre():
                act.wait_ge(consts_ready, 1)
                act.wait_ge(ln1_step, 2)
                nc.scalar.activation(ln1_sd[:], ln1_mv[:, 1:2], ACT.Sqrt, bias=ln_eps[0:L]).then_inc(ln1_sd_done, 1)
                split_ctx(0)

                def piece(j):
                    act.wait_ge(piece_loaded[j % 2], 16 * (j // 2) + 16)
                    nc.scalar.activation(w_hi[W[j // 2]][:, 2 * (j % 2):2 * (j % 2) + 2, :],
                                         stage[:, j % 2, :].rearrange("p (c o) -> p c o", c=2), ACT.Copy).then_inc(piece_hi, 1)

                for j in range(0, 2):
                    piece(j)
                x_hi(0)
                for j in range(2, 5):
                    piece(j)
                act.wait_ge(tails_loaded, 16)
                nc.scalar.activation(k_tail_hi[:], ctx_tail, ACT.Copy).then_inc(tail_split, 1)
                for j in range(5, PIECES):
                    piece(j)
                act.wait_ge(vecs_ready, 1)
                act.wait_ge(b1_full, 1)
                nc.scalar.activation(xT_hi[:], vbias_cols, ACT.Copy).then_inc(bias_split, 1)
                for k in range(4):
                    squares(0, k)
                act.wait_ge(pro_done, 1)
                act.wait_ge(sq_done, 4)
                nc.scalar.activation(sq_junk[0:B], tail_proj, ACT.Square, accum_out=sq_sum[0:B, 4:5]).then_inc(tail_step, 1)
                act.wait_ge(tail_step, 1)
                nc.scalar.activation(rms[:, 4:5], sq_sum[:, 4:5], ACT.Sqrt, bias=rms_eps[:], scale=1.0 / D)
                roots(0, 1, None)
                act.wait_ge(consts_ready, 2)
                kq_hi(0)
                act.wait_ge(tail_turned, 1)
                nc.scalar.activation(k_tail_hi[:], ps[:, 7, 0:KC * B].rearrange("p (c b) -> p c b", c=KC), ACT.Copy).then_inc(tail_hi_done, 1)

            def body(i, n, m, p):
                if n is not None:
                    x_hi(n)
                act.wait_ge(b0_full, 4 * i + 3)
                nc.scalar.activation(v_a[:, :, 0:HD], bank0.rearrange("p (h d) -> p h d", h=NH), ACT.Copy).then_inc(b0_done, 1)
                act.wait_ge(b0_full, 4 * i + 4)
                nc.scalar.activation(v_c[0:TXT, :, VW:VW + HD], bank0[0:TXT].rearrange("p (h d) -> p h d", h=NH), ACT.Copy).then_inc(b0_done, 1)
                if n is not None:
                    split_ctx(n)
                exps(i, 0)
                if n is not None:
                    squares(n, 0)
                exps(i, 1)
                if n is not None:
                    squares(n, 1)
                exps(i, 2)
                if n is not None:
                    squares(n, 2)
                    squares(n, 3)
                roots(n, m, p)
                exps(i, 3)
                if n is not None:
                    kq_hi(n)
                act.wait_ge(b1_full, slot1_own(i, 1))
                nc.scalar.activation(oT_hi[:], bank1[:, 0:KC * L].rearrange("p (c l) -> p c l", c=KC), ACT.Copy).then_inc(oT_hi_done, 1)

            over_batches(act, pre, body)
            roots(None, None, B - 1)

            def token_roots(k):
                act.wait_ge(sums_ready, k + 1)
                nc.scalar.activation(rstd[:], sums[:], ACT.Sqrt, bias=rms_eps[0:L], scale=1.0 / D).then_inc(root_ready, 1)

            def hT_scaled(k, at):
                act.wait_ge(fvec_loaded, 32)
                for kc in range(KC):
                    act.wait_ge(hT_full, KC * k + kc + 1)
                    nc.scalar.activation(hT_hi[:, kc, :], ps[:, 4 + kc, 0:S], ACT.Copy, scale=fvec[:, at + kc:at + kc + 1]).then_inc(hT_hi_done, 1)

            def weights_hi(h):
                act.wait_ge(ring_loaded[0 if h < FH else 1], 16 if h < FH else 32)
                if 4 <= h < FH + FKV:
                    act.wait_ge(head_full, h - 3)
                if h >= FH + FKV:
                    act.wait_ge(head_full, FH)
                w, _, hi = head_weights(h)
                nc.scalar.activation(hi, w, ACT.Copy).then_inc(w_hi_done, 1)

            for h in range(4):
                weights_hi(h)

            for k, table in enumerate((cos, sin)):
                act.wait_ge(rope_full, k + 1)
                nc.scalar.activation(table[:], ps[:, 2 + k, 0:S], ACT.Copy).then_inc(rope_ready, 1)
            token_roots(0)
            hT_scaled(0, FH + FKV)
            for h in range(FH + FKV):
                act.wait_ge(head_full, h + 1)
                if h >= 2:
                    act.wait_ge(head_ready, h - 1)
                nc.scalar.activation(biased[:, h % 2, :], ps[:, h % 2, 0:S], ACT.Identity, bias=fvec[:, h:h + 1]).then_inc(head_biased, 1)
                if h + 4 < FH + FKV + 2:
                    weights_hi(h + 4)
            act.wait_ge(gate_step, NC)
            nc.scalar.activation(gate_e[:], sel_score[:], ACT.Exp, scale=-1.0).then_inc(gate_exp, 1)

            def turn_evac(k):
                c = k % NC
                act.wait_ge(pT_full, k + 1)
                if c == 0 and k:
                    act.wait_ge(attn_full, k // NC)
                nc.scalar.activation(probT[:, 0:c + 1, c * L:(c + 1) * L],
                                     ps[0:L, 4 + k % 2, 0:(c + 1) * L].rearrange("t (b q) -> t b q", b=c + 1), ACT.Copy).then_inc(pT_ready, 1)

            for k in range(FH * NC + LAG):
                if k < FH * NC:
                    c = k % NC
                    n_keys = (c + 1) * L
                    act.wait_ge(top_ready, k + 1)
                    if k > LAG:
                        act.wait_ge(pT_full, k - LAG)
                    nc.scalar.activation(prob2[:, k % (LAG + 1), 0:n_keys], ps[0:L, c, 0:n_keys], ACT.Exp, bias=neg_top[:, c:c + 1],
                                         accum_out=prob_sum[:, c:c + 1]).then_inc(prob_ready, 1)
                if k >= LAG:
                    turn_evac(k - LAG)
            def gate_up_rounded(j):
                if j >= 3:
                    act.wait_ge(mlp_full, j - 2)
                for e, w in enumerate((w_gate, w_up)):
                    last = nc.scalar.activation(gate_up_hi[:, j % 3, e], w[:, :, j * P:(j + 1) * P], ACT.Copy)
                last.then_inc(gate_up_hi_done, 1)

            def hidden_rounded(j):
                act.wait_ge(hid_ready, j + 1)
                if j >= 2:
                    act.wait_ge(down_step, j - 1)
                nc.scalar.activation(m_hi[:, j % 2, :], m_prod[:, j % 2, :], ACT.Copy).then_inc(m_hi_done, 1)

            act.wait_ge(attn_full, FH)
            act.wait_ge(ring_loaded[0], 32)
            act.wait_ge(ring_loaded[1], 48)
            gate_up_rounded(0)
            gate_up_rounded(1)
            token_roots(1)
            hT_scaled(1, FH + FKV + KC)
            for j in range(FC):
                if j + 2 < FC:
                    gate_up_rounded(j + 2)
                act.wait_ge(mlp_full, j + 1)
                if j >= 2:
                    act.wait_ge(hid_ready, j - 1)
                nc.scalar.activation(silu_e[:, j % 2, :], ps[:, 2 * (j % 2), 0:S], ACT.Exp, scale=-1.0).then_inc(silu_exp, 1)
                if j:
                    hidden_rounded(j - 1)
                if j == 0:
                    act.wait_ge(ring_loaded[2], 32)
                if j >= 3:
                    act.wait_ge(down_step, j - 2)
                nc.scalar.activation(down_hi[:, j % 3], w_down[:, j, :], ACT.Copy).then_inc(down_hi_done, 1)
            hidden_rounded(FC - 1)

        @block.vector
        def _(dve):
            def ln1(m):
                dve.wait_ge(x_loaded, 16 * m + 16)
                nc.vector.bn_stats(ln1_stats[:], x_in[:]).then_inc(ln1_step, 1)
                dve.wait_ge(ln1_step, 3 * m + 1)
                dve.sem_inc(passed, 1)
                nc.vector.bn_aggr(ln1_mv[:], ln1_stats[:]).then_inc(ln1_step, 1)

            def ln1_finish(m):
                dve.wait_ge(ln1_sd_done, m + 1)
                nc.vector.reciprocal(ln1_rstd[:], ln1_sd[:]).then_inc(ln1_step, 1)

            def x_rest(n):
                dve.wait_ge(xT_hi_done, n + 1)
                nc.vector.tensor_tensor(xT_lo[:], ps[:, 6, 0:KC * L].rearrange("p (c l) -> p c l", c=KC),
                                        xT_hi[:].bitcast(F32), ALU.subtract).then_inc(xT_lo_done, 1)

            def add_bias(n, k):
                rows, bias = TOK_ROWS[k], (q_bias, k_bias, ki_bias, ki_bias)[k]
                full, done, bank, slot = ((b1_full, b1_done, bank1, slot1(n, k // 2)), (b0_full, b0_done, bank0, 4 * n + k // 2))[k % 2]
                dve.wait_ge(full, slot + 1)
                nc.vector.tensor_tensor(proj[0:rows, k, :], bank[0:rows], bias[0:rows], ALU.add).then_inc(done, 1)

            def rms_scale(n):
                dve.wait_ge(rms_done, n + 1)
                nc.vector.reciprocal(rstd1[:], rms[:]).then_inc(rms_inv, 1)
                dve.wait_ge(rms_inv, n + 1)
                nc.vector.tensor_scalar(proj[0:L, 0, :], proj[0:L, 0, :], rstd1[0:L, 0:1], None, ALU.mult).then_inc(scaled, 1)
                for k in range(1, 4):
                    rows = TOK_ROWS[k]
                    nc.vector.scalar_tensor_tensor(proj[0:rows, k, :], proj[0:rows, k, :], rstd1[0:rows, k:k + 1],
                                                   (w_txt if k == 1 else w_img)[0:rows], ALU.mult, ALU.mult).then_inc(scaled, 1)

            def q_rest(n):
                dve.wait_ge(q_hi_done, n + 1)
                for j in range(GH):
                    part = slice(HD * j, HD * (j + 1))
                    nc.vector.tensor_tensor(q_lo[part, :, j, :], ps[part, 2, 0:NG * L].rearrange("p (g l) -> p g l", g=NG),
                                            q_hi[part, :, j, :].bitcast(F32), ALU.subtract)

            def k_rest(n, k):
                rows = TOK_ROWS[k]
                cols = slice(KEY_AT[k], KEY_AT[k] + rows)
                dve.wait_ge(k_hi_done, 3 * n + k)
                return nc.vector.tensor_tensor(k_lo[:, :, cols], ps[:, 2 + k, 0:KC * rows].rearrange("p (c l) -> p c l", c=KC),
                                               k_hi[:, :, cols].bitcast(F32), ALU.subtract)

            def tail_keys(n):
                nc.vector.tensor_copy(k_hi[:, :, TAIL:TAIL + 1], k_tail_hi[:, :, bass.ds(n, 1)])
                nc.vector.tensor_copy(k_lo[:, :, TAIL:TAIL + 1], k_tail_lo[:, :, bass.ds(n, 1)]).then_inc(kq_lo_done, 1)

            def pair_max(i, p):
                dve.wait_ge(s_full, 8 * i + p + 1)
                bank = 2 + 2 * (p % 2)
                heads = slice(2 * (p % 2), 2 * (p % 2) + 2)
                nc.vector.tensor_reduce(top[:, p // 2, 0, heads], ps[0:L, bank:bank + 2, 0:TXT], AX.X, ALU.max)
                nc.vector.tensor_reduce(top[:, p // 2, 1, heads], ps[0:L, bank:bank + 2, TAIL:CTX], AX.X, ALU.max).then_inc(s_done, 1)

            def normalise(i, g):
                dve.wait_ge(pv_full, 4 * i + g + 1)
                pv = ps[0:L, 6 + g % 2, 0:GH * 2 * VW].rearrange("l (h s w) -> l h s w", h=GH, s=2)
                nc.vector.reciprocal(rec[:], pv[:, :, :, HD]).then_inc(norm_step, 1)
                dve.wait_ge(norm_step, 8 * i + 2 * g + 1)
                o_g = o[:, g * P:(g + 1) * P].rearrange("l (h d) -> l h d", h=GH)
                nc.vector.tensor_tensor(o_g, pv[:, :, 0, 0:HD], rec[:, :, 0:1].to_broadcast([L, GH, HD]), ALU.mult)
                nc.vector.tensor_tensor(o_txt[:], pv[:, :, 1, 0:HD], rec[:, :, 1:2].to_broadcast([L, GH, HD]), ALU.mult).then_inc(norm_step, 1)
                dve.wait_ge(norm_step, 8 * i + 2 * g + 2)
                nc.vector.tensor_tensor(o_g, o_g, o_txt[:], ALU.add).then_inc(pv_done, 1)

            def ln2(p):
                dve.wait_ge(b1_done, slot1_own(p, 2))
                nc.vector.bn_stats(ln2_stats[:], xh[:, 0]).then_inc(ln2_step, 1)
                dve.wait_ge(ln2_step, 3 * p + 1)
                dve.sem_inc(passed, 1)
                nc.vector.bn_aggr(ln2_mv[:], ln2_stats[:]).then_inc(ln2_step, 2)

            def ranks(q):
                dve.wait_ge(score_row_loaded, 16 * q + 16)
                nc.vector.scalar_tensor_tensor(equal, score_row[:], score_now[:], earlier[:], ALU.is_equal, ALU.mult).then_inc(rank_step, 1)
                dve.wait_ge(rank_step, q + 1)
                nc.vector.scalar_tensor_tensor(equal, score_row[:], score_now[:], equal, ALU.is_gt, ALU.add,
                                               accum_out=rank[:, bass.ds(q, 1)]).then_inc(rank_done, 1)

            def ln2_finish(p):
                dve.wait_ge(ln2_sd_done, p + 1)
                nc.vector.reciprocal(ln2_rstd[:], ln2_sd[:]).then_inc(h_step, 1)
                dve.wait_ge(h_step, p + 1)
                nc.vector.tensor_scalar(xh[:, 1], xh[:, 0], ln2_mv[:, 0:1], ln2_rstd[:], ALU.subtract, ALU.mult).then_inc(h_ready, 1)
                dve.wait_ge(h_ready, p + 1)
                dve.wait_ge(out_stored, 16 * p + 16)
                nc.vector.scalar_tensor_tensor(score_junk[:], xh[:, 1], 1.0, wr[:], ALU.mult, ALU.mult,
                                               accum_out=score_now[:]).then_inc(score_ready, 1)

            def pre():
                ln1(0)
                ln1_finish(0)
                dve.wait_ge(vecs_loaded, 16)
                nc.vector.tensor_tensor(vbias_cols, vecs[:, 0, :].unsqueeze(2).to_broadcast([P, KC, L]),
                                        vecs[:, 1, :].unsqueeze(2).to_broadcast([P, KC, L]), ALU.add).then_inc(vecs_ready, 1)

                def piece(j):
                    dve.wait_ge(piece_hi, j + 1)
                    c2 = slice(2 * (j % 2), 2 * (j % 2) + 2)
                    nc.vector.tensor_tensor(w_lo[W[j // 2]][:, c2, :], stage[:, j % 2, :].rearrange("p (c o) -> p c o", c=2),
                                            w_hi[W[j // 2]][:, c2, :].bitcast(F32), ALU.subtract).then_inc(piece_lo, 1)

                for j in range(2):
                    piece(j)
                x_rest(0)
                dve.wait_ge(rows_loaded, 16 * 7)
                nc.vector.scalar_tensor_tensor(w_txt[:], nq_row[:], SCALE, w_txt[:], ALU.mult, ALU.mult)
                nc.vector.scalar_tensor_tensor(w_img[:], nq_row[:], SCALE, w_img[:], ALU.mult, ALU.mult).then_inc(rows_ready, 1)
                for j in range(2, 5):
                    piece(j)
                dve.wait_ge(tail_split, 1)
                nc.vector.tensor_tensor(k_tail_lo[:], ctx_tail, k_tail_hi[:].bitcast(F32), ALU.subtract).then_inc(tail_split, 1)
                piece(5)
                dve.wait_ge(rows_loaded, 16 * 8)
                add_bias(0, 1)
                add_bias(0, 0)
                for j in range(6, PIECES):
                    piece(j)
                dve.wait_ge(bias_split, 1)
                nc.vector.tensor_tensor(xT_lo[:], vbias_cols, xT_hi[:].bitcast(F32), ALU.subtract).then_inc(bias_split, 1)
                add_bias(0, 2)
                add_bias(0, 3)
                ln1(1)
                dve.wait_ge(pro_full, 1)
                nc.vector.tensor_tensor(tail_proj, ps[0:B, 7, :], ki_bias[0:B], ALU.add).then_inc(pro_done, 1)
                dve.wait_ge(pro_full, 2)
                dve.wait_ge(consts_ready, 3)
                nc.vector.tensor_copy(v_tail[:, :, 0:HD], ps[0:B, 6, :].rearrange("b (h d) -> b h d", h=NH)).then_inc(pro_done, 1)
                dve.wait_ge(rows_ready, 1)
                rms_scale(0)
                nc.vector.scalar_tensor_tensor(tail_proj, tail_proj, rstd1[0:B, 4:5], w_img[0:B], ALU.mult, ALU.mult).then_inc(tail_scaled, 1)
                ln1_finish(1)
                dve.wait_ge(pro_full, 3)
                nc.vector.tensor_tensor(out_bias[:], ps[0:L, 7, :], out_bias[:], ALU.add).then_inc(rows_ready, 1)
                q_rest(0)
                for k in range(1, 4):
                    k_rest(0, k)
                dve.wait_ge(tail_hi_done, 1)
                nc.vector.tensor_tensor(k_tail_lo[:], ps[:, 7, 0:KC * B].rearrange("p (c b) -> p c b", c=KC),
                                        k_tail_hi[:].bitcast(F32), ALU.subtract).then_inc(tail_ready, 1)
                dve.wait_ge(tail_ready, 1)
                tail_keys(0)

            def body(i, n, m, p):
                pair_max(i, 0)
                pair_max(i, 1)
                if n is not None:
                    x_rest(n)
                pair_max(i, 2)
                pair_max(i, 3)
                dve.wait_ge(b1_full, 5 * i + 3)
                nc.vector.tensor_copy(v_b[:, :, 0:HD], bank1.rearrange("p (h d) -> p h d", h=NH)).then_inc(b1_done, 1)
                for k in range(4, 8):
                    pair_max(i, k)
                if p is not None:
                    ln2(p)
                if n is not None:
                    add_bias(n, 0)
                if m is not None:
                    ln1(m)
                if not isinstance(i, int) or i >= 2:
                    ranks(i - 2)
                normalise(i, 0)
                if n is not None:
                    for k in range(1, 4):
                        add_bias(n, k)
                normalise(i, 1)
                if m is not None:
                    ln1_finish(m)
                if n is not None:
                    rms_scale(n)
                if p is not None:
                    ln2_finish(p)
                normalise(i, 2)
                normalise(i, 3)
                if n is not None:
                    q_rest(n)
                dve.wait_ge(oT_hi_done, i + 1)
                nc.vector.tensor_tensor(oT_lo[:], bank1[:, 0:KC * L].rearrange("p (c l) -> p c l", c=KC),
                                        oT_hi[:].bitcast(F32), ALU.subtract).then_inc(b1_done, 1)
                if n is not None:
                    for k in range(1, 4):
                        k_rest(n, k)
                    tail_keys(n)
                dve.wait_ge(b1_full, slot1_own(i, 2))
                dve.wait_ge(xres_ready, i + 1)
                if p is not None:
                    dve.wait_ge(xh_stored, 16 * i)
                    dve.wait_ge(out_ready, i)
                nc.vector.tensor_tensor(xh[:, 0], bank1[0:L], x_res[:], ALU.add).then_inc(b1_done, 1)

            over_batches(dve, pre, body)
            ranks(B - 2)
            ln2(B - 1)
            ln2_finish(B - 1)
            ranks(B - 1)

            dve.wait_ge(topk_loaded, 16 * 6)
            dve.wait_ge(rank_done, B)
            nc.vector.tensor_scalar(chosen[:], rank[:], TOPK - 0.5, None, ALU.is_lt).then_inc(chosen_ready, 1)
            dve.wait_ge(before_full, 1)
            nc.vector.scalar_tensor_tensor(before[:], chosen[:], -FAR, ps[0:L, 0, 0:B], ALU.mult, ALU.add).then_inc(rank_step, 1)
            dve.wait_ge(rank_step, B + 1)
            nc.vector.tensor_tensor(slot_hot[:], before[:].unsqueeze(2).to_broadcast([L, B, TOPK]),
                                    slot_far[:].unsqueeze(1).to_broadcast([L, B, TOPK]), ALU.is_equal).then_inc(hot_ready, 1)
            dve.wait_ge(tok_full, 1)
            nc.vector.tensor_tensor(tok[:], ps[0:L, 1, 0:NC], token_base[:], ALU.add).then_inc(tok_ready, 1)

            def normalise_tokens(k, src):
                dve.wait_ge(root_ready, k + 1)
                nc.vector.reciprocal(rstd[:], rstd[:]).then_inc(rstd_ready, 1)
                dve.wait_ge(rstd_ready, k + 1)
                for c in range(NC):
                    nc.vector.tensor_scalar(normed[:, c], src(c), rstd[:, c:c + 1], None, ALU.mult).then_inc(normed_ready, 1)

            for c in range(NC):
                dve.wait_ge(gathered[c], 16)
                last = nc.vector.scalar_tensor_tensor(normed[:, c], xh_sel[:, c, 1], 1.0, xh_sel[:, c, 1], ALU.mult, ALU.mult,
                                                      accum_out=sums[:, c:c + 1])
            last.then_inc(sums_ready, 1)
            dve.wait_ge(sums_ready, 1)
            normalise_tokens(0, lambda c: xh_sel[:, c, 1])
            def hT_rest(k, at):
                dve.wait_ge(hT_full, KC * k + KC)
                dve.wait_ge(fvec_loaded, 32)
                for kc in range(KC):
                    dve.wait_ge(hT_hi_done, KC * k + kc + 1)
                    nc.vector.scalar_tensor_tensor(hT_lo[:, kc, :], ps[:, 4 + kc, 0:S], fvec[:, at + kc:at + kc + 1],
                                                   hT_hi[:, kc, :].bitcast(F32), ALU.mult, ALU.subtract).then_inc(hT_ready, 1)

            hT_rest(0, FH + FKV)
            dve.wait_ge(rope_ready, 2)
            for h in range(FH + FKV):
                dve.wait_ge(head_biased, h + 1)
                b = biased[:, h % 2, :]
                dst = qT[:, h, :] if h < FH else kT[:, h - FH, :]
                if h >= 2:
                    dve.wait_ge(head_ready, h - 1)
                r = rot[:, h % 2, :]
                scale = 1.0 if h < FH else FSCALE
                nc.vector.scalar_tensor_tensor(r[0:HALF], b[HALF:P], scale, sin[HALF:P], ALU.mult, ALU.mult)
                nc.vector.scalar_tensor_tensor(r[HALF:P], b[0:HALF], scale, sin[0:HALF], ALU.mult, ALU.mult)
                nc.vector.scalar_tensor_tensor(dst, b, scale, cos[:], ALU.mult, ALU.mult).then_inc(rot_step, 1)
                dve.wait_ge(rot_step, h + 1)
                nc.vector.tensor_tensor(dst, dst, r, ALU.add).then_inc(head_ready, 1)
            dve.wait_ge(head_ready, FH + FKV)
            for c in range(NC):
                if c:
                    dve.wait_ge(gate_step, c)
                nc.vector.scalar_tensor_tensor(rows4[0:L].rearrange("l a s -> l (a s)")[:, 0:D], xh_sel[:, c, 1], 1.0, wr[:],
                                               ALU.mult, ALU.mult, accum_out=sel_score[:, c:c + 1]).then_inc(gate_step, 1)
            dve.wait_ge(fvec_loaded, 32)
            for k in range(2 * NC):
                dve.wait_ge(val_full, k + 1)
                half = slice(512 * (k // NC), 512 * (k // NC) + 512)
                nc.vector.tensor_tensor(vals[:, k % NC, half], ps[0:L, 2 + k % 2, :], bv_row[:, half], ALU.add).then_inc(val_ready, 1)
            dve.wait_ge(gate_exp, 1)
            nc.vector.tensor_scalar(gate_e[:], gate_e[:], 1.0, None, ALU.add).then_inc(gate_step, 1)
            dve.wait_ge(gate_step, NC + 1)
            nc.vector.reciprocal(gate[:], gate_e[:]).then_inc(gate_step, 1)
            dve.wait_ge(gate_step, NC + 2)
            nc.vector.tensor_scalar(gate_e[:], gate[:], -1.0, 1.0, ALU.mult, ALU.add).then_inc(gate_step, 1)
            dve.wait_ge(gate_step, NC + 3)
            for c in range(NC):
                last = nc.vector.scalar_tensor_tensor(keep[:, c], xh_sel[:, c, 1], gate_e[:, c:c + 1], xh_sel[:, c, 0], ALU.mult, ALU.add)
            last.then_inc(gate_step, 1)

            def scale_probs(k):
                c = k % NC
                dve.wait_ge(prob_ready, k + 1)
                nc.vector.reciprocal(prob_sum[:, c:c + 1], prob_sum[:, c:c + 1]).then_inc(inv_ready, 1)
                dve.wait_ge(inv_ready, k + 1)
                part = prob2[:, k % (LAG + 1), 0:(c + 1) * L]
                nc.vector.tensor_scalar(part, part, prob_sum[:, c:c + 1], None, ALU.mult).then_inc(prob_scaled, 1)

            for k in range(FH * NC + LAG + 2):
                c = k % NC
                if k < FH * NC:
                    dve.wait_ge(att_full, k + 1)
                    nc.vector.tensor_reduce(neg_top[:, c:c + 1], ps[0:L, c, 0:(c + 1) * L], AX.X, ALU.max, negate=True).then_inc(top_ready, 1)
                if 1 <= k <= FH * NC:
                    scale_probs(k - 1)
                h = (k - LAG - 1) // NC - 1
                if (k - LAG - 1) % NC == 0 and h >= 0:
                    dve.wait_ge(attn_full, h + 1)
                    nc.vector.tensor_copy(attnT[:, h, :], ps[:, 6 + h % 2, 0:S]).then_inc(attn_ready, 1)
            for c in range(NC):
                dve.wait_ge(mid_full, c + 1)
                nc.vector.tensor_tensor(x_mid[:, c], ps[0:L, c, :], xh_sel[:, c, 1], ALU.add).then_inc(mid_ready, 1)
            for c in range(NC):
                dve.wait_ge(mid_ready, c + 1)
                last = nc.vector.scalar_tensor_tensor(normed[:, c], x_mid[:, c], 1.0, x_mid[:, c], ALU.mult, ALU.mult,
                                                      accum_out=sums[:, c:c + 1])
            last.then_inc(sums_ready, 1)
            dve.wait_ge(sums_ready, 2)
            normalise_tokens(1, lambda c: x_mid[:, c])
            hT_rest(1, FH + FKV + KC)

            def hidden_rest(j):
                dve.wait_ge(m_hi_done, j + 1)
                if j >= 2:
                    dve.wait_ge(down_step, j - 1)
                nc.vector.tensor_tensor(m_lo[:, j % 2, :], m_prod[:, j % 2, :], m_hi[:, j % 2, :].bitcast(F32), ALU.subtract).then_inc(m_lo_done, 1)

            for j in range(FC):
                e = silu_e[:, j % 2, :]
                g, u = (ps[:, 2 * (j % 2) + a, 0:S] for a in range(2))
                dve.wait_ge(silu_exp, j + 1)
                nc.vector.tensor_scalar(e, e, 1.0, None, ALU.add).then_inc(silu_step, 1)
                dve.wait_ge(silu_step, 3 * j + 1)
                nc.vector.reciprocal(e, e).then_inc(silu_step, 1)
                dve.wait_ge(silu_step, 3 * j + 2)
                nc.vector.tensor_tensor(silu_g[:, j % 2, :], g, e, ALU.mult).then_inc(silu_step, 1)
                dve.wait_ge(silu_step, 3 * j + 3)
                nc.vector.tensor_tensor(m_prod[:, j % 2, :], u, silu_g[:, j % 2, :], ALU.mult).then_inc(hid_ready, 1)
                if j:
                    hidden_rest(j - 1)
            hidden_rest(FC - 1)
            dve.wait_ge(gate_step, NC + 4)
            for c in range(NC):
                dve.wait_ge(down_full, c + 1)
                nc.vector.tensor_tensor(x_mid[:, c], ps[0:L, 4 + c, :], x_mid[:, c], ALU.add).then_inc(sum_ready, 1)
                dve.wait_ge(sum_ready, c + 1)
                nc.vector.scalar_tensor_tensor(keep[:, c], x_mid[:, c], gate[:, c:c + 1], keep[:, c], ALU.mult, ALU.add).then_inc(final_ready, 1)

        @block.tensor
        def _(pe):
            def mm3(o_, a_hi, a_lo, b_hi, b_lo, start, stop):
                nc.tensor.matmul(o_, a_hi, b_hi, start=start, stop=False)
                nc.tensor.matmul(o_, a_hi, b_lo, start=False, stop=False)
                return nc.tensor.matmul(o_, a_lo, b_hi, start=False, stop=stop)

            def project(o_, a_hi, a_lo, cols, w, chunks=range(KC)):
                for kc in chunks:
                    last = mm3(o_, a_hi[:, kc, cols], a_lo[:, kc, cols], w_hi[w][:, kc, :], w_lo[w][:, kc, :], kc == 0, kc == KC - 1)
                return last

            def transpose_x(n):
                pe.wait_ge(xn_ready, n + 1)
                for c in range(KC):
                    last = nc.tensor.transpose(ps[:, 6, c * L:(c + 1) * L], xn[:, c * P:(c + 1) * P], ident[0:L, 0:L])
                last.then_inc(xT_full, 1)

            def queries(n, part):
                if part == 0:
                    pe.wait_ge(xT_lo_done, n + 1)
                    if not isinstance(n, int) or n:
                        pe.wait_ge(b1_done, slot1(n, 0))
                last = project(bank1[0:L], xT_hi, xT_lo, slice(0, L), "q", range(2 * part, 2 * part + 2))
                if part == 1:
                    last.then_inc(b1_full, 1)

            def keys(n, k):
                cols, w, rows = ((slice(0, TXT), "k", TXT), (slice(TXT, TXT + P), "k_img", P), (slice(TXT + P, CTXC), "k_img", P))[k]
                if k == 0:
                    pe.wait_ge(ctx_lo_done, n + 1)
                if not isinstance(n, int) or n or k:
                    if k % 2:
                        pe.wait_ge(b1_done, slot1(n, 1))
                    else:
                        pe.wait_ge(b0_done, 4 * n + k // 2)
                project((bank0, bank1)[k % 2][0:rows], ctx_hi, ctx_lo, cols, w).then_inc((b0_full, b1_full)[k % 2], 1)

            def turn(n, k):
                rows = TOK_ROWS[k]
                pe.wait_ge(scaled, 4 * n + k + 1)
                for c in range(KC):
                    last = nc.tensor.transpose(ps[:, 2 + k, c * rows:(c + 1) * rows], proj[0:rows, k, c * P:(c + 1) * P], ident[0:rows, 0:rows])
                last.then_inc(turned, 1)

            def values(i, k, part):
                cols, w, rows = ((slice(TXT, TXT + P), "v_img", P), (slice(TXT + P, CTXC), "v_img", P), (slice(0, TXT), "v", TXT))[k]
                if part == 0:
                    if k == 1:
                        pe.wait_ge(b1_done, 5 * i + 2)
                    else:
                        pe.wait_ge(b0_done, 4 * i + 2 + k // 2)
                last = project((bank0, bank1)[k % 2][0:rows], ctx_hi, ctx_lo, cols, w, range(2 * part, 2 * part + 2))
                if part == 1:
                    last.then_inc((b0_full, b1_full)[k % 2], 1)

            def scores(i, p):
                if p == 0:
                    pe.wait_ge(kq_lo_done, i + 1)
                if p >= 2:
                    pe.wait_ge(s_done, 8 * i + p - 1)
                for e in range(2):
                    g, j = p // 2, 2 * (p % 2) + e
                    last = nc.tensor.matmul(ps[0:L, 2 + 2 * (p % 2) + e, 0:NKEY], q_hi[:, g, j, :], k_hi[:, g, :], start=True, stop=True)
                last.then_inc(s_full, 1)

            def scores_T(i, g):
                pe.wait_ge(shift_ready, 4 * i + g + 1)
                for c, (at, rows) in enumerate(CHUNKS):
                    k = 3 * g + c
                    if k == 0:
                        pe.wait_ge(s_done, 8 * i + 7)
                    if k == 2:
                        pe.wait_ge(s_done, 8 * i + 8)
                    if k >= 4:
                        pe.wait_ge(exp_done, 12 * i + k - 3)
                    o_ = ps[0:rows, 2 + k % 4, 0:GH * L]
                    cols = slice(at, at + rows)
                    q = [x[:, g].rearrange("p h q -> p (h q)") for x in (q_hi, q_lo)]
                    sh = [shift[:, g, s].rearrange("l h q -> l (h q)") for s in range(2)]
                    mm3(o_, k_hi[:, g, cols], k_lo[:, g, cols], q[0], q[1], True, False)
                    if c == 0:
                        nc.tensor.matmul(o_, ones_c_txt, sh[0], start=False, stop=False)
                        last = nc.tensor.matmul(o_, ones_c_tail, sh[1], start=False, stop=True)
                    else:
                        last = nc.tensor.matmul(o_, ones_img, sh[1], start=False, stop=True)
                    last.then_inc(st_full, 1)

            def weighted_values(i, g, n):
                pe.wait_ge(exp_done, 12 * i + 3 * g + 3)
                if g == 0:
                    pe.wait_ge(vtail_loaded, 16 * i + 16)
                    pe.wait_ge(b0_done, 4 * i + 4)
                    pe.wait_ge(b1_done, 5 * i + 3)
                    if n is not None:
                        pe.wait_ge(xT_lo_done, n + 1)
                if g >= 2:
                    pe.wait_ge(pv_done, 4 * i + g - 1)
                for j in range(GH):
                    h, at = GH * g + j, 2 * VW * j
                    qs = slice(L * j, L * (j + 1))
                    bank = ps[0:L, 6 + g % 2, :]
                    nc.tensor.matmul(bank[:, at:at + 2 * VW], prob[0:CHUNK_C, g % 2, 0, qs], v_c[:, h, :], start=True, stop=False)
                    nc.tensor.matmul(bank[:, at:at + VW], prob[:, g % 2, 1, qs], v_a[:, h, :], start=False, stop=False)
                    last = nc.tensor.matmul(bank[:, at:at + VW], prob[:, g % 2, 2, qs], v_b[:, h, :], start=False, stop=True)
                last.then_inc(pv_full, 1)

            def pre():
                pe.wait_ge(consts_ready, 1)
                transpose_x(0)
                pe.wait_ge(piece_lo, 2)
                keys(0, 0)
                pe.wait_ge(piece_lo, 4)
                queries(0, 0)
                queries(0, 1)
                pe.wait_ge(piece_lo, 6)
                keys(0, 1)
                keys(0, 2)
                pe.wait_ge(tail_split, 2)
                for bank, w, pieces in ((7, "k_img", 6), (6, "v_img", 8)):
                    pe.wait_ge(piece_lo, pieces)
                    project(ps[0:B, bank, :], k_tail_hi, k_tail_lo, slice(0, B), w).then_inc(pro_full, 1)
                pe.wait_ge(piece_lo, PIECES)
                pe.wait_ge(bias_split, 2)
                pe.wait_ge(pro_done, 1)
                project(ps[0:L, 7, :], xT_hi, xT_lo, slice(0, L), "o").then_inc(pro_full, 1)
                for k in range(4):
                    turn(0, k)
                pe.wait_ge(tail_scaled, 1)
                pe.wait_ge(rows_ready, 2)
                for c in range(KC):
                    last = nc.tensor.transpose(ps[:, 7, c * B:(c + 1) * B], tail_proj[:, c * P:(c + 1) * P], ident[0:B, 0:B])
                last.then_inc(tail_turned, 1)
                values(0, 0, 0)
                values(0, 0, 1)

            def body(i, n, m, p):
                if n is not None:
                    if p is None:
                        pe.wait_ge(pro_done, 2)
                    else:
                        pe.wait_ge(pv_done, 4 * i)
                    transpose_x(n)
                scores(i, 0)
                scores(i, 1)
                for k in (1, 2):
                    for part in range(2):
                        values(i, k, part)
                        scores(i, 2 * k + part)
                for part in range(2):
                    if n is not None:
                        queries(n, part)
                    scores(i, 6 + part)
                scores_T(i, 0)
                scores_T(i, 1)
                weighted_values(i, 0, n)
                if n is not None:
                    keys(n, 0)
                scores_T(i, 2)
                if n is not None:
                    keys(n, 1)
                    keys(n, 2)
                weighted_values(i, 1, n)
                scores_T(i, 3)
                weighted_values(i, 2, n)
                if n is not None:
                    pe.wait_ge(exp_done, 12 * i + 10)
                    turn(n, 0)
                    turn(n, 1)
                weighted_values(i, 3, n)
                if n is not None:
                    turn(n, 2)
                    turn(n, 3)
                pe.wait_ge(pv_done, 4 * i + 4)
                pe.wait_ge(b1_done, slot1_own(i, 0))
                for c in range(KC):
                    last = nc.tensor.transpose(bank1[:, c * L:(c + 1) * L], o[:, c * P:(c + 1) * P], ident[0:L, 0:L])
                last.then_inc(b1_full, 1)
                if n is not None:
                    values(n, 0, 0)
                    values(n, 0, 1)
                pe.wait_ge(b1_done, slot1_own(i, 1))
                project(bank1[0:L], oT_hi, oT_lo, slice(0, L), "o").then_inc(b1_full, 1)

            over_batches(pe, pre, body)

            pe.wait_ge(chosen_ready, 1)
            nc.tensor.matmul(ps[0:L, 0, 0:B], later[:], chosen[:], start=True, stop=True).then_inc(before_full, 1)
            pe.wait_ge(hot_ready, 1)
            hot = slot_hot[:].rearrange("l b k -> l (b k)")
            for c in range(NC):
                last = nc.tensor.matmul(ps[0:L, 1, c:c + 1], hot[:, c * L:(c + 1) * L], token_no[:], start=True, stop=True)
            last.then_inc(tok_full, 1)
            for k, table in enumerate((cos_tab, sin_tab)):
                nc.tensor.matmul(ps[:, 2 + k, 0:S], table[:], hot, start=True, stop=True).then_inc(rope_full, 1)

            def turn_tokens(k):
                pe.wait_ge(normed_ready, NC * k + NC)
                for kc in range(KC):
                    for c in range(NC):
                        last = nc.tensor.transpose(ps[:, 4 + kc, c * L:(c + 1) * L], normed[:, c, kc * P:(kc + 1) * P], ident[0:L, 0:L])
                    last.then_inc(hT_full, 1)

            turn_tokens(0)
            pe.wait_ge(hT_ready, KC)
            for h in range(FH + FKV):
                pe.wait_ge(w_lo_done, h + 1)
                if h >= 2:
                    pe.wait_ge(head_biased, h - 1)
                _, lo, hi = head_weights(h)
                for kc in range(KC):
                    last = mm3(ps[:, h % 2, 0:S], hi[:, kc, :], lo[:, kc, :], hT_hi[:, kc, :], hT_lo[:, kc, :], kc == 0, kc == KC - 1)
                last.then_inc(head_full, 1)
            for k in range(2 * NC):
                half, c = k // NC, k % NC
                pe.wait_ge(w_lo_done, FH + FKV + half + 1)
                if k >= 2:
                    pe.wait_ge(val_ready, k - 1)
                _, lo, hi = head_weights(FH + FKV + half)
                cols = slice(c * L, (c + 1) * L)
                for kc in range(KC):
                    last = mm3(ps[0:L, 2 + k % 2, :], hT_hi[:, kc, cols], hT_lo[:, kc, cols], hi[:, kc, :], lo[:, kc, :], kc == 0, kc == KC - 1)
                last.then_inc(val_full, 1)

            def att(k):
                h, c = k // NC, k % NC
                if c == 0:
                    pe.wait_ge(head_ready, FH + h // 2 + 1)
                if k >= NC:
                    pe.wait_ge(prob_ready, k - NC + 1)
                o_ = ps[0:L, c, 0:(c + 1) * L]
                nc.tensor.matmul(o_, qT[:, h, c * L:(c + 1) * L], kT[:, h // 2, 0:(c + 1) * L], start=True, stop=False)
                nc.tensor.matmul(o_[:, c * L:(c + 1) * L], ident_bf[:], causal[:], start=False, stop=True).then_inc(att_full, 1)

            def turn_probs(k):
                c = k % NC
                pe.wait_ge(prob_scaled, k + 1)
                if k >= 2:
                    pe.wait_ge(pT_ready, k - 1)
                for b in range(c + 1):
                    last = nc.tensor.transpose(ps[0:L, 4 + k % 2, b * L:(b + 1) * L], prob2[:, k % (LAG + 1), b * L:(b + 1) * L], ident[0:L, 0:L])
                last.then_inc(pT_full, 1)

            def weigh(h):
                pe.wait_ge(pT_ready, NC * h + NC)
                if h >= 2:
                    pe.wait_ge(attn_ready, h - 1)
                for b in range(NC):
                    last = nc.tensor.matmul(ps[:, 6 + h % 2, b * L:S], vals[:, b, (h // 2) * FD:(h // 2 + 1) * FD], probT[:, b, b * L:S],
                                            start=b == 0, stop=b == NC - 1)
                last.then_inc(attn_full, 1)

            pe.wait_ge(consts2, 2)
            pe.wait_ge(val_ready, 2 * NC)
            for k in range(FH * NC + LAG + 1):
                if k < FH * NC:
                    att(k)
                if LAG <= k < FH * NC + LAG:
                    turn_probs(k - LAG)
                if k >= NC + LAG and (k - LAG) % NC == 0:
                    weigh((k - LAG) // NC - 1)
            pe.wait_ge(ring_loaded[2], 16)
            pe.wait_ge(attn_ready, FH)
            for c in range(NC):
                for h in range(FH):
                    last = nc.tensor.matmul(ps[0:L, c, :], attnT[:, h, c * L:(c + 1) * L], wo[:, h, :], start=h == 0, stop=h == FH - 1)
                last.then_inc(mid_full, 1)
            turn_tokens(1)
            pe.wait_ge(hT_ready, 2 * KC)
            pe.wait_ge(mid_ready, NC)

            def down(j):
                pe.wait_ge(m_lo_done, j + 1)
                pe.wait_ge(down_lo_done, j + 1)
                for c in range(NC):
                    cols = slice(c * L, (c + 1) * L)
                    last = mm3(ps[0:L, 4 + c, :], m_hi[:, j % 2, cols], m_lo[:, j % 2, cols], down_hi[:, j % 3], w_down_lo[:, j, :],
                               j == 0, j == FC - 1)
                    if j == FC - 1:
                        last.then_inc(down_full, 1)
                if j < FC - 1:
                    last.then_inc(down_step, 1)

            for j in range(FC + 2):
                if j < FC:
                    if j >= 2:
                        pe.wait_ge(hid_ready, j - 1)
                    pe.wait_ge(gate_up_lo_done, j + 1)
                    for e, lo in enumerate((w_gate_lo, w_up_lo)):
                        for kc in range(KC):
                            last = mm3(ps[:, 2 * (j % 2) + e, 0:S], gate_up_hi[:, j % 3, e, kc, :], lo[:, kc, j * P:(j + 1) * P],
                                       hT_hi[:, kc, :], hT_lo[:, kc, :], kc == 0, kc == KC - 1)
                    last.then_inc(mlp_full, 1)
                if j >= 2:
                    down(j - 2)


def kernel(**inputs):
    import numpy as np
    import concourse.bacc as bacc
    from concourse.bass_utils import run_bass_kernel_spmd as run

    nc = bacc.Bacc("TRN2", target_bir_lowering=False, num_devices=1)
    a = {k: np.asarray(v) for k, v in inputs.items()}
    c, f = np.ascontiguousarray, np.float32

    def columns(v):
        return v.reshape(KC, P).T

    x_ = "L0_xattn_"
    ctxT = a["ctx_2048"].transpose(0, 2, 1)
    order = np.concatenate([np.arange(IMG, CTX), np.arange(IMG_MAIN)])
    arrays = {
        "x": c(a["x"]),
        "ctx": c(ctxT[:, :, order].reshape(B, KC, P, CTXC).transpose(0, 2, 1, 3)),
        "ctx_tail": c(ctxT[:, :, IMG_MAIN].T.reshape(KC, P, B).transpose(1, 0, 2)),
        "vecs": c(np.stack([columns(a[x_ + n]) for n in ("v_b", "v_img_b")], 1)),
        "w_router": c(a["L0_ffn_w_router"]),
    }
    for n in ("q_b", "k_b", "k_img_b", "norm_q_w", "norm_k_w", "norm_k_img_w", "o_b"):
        arrays[n] = c(a[x_ + n])
    f_ = "L0_ffn_"
    arrays["fvec"] = c(np.concatenate([a[f_ + "bq"].reshape(FH, FD).T, a[f_ + "bk"].reshape(FKV, FD).T,
                                       columns(a[f_ + "ln1_w"]), columns(a[f_ + "ln2_w"])], 1))
    arrays["bv"] = c(a[f_ + "bv"])
    for w in ("wq", "wk", "wv", "wo", "w_gate", "w_up", "w_down"):
        arrays[w] = c(a[f_ + w])
    token = np.arange(L)
    arrays["later"] = (token[None, :] > token[:, None]).astype(f)
    arrays["slot_far"] = np.broadcast_to(np.arange(TOPK, dtype=f) - f(FAR), (L, TOPK)).copy()
    arrays["token_no"] = token.astype(f)[:, None].copy()
    arrays["token_base"] = (L * (BPC * np.arange(NC)[None, :] + token[:, None] // TOPK)).astype(f)
    freq = f(1.0) / np.power(f(10000.0), np.arange(0, FD, 2, dtype=f) / f(FD))
    angle = token.astype(f)[:, None] * freq
    arrays["cos_tab"] = np.concatenate([np.cos(angle), np.cos(angle)], 1).astype(f)
    arrays["sin_tab"] = np.concatenate([np.sin(angle), -np.sin(angle)], 1).astype(f)
    for w in ("q", "k", "v", "k_img", "v_img", "o"):
        arrays["w_" + w] = c(a[x_ + w + "_w"].T)
    feeds, t = {}, {}
    for k, v in arrays.items():
        feeds[f"in_{k}_dram"] = v
        t[k] = nc.dram_tensor(f"in_{k}_dram", v.shape, mybir.dt.from_np(v.dtype), kind="ExternalInput").ap()
    out = nc.dram_tensor("out_dram", (B, L, D), F32, kind="ExternalOutput").ap()
    build(nc, t, out)
    r = run(nc, [feeds], core_ids=[0])
    return r.results[0]["out_dram"]
```
